# Optimizing a Trainium2 kernel written in Bass

```python
import numpy as np
import jax
import jax.numpy as jnp

def _softmax(x, axis=-1):
    return jax.nn.softmax(x, axis=axis)

def _gelu(x):
    return jax.nn.gelu(x, approximate=True)

def _silu(x):
    return jax.nn.silu(x)

def _sigmoid(x):
    return jax.nn.sigmoid(x)

def _layernorm(x, axis=-1, eps=1e-05):
    m = jnp.mean(x, axis=axis, keepdims=True)
    v = jnp.var(x, axis=axis, keepdims=True)
    return (x - m) / jnp.sqrt(v + eps)

def _scatter_add(tgt, idx, src, axis=0):
    return tgt.at[idx].add(src)

def _segment_sum(src, seg, n):
    return jax.ops.segment_sum(src, seg, n)
kernel_name = 'mk_gnn_preln_d4_gnn_r8_c5aa60'

def setup_inputs(seed: int=0):
    np.random.seed(seed)
    _w = jnp.asarray

    def _rec_inputs():
        import jax
        import jax.numpy as jnp
        _gk = jax.random.key(seed)
        x = -0.0007083 + 1.001 * jax.random.normal(jax.random.fold_in(_gk, 1), (6250, 48), jnp.float32)
        _s = jax.random.randint(jax.random.fold_in(_gk, 2), (100000,), 0, 6250, jnp.int32)
        _d = jax.random.randint(jax.random.fold_in(_gk, 3), (100000,), 0, 6250, jnp.int32)
        _loop = jnp.arange(6250, dtype=jnp.int32)
        src = jnp.concatenate([_s, _d, _loop])
        dst = jnp.concatenate([_d, _s, _loop])
        _o = jnp.argsort(dst, stable=True)
        src = src[_o]
        dst = dst[_o]
        edge_attr_40 = jax.random.uniform(jax.random.fold_in(_gk, 13), (206250, 40), jnp.float32, 0.0, 1)
        edge_type_4 = jax.random.randint(jax.random.fold_in(_gk, 15), (206250,), 0, 4, jnp.int32)
        edge_type_8 = jax.random.randint(jax.random.fold_in(_gk, 16), (206250,), 0, 8, jnp.int32)
        edge_weight = jax.random.uniform(jax.random.fold_in(_gk, 17), (206250,), jnp.float32, 0.0, 6.99999)
        edge_weight1 = jax.random.uniform(jax.random.fold_in(_gk, 18), (206250, 1), jnp.float32, 0.0, 1)
        node_type_119 = jax.random.randint(jax.random.fold_in(_gk, 19), (6250,), 0, 119, jnp.int32)
        node_vec = jax.random.uniform(jax.random.fold_in(_gk, 20), (6250,), jnp.float32, 0.0, 1.49999)
        return (x, src, dst, edge_attr_40, edge_type_4, edge_type_8, edge_weight, edge_weight1, node_type_119, node_vec)
    x, src, dst, edge_attr_40, edge_type_4, edge_type_8, edge_weight, edge_weight1, node_type_119, node_vec = _rec_inputs()

    def _L0_gnn_setup():
        import jax, jax.numpy as jnp
        import numpy as np
        CUTOFF = 6.0
        LN_EPS = 1e-05
        key = jax.random.key(seed)
        ks = jax.random.split(key, 16)
        N, E, H, R, NEL, G = (6250, 100000, 48, 40, 119, 32)
        inp = {'h': jax.random.normal(ks[0], (N, H), jnp.float32), 'edge_index': jax.random.randint(ks[1], (2, E), 0, N, jnp.int64), 'edge_attr': jax.random.uniform(ks[2], (E, R), jnp.float32), 'distances': jax.random.uniform(ks[3], (E,), jnp.float32) * 7.0, 'atom_z': jax.random.randint(ks[4], (N,), 0, NEL, jnp.int64), 'node_mult': jax.random.uniform(ks[5], (N,), jnp.float32) + 0.5, 'batch': jnp.zeros((N,), jnp.int64), 'W1': jax.random.normal(ks[6], (H, R), jnp.float32) / np.sqrt(R), 'b1': jax.random.normal(ks[7], (H,), jnp.float32) * 0.01, 'W2': jax.random.normal(ks[8], (H, H), jnp.float32) / np.sqrt(H), 'b2': jax.random.normal(ks[9], (H,), jnp.float32) * 0.01, 'emb': jax.random.normal(ks[10], (NEL, G), jnp.float32) * 0.01, 'adaptW': jax.random.normal(ks[11], (G, G), jnp.float32) * 0.01, 'gamma': jnp.ones((H,), jnp.float32), 'beta': jnp.zeros((H,), jnp.float32)}
        return inp
    _L0_gnn_all = _L0_gnn_setup()
    _L0_gnn_in = {k: v for k, v in _L0_gnn_all.items() if k in ('W1', 'b1', 'W2', 'b2', 'emb', 'adaptW', 'gamma', 'beta')}
    del _L0_gnn_all

    def _L1_gnn_setup():
        import jax, jax.numpy as jnp
        import numpy as np
        N_NODES = 12500
        N_EDGES = 200000
        D_IN = 48
        D_OUT = 48
        N_REL = 4
        key = jax.random.key(seed)
        k1, k2, k3, k4, k5, k6 = jax.random.split(key, 6)
        h = jax.random.normal(k1, (N_NODES, D_IN), dtype=jnp.float32)
        norm_vals = jax.random.uniform(k2, (N_EDGES,), dtype=jnp.float32)
        W = jax.random.normal(k3, (N_REL * D_IN, D_OUT), dtype=jnp.float32) * 0.05
        b = jax.random.normal(k4, (D_OUT,), dtype=jnp.float32) * 0.05
        edge_index = jax.random.randint(k5, (2, N_EDGES), 0, N_NODES, dtype=jnp.int64)
        edge_relation = jax.random.randint(k6, (N_EDGES,), 0, N_REL, dtype=jnp.int32)
        return {'h': h, 'norm_vals': norm_vals, 'W': W, 'b': b, 'edge_index': edge_index, 'edge_relation': edge_relation}
    _L1_gnn_all = _L1_gnn_setup()
    _L1_gnn_in = {k: v for k, v in _L1_gnn_all.items() if k in ('W', 'b')}
    del _L1_gnn_all

    def _L2_gnn_setup():
        import jax, jax.numpy as jnp
        import numpy as np
        N_NODES = 6250
        N_EDGES = 200000
        IN_FEAT = 48
        OUT_FEAT = 48
        NUM_RELS = 8
        key = jax.random.key(seed)
        ks = jax.random.split(key, 9)
        s1 = float(np.sqrt(2.0) * np.sqrt(6.0 / (IN_FEAT + IN_FEAT)))
        s2 = float(np.sqrt(2.0) * np.sqrt(6.0 / (IN_FEAT + OUT_FEAT)))
        return {'inputs': jax.random.normal(ks[0], (N_NODES, IN_FEAT), dtype=jnp.float32), 'norm': jax.random.uniform(ks[1], (N_EDGES, 1), dtype=jnp.float32), 'weight1': jax.random.uniform(ks[2], (NUM_RELS, IN_FEAT, IN_FEAT), jnp.float32, -s1, s1), 'weight2': jax.random.uniform(ks[3], (NUM_RELS, IN_FEAT, OUT_FEAT), jnp.float32, -s2, s2), 'bias1': jax.random.normal(ks[4], (IN_FEAT,), dtype=jnp.float32) * 0.1, 'bias2': jax.random.normal(ks[5], (OUT_FEAT,), dtype=jnp.float32) * 0.1, 'src': jax.random.randint(ks[6], (N_EDGES,), 0, N_NODES, dtype=jnp.int64) if jax.config.jax_enable_x64 else jax.random.randint(ks[6], (N_EDGES,), 0, N_NODES).astype(jnp.int32), 'dst': jax.random.randint(ks[7], (N_EDGES,), 0, N_NODES).astype(jnp.int32), 'rel_type': jax.random.randint(ks[8], (N_EDGES,), 0, NUM_RELS).astype(jnp.int32)}
    _L2_gnn_all = _L2_gnn_setup()
    _L2_gnn_in = {k: v for k, v in _L2_gnn_all.items() if k in ('weight1', 'weight2', 'bias1', 'bias2')}
    del _L2_gnn_all

    def _L3_gnn_setup():
        import jax, jax.numpy as jnp
        import numpy as np
        N_NODES = 12500
        N_EDGES = 200000
        D_FEAT = 48
        key = jax.random.key(seed)
        k1, k2, k3 = jax.random.split(key, 3)
        x = jax.random.normal(k1, (N_NODES, D_FEAT), dtype=jnp.float32)
        edge_index = jax.random.randint(k2, (2, N_EDGES), 0, N_NODES, dtype=jnp.int64)
        edge_weights = jax.random.uniform(k3, (N_EDGES,), dtype=jnp.float32)
        return {'x': x, 'edge_index': edge_index, 'edge_weights': edge_weights}
    _L3_gnn_all = _L3_gnn_setup()
    _L3_gnn_in = {k: v for k, v in _L3_gnn_all.items() if k in ()}
    del _L3_gnn_all
    return {'x': x, 'src': src, 'dst': dst, 'edge_attr_40': edge_attr_40, 'edge_type_4': edge_type_4, 'edge_type_8': edge_type_8, 'edge_weight': edge_weight, 'edge_weight1': edge_weight1, 'node_type_119': node_type_119, 'node_vec': node_vec, 'L0_gnn_W1': _L0_gnn_in['W1'], 'L0_gnn_b1': _L0_gnn_in['b1'], 'L0_gnn_W2': _L0_gnn_in['W2'], 'L0_gnn_b2': _L0_gnn_in['b2'], 'L0_gnn_emb': _L0_gnn_in['emb'], 'L0_gnn_adaptW': _L0_gnn_in['adaptW'], 'L0_gnn_gamma': _L0_gnn_in['gamma'], 'L0_gnn_beta': _L0_gnn_in['beta'], 'L1_gnn_W': _L1_gnn_in['W'], 'L1_gnn_b': _L1_gnn_in['b'], 'L2_gnn_weight1': _L2_gnn_in['weight1'], 'L2_gnn_weight2': _L2_gnn_in['weight2'], 'L2_gnn_bias1': _L2_gnn_in['bias1'], 'L2_gnn_bias2': _L2_gnn_in['bias2']}

def reference(x, src, dst, edge_attr_40, edge_type_4, edge_type_8, edge_weight, edge_weight1, node_type_119, node_vec, L0_gnn_W1, L0_gnn_b1, L0_gnn_W2, L0_gnn_b2, L0_gnn_emb, L0_gnn_adaptW, L0_gnn_gamma, L0_gnn_beta, L1_gnn_W, L1_gnn_b, L2_gnn_weight1, L2_gnn_weight2, L2_gnn_bias1, L2_gnn_bias2):
    import jax
    import jax.numpy as jnp

    def _L0_gnn_ref(h, edge_index, edge_attr, distances, atom_z, node_mult, batch, W1, b1, W2, b2, emb, adaptW, gamma, beta):
        import jax, jax.numpy as jnp
        import numpy as np
        CUTOFF = 6.0
        LN_EPS = 1e-05
        src, dst = (edge_index[0], edge_index[1])
        N = h.shape[0]
        gate = jax.nn.silu(edge_attr @ W1.T + b1) @ W2.T + b2
        ei = emb[atom_z[src]]
        ej = emb[atom_z[dst]]
        adapt_logit = jnp.sum(ei * (ej @ adaptW.T), axis=-1, keepdims=True)
        gate = gate + adapt_logit
        cw = jnp.where(distances < CUTOFF, 0.5 * (jnp.cos(jnp.pi * distances / CUTOFF) + 1.0), 0.0)
        mj = node_mult[dst]
        msg = gate * h[dst] * (cw * mj)[:, None]
        agg = jax.ops.segment_sum(msg, src, num_segments=N)
        tot = jax.ops.segment_sum(mj, src, num_segments=N)
        agg = agg / jnp.clip(tot, 1e-08, None)[:, None]
        x = h + agg
        mu = jnp.mean(x, axis=-1, keepdims=True)
        var = jnp.mean(jnp.square(x - mu), axis=-1, keepdims=True)
        return (x - mu) / jnp.sqrt(var + LN_EPS) * gamma + beta

    def _L1_gnn_ref(h, norm_vals, W, b, edge_index, edge_relation):
        import jax, jax.numpy as jnp
        import numpy as np
        N_NODES = 12500
        N_EDGES = 200000
        D_IN = 48
        D_OUT = 48
        N_REL = 4
        n_nodes = h.shape[0]
        dst = edge_index[0]
        src = edge_index[1]
        hs = h[src]
        outs = []
        for r in range(N_REL):
            w = jnp.where(edge_relation == r, norm_vals, jnp.float32(0.0))
            msg = hs * w[:, None]
            outs.append(jax.ops.segment_sum(msg, dst, num_segments=n_nodes))
        hcat = jnp.concatenate(outs, axis=1)
        return hcat @ W + b

    def _L2_gnn_ref(inputs, norm, weight1, weight2, bias1, bias2, src, dst, rel_type):
        import jax, jax.numpy as jnp
        import numpy as np
        N_NODES = 6250
        N_EDGES = 200000
        IN_FEAT = 48
        OUT_FEAT = 48
        NUM_RELS = 8
        h1 = jax.nn.relu(jnp.einsum('ni,rij->nrj', inputs, weight1) + bias1)
        h2 = jnp.einsum('nrj,rjo->nro', h1, weight2)
        msg = h2[src, rel_type] * norm
        agg = jax.ops.segment_sum(msg, dst, num_segments=inputs.shape[0])
        return jax.nn.relu(agg + bias2)

    def _L3_gnn_ref(x, edge_index, edge_weights):
        import jax, jax.numpy as jnp
        import numpy as np
        N_NODES = 12500
        N_EDGES = 200000
        D_FEAT = 48
        N = x.shape[0]
        row, col = (edge_index[0], edge_index[1])
        deg = jnp.zeros((N,), dtype=x.dtype).at[row].add(1.0)
        deg = jnp.maximum(deg, 1.0)
        norm = edge_weights / jnp.sqrt(deg[row] * deg[col])
        msg = x[row] * norm[:, None]
        out = jax.ops.segment_sum(msg, col, num_segments=N)
        return out
    edge_index = jnp.stack([src, dst])
    batch0 = jnp.zeros((6250,), jnp.int32)
    h = jnp.maximum(_layernorm(x, axis=-1), 0.0)
    x = x + _L0_gnn_ref(h, edge_index, edge_attr_40, edge_weight, node_type_119, node_vec, batch0, L0_gnn_W1, L0_gnn_b1, L0_gnn_W2, L0_gnn_b2, L0_gnn_emb, L0_gnn_adaptW, L0_gnn_gamma, L0_gnn_beta)
    h = jnp.maximum(_layernorm(x, axis=-1), 0.0)
    x = x + _L1_gnn_ref(h, edge_weight, L1_gnn_W, L1_gnn_b, edge_index, edge_type_4)
    h = jnp.maximum(_layernorm(x, axis=-1), 0.0)
    x = x + _L2_gnn_ref(h, edge_weight1, L2_gnn_weight1, L2_gnn_weight2, L2_gnn_bias1, L2_gnn_bias2, src, dst, edge_type_8)
    h = jnp.maximum(_layernorm(x, axis=-1), 0.0)
    x = x + _L3_gnn_ref(h, edge_index, edge_weight)
    return x

_drawn_inputs = setup_inputs


def setup_inputs(seed=0):
    import zlib

    import numpy as np

    out = dict(_drawn_inputs(seed))
    spreads = {'L0_gnn_gamma': (1.0, 0.2), 'L0_gnn_beta': (0.0, 0.1)}
    factors = {'edge_attr_40': 8.0,
     'node_vec': 8.0,
     'L0_gnn_b1': 63.917,
     'L0_gnn_b2': 39.36,
     'L0_gnn_emb': 64.0,
     'L0_gnn_adaptW': 64.0,
     'L1_gnn_b': 8.0,
     'L2_gnn_bias2': 8.0}
    for name, (base, spread) in spreads.items():
        noise = np.random.default_rng([zlib.crc32(name.encode()), seed]).standard_normal(out[name].shape)
        drawn = base * np.exp(spread * noise) if base else spread * noise
        out[name] = jnp.asarray(drawn.astype(out[name].dtype))
    for name, factor in factors.items():
        out[name] = (out[name] * factor).astype(out[name].dtype)
    return out
```

```python
import concourse.bass as bass
from concourse import mybir
from contextlib import ExitStack
import numpy as np

fp32 = mybir.dt.float32
bf16 = mybir.dt.bfloat16
i32 = mybir.dt.int32
ALU = mybir.AluOpType
ACT = mybir.ActivationFunctionType
AX = mybir.AxisListType

P = 128
N = 6250
H = 48
E = 206250
R = 40
G = 32
NTYPE = 119
NREL1, NREL2 = 4, 8
NT = -(-N // P)
NP = NT * P
T = 16
CH = T * P
NC = -(-E // CH)
EP = NC * CH
NE = NC * T
ITEMS = NC + NT - 1
REC = 2 * H + G + 4
SRC, ROW1, WEIGHT = 2 * H + G + 1, 2 * H + G + 2, 2 * H + G + 3
TW = H + G + 1
CUTOFF = 6.0
EPS = 1e-5
HALFPI = float(np.pi / 2)


class Memory:

    def in_src_order(self):
        return self.cut[:, :], self.place[:, :], self.row1[:, :].bitcast(fp32)


def allocate(nc, ctx):
    m = Memory()

    def sb(name, shape, dt=fp32):
        return ctx.enter_context(nc.sbuf_tensor(name, shape, dt))

    m.srcf = sb("srcf", [P, NE])
    m.dstf = sb("dstf", [P, NE])
    m.w = sb("w", [P, NE])
    m.w1 = sb("w1", [P, NE])
    m.cut = sb("cut", [P, NE])
    m.row1 = sb("row1", [P, NE], i32)
    m.row2 = sb("row2", [P, NE], i32)
    m.place = sb("place", [P, NE], i32)
    m.x = sb("x_res", [P, NT, H])
    m.h = sb("h_norm", [P, NT, H])
    m.acc = sb("acc", [P, NT, H + 2])
    m.emb = sb("emb_rows", [P, NT, 2 * G])
    m.mult = sb("mult", [P, NT])
    m.rdeg = sb("rdeg", [P, NT])
    m.iota = sb("iota", [P, P])
    m.node = sb("node", [P, NT])
    m.base = sb("base", [P, NT])
    m.ident = sb("ident", [P, P])
    m.lower = sb("lower", [P, P])
    m.ones = sb("ones", [P, P])
    m.sfirst = sb("sfirst", [1, NC], i32)
    m.slast = sb("slast", [1, NC], i32)
    m.dfirst = sb("dfirst", [1, NC], i32)
    m.dlast = sb("dlast", [1, NC], i32)
    m.stat = sb("stat", [P, 4, NT])
    m.zero = sb("zero_bf", [P, 512], bf16)
    m.work = sb("work", [P, WORK + NT * TW])
    m.t0 = m.work[:, WORK:].rearrange("p (j f) -> p j f", f=TW)
    m.ichunk = sb("ichunk", [1, ITEMS], i32)
    m.itile = sb("itile", [1, ITEMS], i32)
    m.ibase = sb("item_base", [P, ITEMS])
    m.unsorted = sb("unsorted", [1, 1], i32)
    return m


WORK = 13696
SORTED = R + 6


def carve(m, *shapes, all_of_it=False):
    at, out = 0, []
    for shape in shapes:
        n = int(np.prod(shape))
        v = m.work[:, at:at + n]
        if len(shape) == 2:
            v = v.rearrange("p (a b) -> p a b", b=shape[1])
        out.append(v)
        at += n
    assert at <= (WORK + NT * TW if all_of_it else WORK), at
    return out


def over_steps(eng, total, ring, step):
    for n in range(ring):
        step(n, 0, n)
    rounds = total // ring
    with eng.Fori(1, rounds) as v:
        u = eng.snap(v, min_val=1, max_val=rounds - 1)
        for s in range(ring):
            step(u * ring + s, u, s)
    for n in range(rounds * ring, total):
        step(n, rounds, n % ring)


def over_chunks(eng, chunk, ring=2):
    over_steps(eng, NC, ring, chunk)


def before(n, least):
    return isinstance(n, int) and n < least


def col(n):
    return bass.ds(n, 1) if not isinstance(n, int) else slice(n, n + 1)


def over_items(eng, k, first, last, c, item):
    at = bass.ds(c, 1) if not isinstance(c, int) else slice(c, c + 1)
    lo = eng.value_load(first[0:1, at], min_val=0, max_val=NT - 1)
    hi = eng.value_load(last[0:1, at], min_val=0, max_val=NT - 1)
    with eng.Fori(lo, hi + 1) as v:
        item(eng.snap(k, min_val=0, max_val=NC + NT), eng.snap(v, min_val=0, max_val=NT - 1))
        eng.reg_add(k, k, 1)


def cols(c, n=T):
    return bass.ds(c * n, n) if not isinstance(c, int) else slice(c * n, (c + 1) * n)


class Chain:

    def __init__(self, eng, sem):
        self.eng, self.sem, self.n = eng, sem, 0

    def __call__(self, step):
        self.n += 1
        step.then_inc(self.sem, 1)
        self.eng.wait_ge(self.sem, self.n)


def layer_norm(nc, dve, link, m, src, out, scratch, var_ready, std_ready, nth, gamma=None, beta=None):
    mean, var = m.stat[:, 0, :], m.stat[:, 1, :]
    wide = lambda a: a.unsqueeze(2).to_broadcast([P, NT, H])
    link(nc.vector.reduce_sum(mean, src, AX.X))
    link(nc.vector.tensor_scalar(mean, mean, -1.0 / H, None, ALU.mult))
    link(nc.vector.tensor_tensor(out, src, wide(mean), ALU.add))
    link(nc.vector.tensor_tensor(scratch, out, out, ALU.mult))
    link(nc.vector.reduce_sum(var, scratch, AX.X))
    nc.vector.tensor_scalar(var, var, 1.0 / H, EPS, ALU.mult, ALU.add).then_inc(var_ready, 1)
    dve.wait_ge(std_ready, nth)
    link(nc.vector.reciprocal(var, m.stat[:, 2, :]))
    link(nc.vector.tensor_tensor(out, out, wide(var), ALU.mult))
    if gamma is None:
        link(nc.vector.tensor_scalar(out, out, 0.0, None, ALU.max))
    else:
        feat = lambda a: a.unsqueeze(1).to_broadcast([P, NT, H])
        link(nc.vector.tensor_tensor(out, out, feat(gamma), ALU.mult))
        link(nc.vector.tensor_tensor(out, out, feat(beta), ALU.add))


def square_root(nc, act, m, var_ready, std_ready, nth):
    act.wait_ge(var_ready, nth)
    nc.scalar.activation(m.stat[:, 2, :], m.stat[:, 1, :], ACT.Sqrt).then_inc(std_ready, 1)


def sort_buffers(nc, ctx, m, name):
    b = Memory()
    sb = lambda n, s, d=fp32: ctx.enter_context(nc.sbuf_tensor(name + n, s, d))
    b.count = sb("count", [P, NT])
    b.offset = sb("offset", [P, NT])
    b.end = sb("end", [P, NT])
    b.before_ps = ctx.enter_context(nc.psum_tensor(name + "before_ps", [P, NT], fp32))
    b.total_ps = ctx.enter_context(nc.psum_tensor(name + "total_ps", [P, NT], fp32))
    b.counted = ctx.enter_context(nc.semaphore(name + "counted"))
    b.summed = ctx.enter_context(nc.semaphore(name + "summed"))
    return b


def sort_places(nc, dve, link, b, raw, bucket_raw, bucket, mask, scan, one, place, out):
    link(nc.vector.tensor_scalar(bucket_raw, raw, 7, None, ALU.arith_shift_right))
    link(nc.vector.tensor_copy(bucket, bucket_raw))
    for t in range(NT):
        link(nc.vector.tensor_scalar(mask, bucket, float(t), 0.0, ALU.is_equal, ALU.add,
                                     accum_out=b.count[:, t:t + 1]))
    link(nc.vector.memset(place, -1.0))
    nc.vector.engine_nop().then_inc(b.counted, 1)
    dve.wait_ge(b.summed, 1)
    link(nc.vector.tensor_copy(b.offset[:, :], b.before_ps[:, :]))
    link(nc.vector.tensor_tensor_scan(b.end[:, :], one[:, 0:NT], b.total_ps[:, :], 0.0, ALU.mult, ALU.add))
    link(nc.vector.tensor_tensor(b.offset[:, 1:NT], b.offset[:, 1:NT], b.end[:, 0:NT - 1], ALU.add))
    for t in range(NT):
        link(nc.vector.tensor_scalar(mask, bucket, float(t), None, ALU.is_equal))
        link(nc.vector.tensor_tensor_scan(scan, one, mask, b.offset[:, t:t + 1], ALU.mult, ALU.add))
        link(nc.vector.tensor_tensor(scan, scan, mask, ALU.mult))
        link(nc.vector.tensor_tensor(place, place, scan, ALU.add))
    link(nc.vector.tensor_copy(out, place))


def sort_sums(nc, pe, m, b):
    pe.wait_ge(b.counted, 1)
    nc.tensor.matmul(b.before_ps[:, :], m.lower[:, :], b.count[:, :], start=True, stop=True)
    nc.tensor.matmul(b.total_ps[:, :], m.ones[:, :], b.count[:, :], start=True, stop=True).then_inc(b.summed, 1)


def raw_views(m):
    return m.place[:, :], m.work[:, 0:NE].bitcast(i32)


def load(nc, ctx, m, ins, dram):
    raw_src, raw_dst = raw_views(m)
    _, after, tile_a, tile_b, diff = carve(m, [NE], [NE], [NE], [NE], [NE])
    after = after.bitcast(i32)
    worst, row = m.stat[:, 0, 0:1], m.work[0:1, 5 * NE:5 * NE + P]
    sb = lambda n, s, d=fp32: ctx.enter_context(nc.sbuf_tensor(n, s, d))
    icol, inode, ibase = sb("icol", [P, P], i32), sb("inode", [P, NT], i32), sb("ibase", [P, NT], i32)
    worst_ps = ctx.enter_context(nc.psum_tensor("worst_ps", [1, P], fp32))
    sem = lambda n: ctx.enter_context(nc.semaphore(n))
    dst_in, rest_in, iotas, dchain, worst_ready, worst_row = (
        sem("dst_in"), sem("rest_in"), sem("iotas"), sem("load_chain"), sem("worst_ready"), sem("worst_row"))

    with nc.Block() as block:

        @block.sync
        def _(sp):
            sp.dma_start(raw_dst, ins.dst_laid).then_inc(dst_in, 16)
            sp.dma_start(after, ins.dst_after).then_inc(dst_in, 16)
            for to, what in ((raw_src, ins.src), (m.w[:, :], ins.w), (m.w1[:, :], ins.w1),
                             (m.row1[:, :], ins.type4), (m.row2[:, :], ins.type8)):
                sp.dma_start(to, what).then_inc(rest_in, 16)
            sp.wait_ge(rest_in, 80)

        @block.gpsimd
        def _(pool):
            nc.gpsimd.iota(icol[:, :], [[1, P]], 0, 0)
            nc.gpsimd.iota(inode[:, :], [[P, NT]], 0, 1)
            nc.gpsimd.iota(ibase[:, :], [[P, NT]], 0, 0).then_inc(iotas, 1)

        @block.vector
        def _(dve):
            link = Chain(dve, dchain)
            dve.wait_ge(iotas, 1)
            nc.vector.tensor_copy(m.iota[:, :], icol[:, :])
            nc.vector.tensor_copy(m.base[:, :], ibase[:, :])
            nc.vector.memset(m.zero[:, :], 0.0)
            nc.vector.memset(m.ones[:, :], 1.0)
            link(nc.vector.tensor_copy(m.node[:, :], inode[:, :]))
            number = m.node[:, 0:1]
            nc.vector.tensor_scalar(m.lower[:, :], m.iota[:, :], number, None, ALU.is_gt)
            link(nc.vector.tensor_scalar(m.ident[:, :], m.iota[:, :], number, None, ALU.is_equal))
            dve.wait_ge(dst_in, 32)
            link(nc.vector.tensor_scalar(tile_a.bitcast(i32), raw_dst, 7, None, ALU.arith_shift_right))
            link(nc.vector.tensor_scalar(tile_b.bitcast(i32), after, 7, None, ALU.arith_shift_right))
            link(nc.vector.tensor_tensor(diff, tile_a.bitcast(i32), tile_b.bitcast(i32), ALU.subtract))
            nc.vector.tensor_reduce(worst, diff, AX.X, ALU.max).then_inc(worst_ready, 1)
            dve.wait_ge(worst_row, 1)
            link(nc.vector.tensor_reduce(row[0:1, 0:1], worst_ps[0:1, :], AX.X, ALU.max))
            link(nc.vector.tensor_scalar(m.unsorted[:, :], row[0:1, 0:1], 0.0, None, ALU.is_gt))

        @block.tensor
        def _(pe):
            pe.wait_ge(worst_ready, 1)
            nc.tensor.matmul(worst_ps[0:1, :], worst, m.ident[:, :], start=True, stop=True).then_inc(worst_row, 1)


def reorder(nc, ctx, m, ins, dram):
    raw_src, raw_dst = raw_views(m)
    _, bucket, mask, scan, one, place, edge = carve(m, [NE], [NE], [NE], [NE], [NE], [NE], [T, SORTED])
    fields = (raw_src, raw_dst, m.w[:, :], m.w1[:, :], m.row1[:, :], m.row2[:, :])
    spot_all = m.acc[:, :, :].rearrange("p j f -> p (j f)")[:, 0:NE].bitcast(i32)
    spot = ctx.enter_context(nc.sbuf_tensor("spot", [P, T], i32))
    b = sort_buffers(nc, ctx, m, "r_")
    sem = lambda n: ctx.enter_context(nc.semaphore(n))
    dchain, attr_in, filled, scattered, fields_in, dst_out, placed = (
        sem("r_chain"), sem("r_attr"), sem("r_filled"), sem("r_scattered"), sem("r_fields"), sem("r_dst"), sem("r_placed"))
    buffer_free, pool_turns, sp_turns = sem("r_free"), sem("r_pool_turns"), sem("r_sp_turns")

    def flag(eng):
        return eng.value_load(m.unsorted[0:1, 0:1], min_val=0, max_val=1)

    with nc.Block() as block:

        @block.sync
        def _(sp):
            with sp.If(flag(sp)), nc.allow_non_contiguous_dma(reason="the general path"):
                sp.wait_ge(placed, 1)
                with sp.Fori(0, NC) as v:
                    c = sp.snap(v, min_val=0, max_val=NC - 1)
                    sp.wait_ge(buffer_free, c + 1)
                    sp.sem_inc(sp_turns, 1)
                    sp.dma_start(edge[:, :, 0:R], ins.attr.rearrange("(c p t) r -> p c t r", p=P, t=T)[:, col(c), :, :]
                                 .rearrange("p c t r -> p (c t) r")).then_inc(attr_in, 16)
                sp.wait_ge(buffer_free, NC + 1)
                with sp.Fori(0, NC) as v:
                    c = sp.snap(v, min_val=0, max_val=NC - 1)
                    for f, to in enumerate(fields):
                        to = to if f in (2, 3) else to.bitcast(fp32)
                        sp.dma_start(to[:, cols(c)],
                                     dram.sorted.rearrange("(c p t) f -> p c t f", p=P, t=T)[:, col(c), :, R + f]
                                     .rearrange("p c t -> p (c t)")).then_inc(fields_in, 16)
                sp.wait_ge(fields_in, 16 * NC * len(fields))
                sp.dma_start(dram.dst.rearrange("(c p t) -> p c t", p=P, t=T),
                             raw_dst.rearrange("p (c t) -> p c t", t=T)).then_inc(dst_out, 16)
                sp.wait_ge(dst_out, 16)

        @block.tensor
        def _(pe):
            with pe.If(flag(pe)):
                sort_sums(nc, pe, m, b)

        @block.vector
        def _(dve):
            with dve.If(flag(dve)):
                link = Chain(dve, dchain)
                link(nc.vector.memset(one, 1.0))
                sort_places(nc, dve, link, b, raw_dst, spot_all, bucket, mask, scan, one, place, spot_all)
                nc.vector.engine_nop().then_inc(placed, 1)
                with dve.Fori(0, NC) as v:
                    c = dve.snap(v, min_val=0, max_val=NC - 1)
                    dve.wait_ge(attr_in, c * 16 + 16)
                    for f, have in enumerate(fields):
                        to = edge[:, :, R + f]
                        nc.vector.tensor_copy(to if f in (2, 3) else to.bitcast(i32), have[:, cols(c)])
                    nc.vector.tensor_copy(spot[:, :], spot_all[:, cols(c)]).then_inc(filled, 1)

        @block.gpsimd
        def _(pool):
            with pool.If(flag(pool)):
                pool.sem_inc(buffer_free, 1)
                with pool.Fori(0, NC) as v:
                    c = pool.snap(v, min_val=0, max_val=NC - 1)
                    pool.wait_ge(filled, c + 1)
                    pool.sem_inc(pool_turns, 1)
                    for t in range(T):
                        nc.gpsimd.indirect_dma_start(
                            out=dram.sorted, out_offset=bass.IndirectOffsetOnAxis(ap=spot[:, t:t + 1], axis=0),
                            in_=edge[:, t, :], in_offset=None).then_inc(scattered, 16)
                    pool.wait_ge(scattered, c * (16 * T) + 16 * T)
                    pool.sem_inc(buffer_free, 1)


def setup(nc, ctx, m, ins, dram):
    raw_src, raw_dst = raw_views(m)
    _, bucket, mask, scan, one = carve(m, [NE], [NE], [NE], [NE], [NE])
    bucket_raw = m.cut[:, :].bitcast(i32)
    b = sort_buffers(nc, ctx, m, "s_")
    sb = lambda n, s, d=fp32: ctx.enter_context(nc.sbuf_tensor(n, s, d))
    edge0, tiles = sb("edge0", [1, NC]), sb("tiles", [1, NC])
    iitem, item, item_chunk = sb("iitem", [1, ITEMS], i32), sb("item", [1, ITEMS]), sb("item_chunk", [1, ITEMS])
    iedge = sb("iedge", [1, NC], i32)
    draw = sb("draw", [1, 2, NC], i32)
    ztype = sb("ztype", [P, NT], i32)
    embT, adaptT, both = sb("embT", [G, NTYPE]), sb("adaptT", [G, G]), sb("both", [NTYPE, 2 * G])
    ps_emb = ctx.enter_context(nc.psum_tensor("ps_emb", [P, G], fp32))
    ps_base = ctx.enter_context(nc.psum_tensor("ps_base", [P, ITEMS], fp32))
    sem = lambda n: ctx.enter_context(nc.semaphore(n))
    x_in, emb_in, iotas, emb_mm, both_ready, both_out, emb_rows_in, ends_in = (
        sem("x_in"), sem("emb_in"), sem("s_iotas"), sem("emb_mm"), sem("both_ready"), sem("both_out"),
        sem("emb_rows_in"), sem("ends_in"))
    var_ready, std_ready, dchain, cut_ready, angle, item_ready, base_ready = (
        sem("var0"), sem("std0"), sem("setup_chain"), sem("cut_ready"), sem("angle"), sem("item_ready"), sem("base_ready"))
    wide48 = lambda a: a.unsqueeze(2).to_broadcast([P, NT, H])

    with nc.Block() as block:

        @block.sync
        def _(sp):
            with nc.allow_non_contiguous_dma(reason="small arrays, once"):
                sp.dma_start(embT[:, :], ins.embT).then_inc(emb_in, 16)
                sp.dma_start(adaptT[:, :], ins.adaptT).then_inc(emb_in, 16)
                sp.dma_start(both[:, 0:G], ins.emb).then_inc(emb_in, 16)
                sp.dma_start(ztype[:, :], ins.ztype).then_inc(emb_in, 16)
                sp.dma_start(m.x[:, :, :], ins.x.rearrange("(j p) f -> p j f", p=P)).then_inc(x_in, 16)
                sp.dma_start(m.mult[:, :], ins.mult).then_inc(x_in, 16)
                sp.dma_start(draw[0:1, 0, :], raw_dst.rearrange("p (c t) -> p c t", t=T)[0:1, :, 0]).then_inc(ends_in, 16)
                sp.dma_start(draw[0:1, 1, :], raw_dst.rearrange("p (c t) -> p c t", t=T)[P - 1:P, :, T - 1]).then_inc(ends_in, 16)
            sp.wait_ge(both_ready, 1)
            sp.dma_start(dram.emb, both[:, :]).then_inc(both_out, 16)

        @block.gpsimd
        def _(pool):
            nc.gpsimd.iota(iedge[:, :], [[CH, NC]], 0, 0)
            nc.gpsimd.iota(iitem[:, :], [[1, ITEMS]], 0, 0).then_inc(iotas, 1)
            pool.wait_ge(emb_in, 64)
            pool.wait_ge(both_out, 16)
            for j in range(NT):
                nc.gpsimd.indirect_dma_start(
                    out=m.emb[:, j, :], out_offset=None, in_=dram.emb,
                    in_offset=bass.IndirectOffsetOnAxis(ap=ztype[:, j:j + 1], axis=0)).then_inc(emb_rows_in, 16)

        @block.tensor
        def _(pe):
            pe.wait_ge(emb_in, 64)
            nc.tensor.matmul(ps_emb[0:NTYPE, :], embT[:, :], adaptT[:, :], start=True, stop=True).then_inc(emb_mm, 1)
            sort_sums(nc, pe, m, b)
            pe.wait_ge(item_ready, 1)
            nc.tensor.matmul(ps_base[:, :], m.ones[0:1, :], item[:, :], start=True, stop=True).then_inc(base_ready, 1)

        @block.scalar
        def _(act):
            act.wait_ge(angle, 1)
            nc.scalar.activation(m.cut[:, :], m.cut[:, :], ACT.Sin).then_inc(cut_ready, 1)
            square_root(nc, act, m, var_ready, std_ready, 1)

        @block.vector
        def _(dve):
            link = Chain(dve, dchain)
            dve.wait_ge(emb_mm, 1)
            nc.vector.tensor_copy(both[:, G:2 * G], ps_emb[0:NTYPE, :]).then_inc(both_ready, 1)
            nc.vector.memset(one, 1.0)
            nc.vector.tensor_copy(m.srcf[:, :], raw_src)
            link(nc.vector.tensor_copy(m.dstf[:, :], raw_dst))
            link(nc.vector.scalar_tensor_tensor(m.row1[:, :], m.dstf[:, :], float(NREL1), m.row1[:, :], ALU.mult, ALU.add))
            link(nc.vector.scalar_tensor_tensor(m.row2[:, :], m.srcf[:, :], float(NREL2), m.row2[:, :], ALU.mult, ALU.add))
            dve.wait_ge(ends_in, 32)
            nc.vector.tensor_scalar(m.dfirst[:, :], draw[0:1, 0, :], 7, None, ALU.arith_shift_right)
            link(nc.vector.tensor_scalar(m.dlast[:, :], draw[0:1, 1, :], 7, None, ALU.arith_shift_right))

            sort_places(nc, dve, link, b, raw_src, bucket_raw, bucket, mask, scan, one, m.cut[:, :], m.place[:, :])

            link(nc.vector.scalar_tensor_tensor(mask, m.w[:, :], -1.0, m.w[:, :], ALU.mult, ALU.max))
            link(nc.vector.tensor_scalar(mask, mask, CUTOFF, None, ALU.min))
            nc.vector.tensor_scalar(m.cut[:, :], mask, -float(np.pi) / CUTOFF, HALFPI,
                                    ALU.mult, ALU.add).then_inc(angle, 1)
            link(nc.vector.tensor_scalar(scan, m.w[:, :], CUTOFF, 0.5, ALU.is_lt, ALU.mult))
            dve.wait_ge(cut_ready, 1)
            link(nc.vector.scalar_tensor_tensor(m.cut[:, :], m.cut[:, :], 1.0, scan, ALU.add, ALU.mult))

            dve.wait_ge(iotas, 1)
            nc.vector.tensor_copy(item[:, :], iitem[:, :])
            link(nc.vector.tensor_copy(edge0[:, :], iedge[:, :]))
            grid = m.work[0:1, 0:NC * NT].rearrange("p (c b) -> p c b", b=NT)
            tile_end = b.end[0:1, :].unsqueeze(1).to_broadcast([1, NC, NT])
            for out in (m.sfirst, m.slast):
                if out is m.slast:
                    link(nc.vector.tensor_scalar(edge0[:, :], edge0[:, :], float(CH - 1), None, ALU.add))
                link(nc.vector.tensor_tensor(grid, tile_end, edge0[0:1, :].unsqueeze(2).to_broadcast([1, NC, NT]),
                                             ALU.is_le))
                link(nc.vector.reduce_sum(tiles[:, :], grid, AX.X))
                link(nc.vector.tensor_copy(out[:, :], tiles[:, :]))
            link(nc.vector.tensor_tensor(tiles[:, :], tiles[:, :], item[:, 0:NC], ALU.add))
            grid = m.work[0:1, 0:(ITEMS * NC + 1) // 2 * 1].bitcast(bf16)[:, 0:ITEMS * NC].rearrange("p (k c) -> p k c", c=NC)
            link(nc.vector.tensor_tensor(grid, tiles[0:1, :].unsqueeze(1).to_broadcast([1, ITEMS, NC]),
                                         item[0:1, :].unsqueeze(2).to_broadcast([1, ITEMS, NC]), ALU.is_lt))
            link(nc.vector.reduce_sum(item_chunk[:, :], grid, AX.X))
            link(nc.vector.tensor_copy(m.ichunk[:, :], item_chunk[:, :]))
            link(nc.vector.tensor_tensor(item[:, :], item[:, :], item_chunk[:, :], ALU.subtract))
            nc.vector.tensor_copy(m.itile[:, :], item[:, :]).then_inc(item_ready, 1)
            dve.wait_ge(base_ready, 1)
            link(nc.vector.tensor_scalar(m.ibase[:, :], ps_base[:, :], float(P), None, ALU.mult))

            dve.wait_ge(x_in, 32)
            layer_norm(nc, dve, link, m, m.x[:, :, :], m.h[:, :, :],
                       m.work[:, 0:NT * H].rearrange("p (j f) -> p j f", f=H), var_ready, std_ready, 1)
            link(nc.vector.tensor_tensor(m.t0[:, :, 0:H], m.h[:, :, :], wide48(m.mult[:, :]), ALU.mult))
            dve.wait_ge(emb_rows_in, 16 * NT)
            link(nc.vector.tensor_copy(m.t0[:, :, H:H + G], m.emb[:, :, G:2 * G]))
            link(nc.vector.tensor_copy(m.t0[:, :, H + G], m.mult[:, :]))


def layer0_edges(nc, ctx, m, ins, dram):
    attr, dr0, dr1, onehot, z, rec0, rec1 = carve(m, [4, 512], [CH], [CH], [CH], [2, 512], [T, REC], [T, REC])
    rec = (rec0, rec1)
    drow = (dr0.bitcast(i32), dr1.bitcast(i32))
    sb = lambda n, s, d=fp32: ctx.enter_context(nc.sbuf_tensor(n, s, d))
    place = (sb("place_a", [P, T], i32), sb("place_b", [P, T], i32))
    w1T, w2T, b1 = sb("w1T", [R, H]), sb("w2T", [H + 1, H]), sb("b1c", [H, 1])
    pb = lambda n, s: ctx.enter_context(nc.psum_tensor(n, s, fp32))
    rows_ps = pb("rows_ps", [P, T, P])
    gate_ps = pb("gate_ps", [P, T, 64])
    z_ps = pb("z_ps", [P, 2, 512])
    sem = lambda n: ctx.enter_context(nc.semaphore(n))
    weights_in = sem("weights_in")
    attr_in = [sem(f"attr_in{g}") for g in range(4)]
    drow_in = (sem("drow_in0"), sem("drow_in1"))
    tile_in = sem("tile_in")
    onehot_ready, item_done, chunk_items = sem("onehot_ready"), sem("item_done"), sem("chunk_items")
    rows_ready, rows_scaled, rows_copied = sem("rows_ready"), sem("rows_scaled"), sem("rows_copied")
    z_ready, silu_done, gate_ready, rec_ready, ones_set = (
        sem("z_ready"), sem("silu_done"), sem("gate_ready"), sem("rec_ready"), sem("ones_set"))
    scattered = (sem("scattered0"), sem("scattered1"))
    pool_turns, pe_turns, sp_turns = sem("pool_turns"), sem("pe_turns"), sem("sp_turns")

    with nc.Block() as block:

        @block.sync
        def _(sp):
            sp.dma_start(w1T[:, :], ins.W1T).then_inc(weights_in, 16)
            sp.dma_start(w2T[:, :], ins.W2T).then_inc(weights_in, 16)
            sp.dma_start(b1[:, :], ins.b1).then_inc(weights_in, 16)
            laid = ins.attrT.rearrange("r (c g e) -> r c g e", g=4, e=512)
            found = dram.sorted.rearrange("(c p t) f -> f c t p", p=P, t=T)[0:R]

            def loads(dst_row, attributes):
                def chunk(c, u, s):
                    if not before(c, 2):
                        sp.wait_ge(chunk_items, c - 1)
                        sp.sem_inc(sp_turns, 1)
                    sp.dma_start(drow[s], dst_row.rearrange("(c e) -> c e", e=CH)[col(c), :]
                                 .to_broadcast([P, CH])).then_inc(drow_in[s], 16)
                    for g in range(4):
                        if not before(c, 1):
                            sp.wait_ge(z_ready, c * 4 + (g - 3))
                            sp.sem_inc(sp_turns, 1)
                        attributes(c, g)
                over_chunks(sp, chunk)

            unsorted = sp.value_load(m.unsorted[0:1, 0:1], min_val=0, max_val=1)
            def whole_quarter(c, g):
                sp.dma_start(attr[0:R, g, :], laid[:, col(c), g, :].rearrange("r c e -> r (c e)")).then_inc(attr_in[g], 16)

            def tile_by_tile(c, g):
                for t in range(4):
                    sp.dma_start(attr[0:R, g, t * P:(t + 1) * P],
                                 found[:, col(c), 4 * g + t, :].rearrange("r c p -> r (c p)")).then_inc(tile_in, 16)
                sp.wait_ge(tile_in, c * 256 + (g + 1) * 64)
                sp.sem_inc(attr_in[g], 16)

            with sp.If(unsorted), nc.allow_non_contiguous_dma(reason="the general path"):
                loads(dram.dst, tile_by_tile)
            with sp.Else():
                loads(ins.dst, whole_quarter)

        @block.tensor
        def _(pe):
            pe.wait_ge(weights_in, 48)
            pe.wait_ge(ones_set, 1)
            with pe.register("k_edges") as k:
                pe.reg_mov(k, 0)

                def chunk(c, u, s):
                    def hidden(g):
                        pe.wait_ge(attr_in[g], c * 16 + 16)
                        pe.sem_inc(pe_turns, 1)
                        if not (before(c, 1) and g < 2):
                            pe.wait_ge(silu_done, c * 4 + (g - 1))
                            pe.sem_inc(pe_turns, 1)
                        nc.tensor.matmul(z_ps[0:H, g % 2, :], w1T[:, :], attr[0:R, g, :],
                                         start=True, stop=True).then_inc(z_ready, 1)

                    def gates(g):
                        pe.wait_ge(silu_done, c * 4 + (g + 1))
                        if g == 0 and not before(c, 1):
                            pe.wait_ge(rec_ready, c)
                        for t in range(4):
                            last = nc.tensor.matmul(gate_ps[:, 4 * g + t, 0:H], z[0:H + 1, g % 2, t * P:(t + 1) * P],
                                                    w2T[:, :], start=True, stop=True)
                        if g == 3:
                            last.then_inc(gate_ready, 1)

                    hidden(0)
                    for g in range(1, 4):
                        hidden(g)
                        gates(g - 1)
                    gates(3)

                    if not before(c, 1):
                        pe.wait_ge(rows_copied, c)
                    for b in range(4):
                        nc.tensor.matmul(rows_ps[:, 4 * b:4 * b + 4, :].rearrange("p t f -> p (t f)"),
                                         m.zero[:, 0:P], m.zero[:, :], start=True, stop=False)

                    def item(k, j):
                        pe.wait_ge(onehot_ready, k + 1)
                        for t in range(T):
                            last = nc.tensor.matmul(rows_ps[:, t, 0:TW], onehot[:, t:CH:T],
                                                    m.t0[:, col(j), :].rearrange("p j f -> p (j f)"),
                                                    start=False, stop=False)
                        last.then_inc(item_done, 1)
                    over_items(pe, k, m.dfirst, m.dlast, c, item)
                    for b in range(4):
                        last = nc.tensor.matmul(rows_ps[:, 4 * b:4 * b + 4, :].rearrange("p t f -> p (t f)"),
                                                m.zero[:, 0:P], m.zero[:, :], start=False, stop=True)
                    last.then_inc(rows_ready, 1)
                over_chunks(pe, chunk)

        @block.scalar
        def _(act):
            act.wait_ge(ones_set, 1)
            act.wait_ge(weights_in, 48)

            def chunk(c, u, s):
                for g in range(4):
                    act.wait_ge(z_ready, c * 4 + (g + 1))
                    nc.scalar.activation(z[0:H, g % 2, :], z_ps[0:H, g % 2, :], ACT.Silu, bias=b1[:, 0:1]).then_inc(silu_done, 1)
                if not before(u, 1):
                    act.wait_ge(scattered[s], u * (16 * T))
                act.wait_ge(rows_scaled, c + 1)
                nc.scalar.copy(rec[s][:, :, 2 * H:2 * H + G + 1], rows_ps[:, :, H:TW]).then_inc(rows_copied, 1)
            over_chunks(act, chunk)

        @block.vector
        def _(dve):
            nc.vector.memset(z[0:64, :, :], 1.0).then_inc(ones_set, 1)
            with dve.register("k_edges") as k:
                dve.reg_mov(k, 0)

                def chunk(c, u, s):
                    dve.wait_ge(drow_in[s], u * 16 + 16)

                    def item(k, j):
                        nc.vector.tensor_scalar(onehot, drow[s], m.node[:, col(j)], None,
                                                ALU.is_equal).then_inc(onehot_ready, 1)
                        dve.wait_ge(item_done, k + 1)
                    over_items(dve, k, m.dfirst, m.dlast, c, item)
                    if not before(u, 1):
                        dve.wait_ge(scattered[s], u * (16 * T))
                    nc.vector.tensor_copy(place[s][:, :], m.place[:, cols(c)]).then_inc(chunk_items, 1)
                    nc.vector.tensor_copy(rec[s][:, :, SRC], m.srcf[:, cols(c)])
                    nc.vector.tensor_copy(rec[s][:, :, ROW1], m.row1[:, cols(c)])
                    nc.vector.tensor_copy(rec[s][:, :, WEIGHT], m.w[:, cols(c)])
                    dve.wait_ge(rows_ready, c + 1)
                    nc.vector.tensor_tensor(rec[s][:, :, H:2 * H], rows_ps[:, :, 0:H],
                                            m.cut[:, cols(c)].unsqueeze(2).to_broadcast([P, T, H]),
                                            ALU.mult).then_inc(rows_scaled, 1)
                    dve.wait_ge(gate_ready, c + 1)
                    dve.wait_ge(rows_scaled, c + 1)
                    nc.vector.tensor_tensor(rec[s][:, :, 0:H], gate_ps[:, :, 0:H], rec[s][:, :, H:2 * H],
                                            ALU.mult).then_inc(rec_ready, 1)
                over_chunks(dve, chunk)

        @block.gpsimd
        def _(pool):
            def chunk(c, u, s):
                pool.wait_ge(rec_ready, c + 1)
                pool.wait_ge(rows_copied, c + 1)
                pool.sem_inc(pool_turns, 1)
                for t in range(T):
                    nc.gpsimd.indirect_dma_start(
                        out=dram.rec, out_offset=bass.IndirectOffsetOnAxis(ap=place[s][:, t:t + 1], axis=0),
                        in_=rec[s][:, t, :], in_offset=None).then_inc(scattered[s], 16)
            over_chunks(pool, chunk)
            pool.wait_ge(scattered[0], 16 * T * ((NC + 1) // 2))
            pool.wait_ge(scattered[1], 16 * T * (NC // 2))


def layer0_sums(nc, ctx, m, dram):
    r0, r1, r2, o0, o1, o2, onehotT, a0, a1, m0, m1 = carve(
        m, [T, REC], [T, REC], [T, REC], [T, P], [T, P], [T, P], [T, P], [T, H], [T, H], [T, H + 2], [T, H + 2],
        all_of_it=True)
    rec, onehot, scaled, msg = (r0, r1, r2), (o0, o1, o2), (a0, a1), (m0, m1)
    prod = [a.rearrange("p a b -> p (a b)")[:, 0:T * G].rearrange("p (a b) -> p a b", b=G) for a in scaled]
    s_src, s_row1, s_w = m.in_src_order()
    sb = lambda n, s, d=fp32: ctx.enter_context(nc.sbuf_tensor(n, s, d))
    local, adapt = sb("local", [P, 2, T]), sb("adapt", [P, 2, T])
    pb = lambda n, s: ctx.enter_context(nc.psum_tensor(n, s, fp32))
    tr_ps, emb_ps, sum_ps = pb("tr_ps", [P, T, P]), pb("emb_ps", [P, 2, T, G]), pb("sum_ps", [P, 2, 512])
    sem = lambda n: ctx.enter_context(nc.semaphore(n))
    rec_in = [sem(f"rec_in{i}") for i in range(3)]
    ones_set, local_ready, onehot_ready, tr_ready, tr_copied, kept, emb_ready = (
        sem("c_ones"), sem("c_local"), sem("c_onehot"), sem("c_tr"), sem("c_copied"), sem("c_kept"), sem("c_emb"))
    prod_ready, adapt_ready, scaled_ready, msg_ready, sum_ready, acc_done = (
        sem("c_prod"), sem("c_adapt"), sem("c_scaled"), sem("c_msg"), sem("c_sum"), sem("c_acc"))
    sp_turns = sem("c_sp_turns")
    RING = 6

    with nc.Block() as block:

        @block.sync
        def _(sp):
            def item(k, u, s):
                c = sp.value_load(m.ichunk[0:1, col(k)], min_val=0, max_val=NC - 1)
                if not before(k, 3):
                    sp.wait_ge(msg_ready, k * 2 - 4)
                    sp.sem_inc(sp_turns, 1)
                    sp.wait_ge(kept, k * 3 - 6)
                    sp.sem_inc(sp_turns, 1)
                sp.dma_start(rec[s % 3].rearrange("p t f -> p (t f)"),
                             dram.rec.rearrange("(c p t) f -> p c (t f)", p=P, t=T)[:, col(c), :]
                             .rearrange("p c f -> p (c f)")).then_inc(rec_in[s % 3], 16)
            over_steps(sp, ITEMS, RING, item)

        def arrived(eng, k, u, s):
            eng.wait_ge(rec_in[s % 3], u * 32 + 16 * (s // 3 + 1))

        @block.vector
        def _(dve):
            for a in msg:
                nc.vector.memset(a, 1.0)
            nc.vector.memset(m.acc[:, :, :], 0.0).then_inc(acc_done, 1)
            nc.vector.engine_nop().then_inc(ones_set, 1)

            def build(k, u, s):
                arrived(dve, k, u, s)
                nc.vector.tensor_scalar(local[:, s % 2, :], rec[s % 3][:, :, SRC], m.ibase[:, col(k)], None,
                                        ALU.subtract).then_inc(local_ready, 1)
                dve.wait_ge(local_ready, k + 1)
                if not before(k, 3):
                    dve.wait_ge(sum_ready, k - 2)
                for t in range(T):
                    last = nc.vector.tensor_scalar(onehot[s % 3][:, t, :], m.iota[:, :], local[:, s % 2, t:t + 1], None,
                                                   ALU.is_equal)
                    if t % 4 == 3:
                        last.then_inc(onehot_ready, 1)

            def adapted(k, s):
                r = rec[s % 3]
                dve.wait_ge(emb_ready, k + 1)
                if not before(k, 2):
                    dve.wait_ge(msg_ready, k * 2 - 2)
                nc.vector.tensor_tensor(prod[s % 2], emb_ps[:, s % 2, :, :], r[:, :, 2 * H:2 * H + G],
                                        ALU.mult).then_inc(prod_ready, 1)
                dve.wait_ge(prod_ready, k + 1)
                nc.vector.reduce_sum(adapt[:, s % 2, :], prod[s % 2], AX.X).then_inc(adapt_ready, 1)
                dve.wait_ge(adapt_ready, k + 1)
                nc.vector.tensor_tensor(scaled[s % 2], r[:, :, H:2 * H],
                                        adapt[:, s % 2, :].unsqueeze(2).to_broadcast([P, T, H]),
                                        ALU.mult).then_inc(scaled_ready, 1)

            def add_up(k, s, j):
                dve.wait_ge(sum_ready, k + 1)
                dve.wait_ge(acc_done, k + 1)
                acc = m.acc[:, col(j), :].rearrange("p j f -> p (j f)")
                nc.vector.tensor_tensor(acc, acc, sum_ps[:, s % 2, 0:H + 2], ALU.add).then_inc(acc_done, 1)

            def tile_of(k):
                return dve.value_load(m.itile[0:1, col(k)], min_val=0, max_val=NT - 1)

            def item(k, u, s):
                if not before(k, 2):
                    j = tile_of(k - 2)
                build(k, u, s)
                if not before(k, 1):
                    adapted(k - 1, s + 5)
                if not before(k, 2):
                    add_up(k - 2, s + 4, j)
            over_steps(dve, ITEMS, RING, item)
            end = ITEMS % RING
            adapted(ITEMS - 1, end + 5)
            add_up(ITEMS - 2, end + 4, tile_of(ITEMS - 2))
            add_up(ITEMS - 1, end + 5, tile_of(ITEMS - 1))

        @block.gpsimd
        def _(pool):
            pool.wait_ge(ones_set, 1)

            def item(k, u, s):
                if not before(k, 2):
                    pool.wait_ge(sum_ready, k - 1)
                pool.wait_ge(scaled_ready, k + 1)
                nc.gpsimd.tensor_tensor(msg[s % 2][:, :, 0:H], scaled[s % 2], rec[s % 3][:, :, 0:H],
                                        ALU.add).then_inc(msg_ready, 1)
                nc.gpsimd.tensor_copy(msg[s % 2][:, :, H], rec[s % 3][:, :, 2 * H + G]).then_inc(msg_ready, 1)
            over_steps(pool, ITEMS, RING, item)

        @block.scalar
        def _(act):
            def item(k, u, s):
                c = act.value_load(m.ichunk[0:1, col(k)], min_val=0, max_val=NC - 1)
                arrived(act, k, u, s)
                if not before(k, 1):
                    act.wait_ge(kept, k * 3)
                for to, field in ((s_src, SRC), (s_row1, ROW1), (s_w, WEIGHT)):
                    nc.scalar.copy(to[:, cols(c)], rec[s % 3][:, :, field]).then_inc(kept, 1)
                for g in range(4):
                    act.wait_ge(tr_ready, k * 4 + (g + 1))
                    nc.scalar.copy(onehotT[:, 4 * g:4 * g + 4, :], tr_ps[:, 4 * g:4 * g + 4, :]).then_inc(tr_copied, 1)
            over_steps(act, ITEMS, RING, item)

        @block.tensor
        def _(pe):
            def sums(k, s):
                pe.wait_ge(msg_ready, k * 2 + 2)
                if not before(k, 2):
                    pe.wait_ge(acc_done, k)
                for t in range(T):
                    last = nc.tensor.matmul(sum_ps[:, s % 2, 0:H + 2], onehot[s % 3][:, t, :], msg[s % 2][:, t, :],
                                            start=(t == 0), stop=(t == T - 1))
                last.then_inc(sum_ready, 1)

            def item(k, u, s):
                j = pe.value_load(m.itile[0:1, col(k)], min_val=0, max_val=NT - 1)
                for g in range(4):
                    pe.wait_ge(onehot_ready, k * 4 + (g + 1))
                    if not before(k, 1):
                        pe.wait_ge(tr_copied, k * 4 + (g - 3))
                    for t in range(4 * g, 4 * g + 4):
                        last = nc.tensor.transpose(tr_ps[:, t, :], onehot[s % 3][:, t, :], m.ident[:, :])
                    last.then_inc(tr_ready, 1)
                emb = m.emb[:, col(j), 0:G].rearrange("p j f -> p (j f)")
                if not before(k, 2):
                    pe.wait_ge(prod_ready, k - 1)
                for g in range(4):
                    pe.wait_ge(tr_copied, k * 4 + (g + 1))
                    for t in range(4 * g, 4 * g + 4):
                        last = nc.tensor.matmul(emb_ps[:, s % 2, t, :], onehotT[:, t, :], emb, start=True, stop=True)
                last.then_inc(emb_ready, 1)
                if not before(k, 1):
                    sums(k - 1, s + 5)
            over_steps(pe, ITEMS, RING, item)
            sums(ITEMS - 1, ITEMS % RING + 5)


RING = 4


def gather_sums(nc, ctx, m, name, table, rows, weight, key, first, last_tile):
    *got, onehot = carve(m, *[[T, H]] * RING, [T, P])
    sb = lambda n, s, d=fp32: ctx.enter_context(nc.sbuf_tensor(name + n, s, d))
    row = [sb(f"row{i}", [P, T], i32) for i in range(RING)]
    local = sb("local", [P, T])
    sum_ps = ctx.enter_context(nc.psum_tensor(name + "sum_ps", [P, H], fp32))
    sem = lambda n: ctx.enter_context(nc.semaphore(name + n))
    gathered = [sem(f"gathered{i}") for i in range(RING)]
    pool_turns = sem("pool_turns")
    row_ready, got_used, onehot_ready, sum_ready, acc_done, dchain = (
        sem("row_ready"), sem("got_used"), sem("onehot"), sem("sum"), sem("acc"), sem("chain"))

    with nc.Block() as block:

        @block.scalar
        def _(act):
            def chunk(c, u, s):
                if not before(u, 1):
                    act.wait_ge(gathered[s], u * (16 * T))
                nc.scalar.copy(row[s][:, :], rows[:, cols(c)]).then_inc(row_ready, 1)
            over_chunks(act, chunk, RING)

        @block.gpsimd
        def _(pool):
            def chunk(c, u, s):
                pool.wait_ge(row_ready, c + 1)
                if not before(c, RING):
                    pool.wait_ge(got_used, c - (RING - 1))
                pool.sem_inc(pool_turns, 1)
                for t in range(T):
                    nc.gpsimd.indirect_dma_start(
                        out=got[s][:, t, :], out_offset=None, in_=table,
                        in_offset=bass.IndirectOffsetOnAxis(ap=row[s][:, t:t + 1], axis=0)).then_inc(gathered[s], 16)
            over_chunks(pool, chunk, RING)

        @block.vector
        def _(dve):
            nc.vector.memset(m.acc[:, :, :], 0.0).then_inc(acc_done, 1)
            with dve.register(name + "k") as k:
                dve.reg_mov(k, 0)

                def chunk(c, u, s):
                    dve.wait_ge(gathered[s], u * (16 * T) + 16 * T)

                    def item(k, j):
                        nc.vector.tensor_scalar(local[:, :], key[:, cols(c)], m.base[:, bass.ds(j, 1)], None,
                                                ALU.subtract).then_inc(dchain, 1)
                        dve.wait_ge(dchain, k + 1)
                        for t in range(T):
                            at = c * T + t
                            wt = weight[:, at:at + 1] if isinstance(at, int) else weight[:, bass.ds(at, 1)]
                            last = nc.vector.tensor_scalar(onehot[:, t, :], m.iota[:, :], local[:, t:t + 1], wt,
                                                           ALU.is_equal, ALU.mult)
                            if t % 4 == 3:
                                last.then_inc(onehot_ready, 1)
                        dve.wait_ge(sum_ready, k + 1)
                        dve.wait_ge(acc_done, k + 1)
                        acc = m.acc[:, bass.ds(j, 1), 0:H].rearrange("p j f -> p (j f)")
                        nc.vector.tensor_tensor(acc, acc, sum_ps[:, :], ALU.add).then_inc(acc_done, 1)
                    over_items(dve, k, first, last_tile, c, item)
                    nc.vector.engine_nop().then_inc(got_used, 1)
                over_chunks(dve, chunk, RING)

        @block.tensor
        def _(pe):
            with pe.register(name + "k") as k:
                pe.reg_mov(k, 0)

                def chunk(c, u, s):
                    def item(k, j):
                        for t in range(T):
                            if t % 4 == 0:
                                pe.wait_ge(onehot_ready, k * 4 + (t // 4 + 1))
                            last = nc.tensor.matmul(sum_ps[:, :], onehot[:, t, :], got[s][:, t, :],
                                                    start=(t == 0), stop=(t == T - 1))
                        last.then_inc(sum_ready, 1)
                    over_items(pe, k, first, last_tile, c, item)
                over_chunks(pe, chunk, RING)


GN = 7
NG = NT // GN
assert NG * GN == NT


def node_layer1(nc, ctx, m, ins, dram):
    scratch, hT, y = carve(m, [NT, H], [GN, P], [GN, NREL1 * H])
    sb = lambda n, s, d=fp32: ctx.enter_context(nc.sbuf_tensor(n, s, d))
    gamma, beta, w = sb("gamma", [P, H]), sb("beta", [P, H]), sb("w_rel", [H, NREL1 * H])
    pb = lambda n, s: ctx.enter_context(nc.psum_tensor(n, s, fp32))
    hT_ps, y_ps = pb("hT_ps", [P, 8, P]), pb("y_ps", [P, 8, 256])
    sem = lambda n: ctx.enter_context(nc.semaphore(n))
    in_sem, var_ready, std_ready, dchain, h_ready = sem("n1_in"), sem("n1_var"), sem("n1_std"), sem("n1_chain"), sem("n1_h")
    tr_ready, tr_copied, y_ready, y_copied, y_out = sem("n1_tr"), sem("n1_trc"), sem("n1_y"), sem("n1_yc"), sem("n1_out")
    wide = lambda a: a.unsqueeze(2).to_broadcast([P, NT, H])

    with nc.Block() as block:

        @block.sync
        def _(sp):
            sp.dma_start(gamma[:, :], ins.gamma.to_broadcast([P, H])).then_inc(in_sem, 16)
            sp.dma_start(beta[:, :], ins.beta.to_broadcast([P, H])).then_inc(in_sem, 16)
            sp.dma_start(w[:, :].rearrange("i (r o) -> i r o", o=H), ins.W.rearrange("(r i) o -> i r o", i=H)).then_inc(in_sem, 16)
            for q in range(NG):
                sp.wait_ge(y_copied, q + 1)
                sp.dma_start(dram.tab1.rearrange("(j p r) f -> p j (r f)", p=P, r=NREL1)[:, q * GN:(q + 1) * GN, :],
                             y).then_inc(y_out, 16)
            sp.wait_ge(y_out, 16 * NG)

        @block.scalar
        def _(act):
            for n in (1, 2, 3):
                square_root(nc, act, m, var_ready, std_ready, n)

        @block.vector
        def _(dve):
            link = Chain(dve, dchain)
            total, count = m.stat[:, 3, :], m.stat[:, 1, :]
            dve.wait_ge(in_sem, 48)
            link(nc.vector.tensor_scalar(total, m.acc[:, :, H], 1e-8, None, ALU.max))
            link(nc.vector.reciprocal(total, total))
            link(nc.vector.tensor_tensor(m.acc[:, :, 0:H], m.acc[:, :, 0:H], wide(total), ALU.mult))
            link(nc.vector.tensor_tensor(m.acc[:, :, 0:H], m.acc[:, :, 0:H], m.h[:, :, :], ALU.add))
            layer_norm(nc, dve, link, m, m.acc[:, :, 0:H], m.h[:, :, :], scratch, var_ready, std_ready, 1,
                       gamma[:, :], beta[:, :])
            link(nc.vector.tensor_tensor(m.x[:, :, :], m.x[:, :, :], m.h[:, :, :], ALU.add))
            nc.vector.tensor_scalar(count, m.acc[:, :, H + 1], 1.0, None, ALU.max).then_inc(var_ready, 1)
            dve.wait_ge(std_ready, 2)
            link(nc.vector.reciprocal(m.rdeg[:, :], m.stat[:, 2, :]))
            layer_norm(nc, dve, link, m, m.x[:, :, :], m.h[:, :, :], scratch, var_ready, std_ready, 3)
            nc.vector.engine_nop().then_inc(h_ready, 1)
            for q in range(NG):
                dve.wait_ge(tr_ready, q + 1)
                nc.vector.tensor_copy(hT[0:H, :, :], hT_ps[0:H, 0:GN, :]).then_inc(tr_copied, 1)
                dve.wait_ge(y_ready, q + 1)
                if q:
                    dve.wait_ge(y_out, 16 * q)
                nc.vector.tensor_copy(y, y_ps[:, 0:GN, 0:NREL1 * H]).then_inc(y_copied, 1)

        @block.tensor
        def _(pe):
            pe.wait_ge(h_ready, 1)
            for q in range(NG):
                for t in range(GN):
                    last = nc.tensor.transpose(hT_ps[0:H, t, :], m.h[:, q * GN + t, :], m.ident[:, :])
                last.then_inc(tr_ready, 1)
                pe.wait_ge(tr_copied, q + 1)
                if q:
                    pe.wait_ge(y_copied, q)
                for t in range(GN):
                    last = nc.tensor.matmul(y_ps[:, t, 0:NREL1 * H], hT[0:H, t, :], w[:, :], start=True, stop=True)
                last.then_inc(y_ready, 1)


def node_layer2(nc, ctx, m, ins, dram):
    scratch, hT, mid, y = carve(m, [NT, H], [GN, P], [4, GN * P], [GN, NREL2 * H])
    NPAIR = NREL2 // 2
    sb = lambda n, s, d=fp32: ctx.enter_context(nc.sbuf_tensor(n, s, d))
    bias = sb("n2_bias", [P, H])
    wa, wb, ba = sb("wa", [H, NREL2 * H]), sb("wb", [2 * H, NPAIR, 2 * H]), sb("ba", [2 * H, 1])
    pb = lambda n, s: ctx.enter_context(nc.psum_tensor(n, s, fp32))
    hT_ps, mid_ps, y_ps = pb("n2_hT_ps", [P, 8, P]), pb("mid_ps", [P, 2, 512]), pb("n2_y_ps", [P, 4, 512])
    HALF = (4 * P, 3 * P)
    sem = lambda n: ctx.enter_context(nc.semaphore(n))
    in_sem, z_ready, var_ready, std_ready, dchain, h_ready = (
        sem("n2_in"), sem("n2_zero"), sem("n2_var"), sem("n2_std"), sem("n2_chain"), sem("n2_h"))
    tr_ready, tr_copied, mid_ready, mid_done, y_ready, y_copied, y_out = (
        sem("n2_tr"), sem("n2_trc"), sem("n2_mid"), sem("n2_midc"), sem("n2_y"), sem("n2_yc"), sem("n2_out"))

    with nc.Block() as block:

        @block.sync
        def _(sp):
            sp.wait_ge(z_ready, 1)
            sp.dma_start(bias[:, :], ins.b.to_broadcast([P, H])).then_inc(in_sem, 16)
            sp.dma_start(wa[:, :].rearrange("i (r o) -> i r o", o=H), ins.weight1.rearrange("r i o -> i r o")).then_inc(in_sem, 16)
            for a in (0, 1):
                sp.dma_start(wb[a * H:(a + 1) * H, :, a * H:(a + 1) * H],
                             ins.weight2.rearrange("(q a) i o -> a i q o", a=2)[a]).then_inc(in_sem, 16)
                sp.dma_start(ba[a * H:(a + 1) * H, :], ins.bias1).then_inc(in_sem, 16)
            for q in range(NG):
                sp.wait_ge(y_copied, (q + 1) * GN)
                sp.dma_start(dram.tab2.rearrange("(j p r) f -> p j (r f)", p=P, r=NREL2)[:, q * GN:(q + 1) * GN, :],
                             y).then_inc(y_out, 16)
            sp.wait_ge(y_out, 16 * NG)

        @block.scalar
        def _(act):
            square_root(nc, act, m, var_ready, std_ready, 1)
            act.wait_ge(in_sem, 96)
            for q in range(NG):
                for r in range(NPAIR):
                    for a, at in ((0, 0), (1, 4 * P)):
                        n = (q * NPAIR + r) * 2 + a
                        act.wait_ge(mid_ready, n + 1)
                        nc.scalar.activation(mid[0:2 * H, r, at:at + HALF[a]], mid_ps[0:2 * H, a, 0:HALF[a]],
                                             ACT.Relu, bias=ba[:, 0:1]).then_inc(mid_done, 1)

        @block.vector
        def _(dve):
            link = Chain(dve, dchain)
            nc.vector.memset(wb[:, :, :], 0.0).then_inc(z_ready, 1)
            dve.wait_ge(in_sem, 96)
            link(nc.vector.tensor_tensor(m.x[:, :, :], m.x[:, :, :], m.acc[:, :, 0:H], ALU.add))
            link(nc.vector.tensor_tensor(m.x[:, :, :], m.x[:, :, :],
                                         bias[:, :].unsqueeze(1).to_broadcast([P, NT, H]), ALU.add))
            layer_norm(nc, dve, link, m, m.x[:, :, :], m.h[:, :, :], scratch, var_ready, std_ready, 1)
            nc.vector.engine_nop().then_inc(h_ready, 1)
            for q in range(NG):
                dve.wait_ge(tr_ready, q + 1)
                nc.vector.tensor_copy(hT[0:H, :, :], hT_ps[0:H, 0:GN, :]).then_inc(tr_copied, 1)
                for t in range(GN):
                    dve.wait_ge(y_ready, q * GN + t + 1)
                    if t == 0 and q:
                        dve.wait_ge(y_out, 16 * q)
                    nc.vector.tensor_copy(y[:, t, :], y_ps[:, (q * GN + t) % 4, 0:NREL2 * H]).then_inc(y_copied, 1)

        @block.tensor
        def _(pe):
            pe.wait_ge(h_ready, 1)
            pe.wait_ge(in_sem, 96)
            for q in range(NG):
                for t in range(GN):
                    last = nc.tensor.transpose(hT_ps[0:H, t, :], m.h[:, q * GN + t, :], m.ident[:, :])
                last.then_inc(tr_ready, 1)
                pe.wait_ge(tr_copied, q + 1)
                flat = hT.rearrange("p a b -> p (a b)")
                for r in range(NPAIR):
                    for a, at in ((0, 0), (1, 4 * P)):
                        n = (q * NPAIR + r) * 2 + a
                        if n >= 2:
                            pe.wait_ge(mid_done, n - 1)
                        nc.tensor.matmul(mid_ps[0:2 * H, a, 0:HALF[a]], wa[:, 2 * H * r:2 * H * (r + 1)],
                                         flat[0:H, at:at + HALF[a]], start=True, stop=True).then_inc(mid_ready, 1)
                pe.wait_ge(mid_done, (q + 1) * NPAIR * 2)
                for t in range(GN):
                    n = q * GN + t
                    if n >= 4:
                        pe.wait_ge(y_copied, n - 3)
                    for r in range(NPAIR):
                        last = nc.tensor.matmul(y_ps[:, n % 4, 2 * H * r:2 * H * (r + 1)],
                                                mid[0:2 * H, r, t * P:(t + 1) * P], wb[:, r, :],
                                                start=True, stop=True)
                    last.then_inc(y_ready, 1)


def node_layer3(nc, ctx, m, ins, dram):
    scratch, = carve(m, [NT, H])
    bias = ctx.enter_context(nc.sbuf_tensor("n3_bias", [P, H], fp32))
    sem = lambda n: ctx.enter_context(nc.semaphore(n))
    in_sem, var_ready, std_ready, dchain, tab_out, h_ready = (
        sem("n3_in"), sem("n3_var"), sem("n3_std"), sem("n3_chain"), sem("n3_out"), sem("n3_h"))

    with nc.Block() as block:

        @block.sync
        def _(sp):
            sp.dma_start(bias[:, :], ins.bias2.to_broadcast([P, H])).then_inc(in_sem, 16)
            sp.wait_ge(h_ready, 1)
            sp.dma_start(dram.tab3.rearrange("(j p) f -> p j f", p=P), m.h[:, :, :]).then_inc(tab_out, 16)
            sp.wait_ge(tab_out, 16)

        @block.scalar
        def _(act):
            square_root(nc, act, m, var_ready, std_ready, 1)

        @block.vector
        def _(dve):
            link = Chain(dve, dchain)
            dve.wait_ge(in_sem, 16)
            link(nc.vector.tensor_tensor(m.acc[:, :, 0:H], m.acc[:, :, 0:H],
                                         bias[:, :].unsqueeze(1).to_broadcast([P, NT, H]), ALU.add))
            link(nc.vector.tensor_scalar(m.acc[:, :, 0:H], m.acc[:, :, 0:H], 0.0, None, ALU.max))
            link(nc.vector.tensor_tensor(m.x[:, :, :], m.x[:, :, :], m.acc[:, :, 0:H], ALU.add))
            layer_norm(nc, dve, link, m, m.x[:, :, :], m.h[:, :, :], scratch, var_ready, std_ready, 1)
            nc.vector.tensor_tensor(m.h[:, :, :], m.h[:, :, :], m.rdeg[:, :].unsqueeze(2).to_broadcast([P, NT, H]),
                                    ALU.mult).then_inc(h_ready, 1)


def finish(nc, ctx, m, out):
    sem = lambda n: ctx.enter_context(nc.semaphore(n))
    dchain, x_ready, stored = sem("f_chain"), sem("f_ready"), sem("stored")

    with nc.Block() as block:

        @block.vector
        def _(dve):
            link = Chain(dve, dchain)
            link(nc.vector.tensor_tensor(m.acc[:, :, 0:H], m.acc[:, :, 0:H],
                                         m.rdeg[:, :].unsqueeze(2).to_broadcast([P, NT, H]), ALU.mult))
            nc.vector.tensor_tensor(m.x[:, :, :], m.x[:, :, :], m.acc[:, :, 0:H], ALU.add).then_inc(x_ready, 1)

        @block.sync
        def _(sp):
            sp.wait_ge(x_ready, 1)
            sp.dma_start(out.rearrange("(j p) f -> p j f", p=P), m.x[:, :, :]).then_inc(stored, 16)
            sp.wait_ge(stored, 16)


def gnn(nc, ins, out):
    dram = Memory()
    dram.emb = nc.dram_tensor("emb_both", [NTYPE, 2 * G], fp32).ap()
    dram.sorted = nc.dram_tensor("sorted_edges", [EP, SORTED], fp32).ap()
    dram.dst = nc.dram_tensor("sorted_dst", [EP], i32).ap()
    dram.rec = nc.dram_tensor("records", [EP, REC], fp32).ap()
    dram.tab1 = nc.dram_tensor("table1", [NP * NREL1, H], fp32).ap()
    dram.tab2 = nc.dram_tensor("table2", [NP * NREL2, H], fp32).ap()
    dram.tab3 = nc.dram_tensor("table3", [NP, H], fp32).ap()
    with ExitStack() as whole:
        m = allocate(nc, whole)
        with ExitStack() as ctx:
            load(nc, ctx, m, ins, dram)
        with ExitStack() as ctx:
            reorder(nc, ctx, m, ins, dram)
        with ExitStack() as ctx:
            setup(nc, ctx, m, ins, dram)
        with ExitStack() as ctx:
            layer0_edges(nc, ctx, m, ins, dram)
        with ExitStack() as ctx:
            layer0_sums(nc, ctx, m, dram)
        with ExitStack() as ctx:
            node_layer1(nc, ctx, m, ins, dram)
        with ExitStack() as ctx:
            s_src, s_row1, s_w = m.in_src_order()
            gather_sums(nc, ctx, m, "l1_", dram.tab1, s_row1, s_w, s_src, m.sfirst, m.slast)
        with ExitStack() as ctx:
            node_layer2(nc, ctx, m, ins, dram)
        with ExitStack() as ctx:
            gather_sums(nc, ctx, m, "l2_", dram.tab2, m.row2, m.w1, m.dstf, m.dfirst, m.dlast)
        with ExitStack() as ctx:
            node_layer3(nc, ctx, m, ins, dram)
        with ExitStack() as ctx:
            gather_sums(nc, ctx, m, "l3_", dram.tab3, m.srcf, m.w, m.dstf, m.dfirst, m.dlast)
        with ExitStack() as ctx:
            finish(nc, ctx, m, out)


def kernel(x, src, dst, edge_attr_40, edge_type_4, edge_type_8, edge_weight, edge_weight1, node_type_119, node_vec,
           L0_gnn_W1, L0_gnn_b1, L0_gnn_W2, L0_gnn_b2, L0_gnn_emb, L0_gnn_adaptW, L0_gnn_gamma, L0_gnn_beta,
           L1_gnn_W, L1_gnn_b, L2_gnn_weight1, L2_gnn_weight2, L2_gnn_bias1, L2_gnn_bias2):
    import numpy as _np
    import concourse.bacc as _bacc
    from concourse import mybir as _mybir
    from concourse.bass_utils import run_bass_kernel_spmd as _run

    def padded(a, n, fill=0):
        a = _np.asarray(a)
        out = _np.full((n,) + a.shape[1:], fill, a.dtype)
        out[:a.shape[0]] = a
        return out

    def by_chunk(a):
        return a.reshape(NC, P, T).transpose(1, 0, 2).reshape(P, NE)

    def by_tile(a):
        return a.reshape(NT, P).T

    dst_natural = padded(dst, EP + 1, N)
    attr = padded(edge_attr_40, EP)
    laid = {
        "x": padded(x, NP), "src": by_chunk(padded(src, EP, N)), "dst": dst_natural[:EP],
        "dst_laid": by_chunk(dst_natural[:EP]), "dst_after": by_chunk(dst_natural[1:]),
        "attr": attr, "attrT": attr.reshape(NC, P, T, R).transpose(3, 0, 2, 1).reshape(R, EP),
        "type4": by_chunk(padded(edge_type_4, EP)), "type8": by_chunk(padded(edge_type_8, EP)),
        "w": by_chunk(padded(edge_weight, EP)), "w1": by_chunk(padded(_np.asarray(edge_weight1).reshape(-1), EP)),
        "ztype": by_tile(padded(node_type_119, NP)), "mult": by_tile(padded(node_vec, NP)),
        "W1T": _np.asarray(L0_gnn_W1).T, "b1": _np.asarray(L0_gnn_b1).reshape(H, 1),
        "W2T": _np.concatenate([_np.asarray(L0_gnn_W2).T, _np.asarray(L0_gnn_b2).reshape(1, H)]),
        "emb": L0_gnn_emb, "embT": _np.asarray(L0_gnn_emb).T, "adaptT": _np.asarray(L0_gnn_adaptW).T,
        "gamma": _np.asarray(L0_gnn_gamma).reshape(1, H), "beta": _np.asarray(L0_gnn_beta).reshape(1, H),
        "W": L1_gnn_W, "b": _np.asarray(L1_gnn_b).reshape(1, H),
        "weight1": L2_gnn_weight1, "weight2": L2_gnn_weight2,
        "bias1": _np.asarray(L2_gnn_bias1).reshape(H, 1), "bias2": _np.asarray(L2_gnn_bias2).reshape(1, H),
    }
    nc = _bacc.Bacc("TRN2", target_bir_lowering=False, num_devices=1)
    arrays, ins = {}, Memory()
    for name, a in laid.items():
        a = _np.ascontiguousarray(a)
        arrays[f"in_{name}"] = a
        ins.__dict__[name] = nc.dram_tensor(f"in_{name}", a.shape, _mybir.dt.from_np(a.dtype), kind="ExternalInput").ap()
    out = nc.dram_tensor("out_x", (NP, H), fp32, kind="ExternalOutput").ap()
    gnn(nc, ins, out)
    r = _run(nc, [arrays], core_ids=[0])
    return r.results[0]["out_x"][:N]
```

```python
import concourse.bass as bass
from concourse import mybir
from contextlib import ExitStack
import numpy as np

fp32 = mybir.dt.float32
bf16 = mybir.dt.bfloat16
i32 = mybir.dt.int32
ALU = mybir.AluOpType
ACT = mybir.ActivationFunctionType
AX = mybir.AxisListType

P = 128
N = 6250
H = 48
E = 206250
R = 40
G = 32
NTYPE = 119
NREL1, NREL2 = 4, 8
NT = -(-N // P)
NP = NT * P
T = 16
CH = T * P
NC = -(-E // CH)
EP = NC * CH
NE = NC * T
ITEMS = NC + NT - 1
REC = 2 * H + G + 4
SRC, ROW1, WEIGHT = 2 * H + G + 1, 2 * H + G + 2, 2 * H + G + 3
TW = H + G + 1
CUTOFF = 6.0
EPS = 1e-5
HALFPI = float(np.pi / 2)


class Memory:

    def in_src_order(self):
        return self.cut[:, :], self.place[:, :], self.row1[:, :].bitcast(fp32)


def allocate(nc, ctx):
    m = Memory()

    def sb(name, shape, dt=fp32):
        return ctx.enter_context(nc.sbuf_tensor(name, shape, dt))

    m.srcf = sb("srcf", [P, NE])
    m.dstf = sb("dstf", [P, NE])
    m.w = sb("w", [P, NE])
    m.w1 = sb("w1", [P, NE])
    m.cut = sb("cut", [P, NE])
    m.row1 = sb("row1", [P, NE], i32)
    m.row2 = sb("row2", [P, NE], i32)
    m.place = sb("place", [P, NE], i32)
    m.x = sb("x_res", [P, NT, H])
    m.h = sb("h_norm", [P, NT, H])
    m.acc = sb("acc", [P, NT, H + 2])
    m.emb = sb("emb_rows", [P, NT, 2 * G])
    m.mult = sb("mult", [P, NT])
    m.rdeg = sb("rdeg", [P, NT])
    m.iota = sb("iota", [P, P])
    m.node = sb("node", [P, NT])
    m.base = sb("base", [P, NT])
    m.ident = sb("ident", [P, P])
    m.lower = sb("lower", [P, P])
    m.ones = sb("ones", [P, P])
    m.sfirst = sb("sfirst", [1, NC], i32)
    m.slast = sb("slast", [1, NC], i32)
    m.dfirst = sb("dfirst", [1, NC], i32)
    m.dlast = sb("dlast", [1, NC], i32)
    m.stat = sb("stat", [P, 4, NT])
    m.zero = sb("zero_bf", [P, 512], bf16)
    m.iota_bf = sb("iota_bf", [P, P], bf16)
    m.ident_bf = sb("ident_bf", [P, P], bf16)
    m.work = sb("work", [P, WORK + T0])
    m.t0 = m.work[:, WORK:].bitcast(bf16).rearrange("p (j a f) -> p j a f", a=3, f=TW + 1)
    m.emb3 = m.emb[:, :, 0:3 * G // 2].bitcast(bf16)
    m.ichunk = sb("ichunk", [1, ITEMS], i32)
    m.itile = sb("itile", [1, ITEMS], i32)
    m.ibase = sb("item_base", [P, ITEMS])
    m.unsorted = sb("unsorted", [1, 1], i32)
    return m


WORK = 15700
T0 = NT * 3 * (TW + 1) // 2
SORTED = R + 6


def carve(m, *shapes, all_of_it=False):
    at, out = 0, []
    for shape in shapes:
        n = int(np.prod(shape))
        v = m.work[:, at:at + n]
        if len(shape) == 2:
            v = v.rearrange("p (a b) -> p a b", b=shape[1])
        out.append(v)
        at += n
    assert at <= (WORK + T0 if all_of_it else WORK), at
    return out


def over_steps(eng, total, ring, step):
    for n in range(ring):
        step(n, 0, n)
    rounds = total // ring
    with eng.Fori(1, rounds) as v:
        u = eng.snap(v, min_val=1, max_val=rounds - 1)
        for s in range(ring):
            step(u * ring + s, u, s)
    for n in range(rounds * ring, total):
        step(n, rounds, n % ring)


def over_chunks(eng, chunk, ring=2):
    over_steps(eng, NC, ring, chunk)


def before(n, least):
    return isinstance(n, int) and n < least


def col(n):
    return bass.ds(n, 1) if not isinstance(n, int) else slice(n, n + 1)


def over_items(eng, k, first, last, c, item):
    at = bass.ds(c, 1) if not isinstance(c, int) else slice(c, c + 1)
    lo = eng.value_load(first[0:1, at], min_val=0, max_val=NT - 1)
    hi = eng.value_load(last[0:1, at], min_val=0, max_val=NT - 1)
    with eng.Fori(lo, hi + 1) as v:
        item(eng.snap(k, min_val=0, max_val=NC + NT), eng.snap(v, min_val=0, max_val=NT - 1))
        eng.reg_add(k, k, 1)


def cols(c, n=T):
    return bass.ds(c * n, n) if not isinstance(c, int) else slice(c * n, (c + 1) * n)


class Chain:

    def __init__(self, eng, sem):
        self.eng, self.sem, self.n = eng, sem, 0

    def __call__(self, step):
        self.n += 1
        step.then_inc(self.sem, 1)
        self.eng.wait_ge(self.sem, self.n)


def layer_norm(nc, dve, link, m, src, out, scratch, var_ready, std_ready, nth, gamma=None, beta=None):
    mean, var = m.stat[:, 0, :], m.stat[:, 1, :]
    wide = lambda a: a.unsqueeze(2).to_broadcast([P, NT, H])
    link(nc.vector.reduce_sum(mean, src, AX.X))
    link(nc.vector.tensor_scalar(mean, mean, -1.0 / H, None, ALU.mult))
    link(nc.vector.tensor_tensor(out, src, wide(mean), ALU.add))
    link(nc.vector.tensor_tensor(scratch, out, out, ALU.mult))
    link(nc.vector.reduce_sum(var, scratch, AX.X))
    nc.vector.tensor_scalar(var, var, 1.0 / H, EPS, ALU.mult, ALU.add).then_inc(var_ready, 1)
    dve.wait_ge(std_ready, nth)
    link(nc.vector.reciprocal(var, m.stat[:, 2, :]))
    link(nc.vector.tensor_tensor(out, out, wide(var), ALU.mult))
    if gamma is None:
        link(nc.vector.tensor_scalar(out, out, 0.0, None, ALU.max))
    else:
        feat = lambda a: a.unsqueeze(1).to_broadcast([P, NT, H])
        link(nc.vector.tensor_tensor(out, out, feat(gamma), ALU.mult))
        link(nc.vector.tensor_tensor(out, out, feat(beta), ALU.add))


def split(nc, link, hi, mid, lo, x, rest):
    link(nc.vector.tensor_copy(hi, x))
    link(nc.vector.tensor_tensor(rest, x, hi, ALU.subtract))
    link(nc.vector.tensor_copy(mid, rest))
    link(nc.vector.tensor_tensor(lo, rest, mid, ALU.subtract))


def square_root(nc, act, m, var_ready, std_ready, nth):
    act.wait_ge(var_ready, nth)
    nc.scalar.activation(m.stat[:, 2, :], m.stat[:, 1, :], ACT.Sqrt).then_inc(std_ready, 1)


def sort_buffers(nc, ctx, m, name):
    b = Memory()
    sb = lambda n, s, d=fp32: ctx.enter_context(nc.sbuf_tensor(name + n, s, d))
    _, bucket, mask, b.scan, one, b.place, prod0, prod1 = carve(
        m, [NE], [NE // 2], [NE // 2], [NE], [NE // 2], [NE], [NE], [NE])
    b.bucket, b.mask, b.one = bucket.bitcast(bf16), mask.bitcast(bf16), one.bitcast(bf16)
    b.prod = (prod0, prod1)
    b.count = sb("count", [P, NT])
    b.offset = sb("offset", [P, NT])
    b.end = sb("end", [P, NT])
    b.before_ps = ctx.enter_context(nc.psum_tensor(name + "before_ps", [P, NT], fp32))
    b.total_ps = ctx.enter_context(nc.psum_tensor(name + "total_ps", [P, NT], fp32))
    sem = lambda n: ctx.enter_context(nc.semaphore(name + n))
    b.counted, b.summed, b.prod_ready, b.added = sem("counted"), sem("summed"), sem("prod_ready"), sem("added")
    return b


def sort_places(nc, dve, link, b, raw, bucket_raw, out):
    link(nc.vector.memset(b.one, 1.0))
    link(nc.vector.tensor_scalar(bucket_raw, raw, 7, None, ALU.arith_shift_right))
    link(nc.vector.tensor_copy(b.bucket, bucket_raw))
    for t in range(NT):
        link(nc.vector.tensor_scalar(b.mask, b.bucket, float(t), 0.0, ALU.is_equal, ALU.add,
                                     accum_out=b.count[:, t:t + 1]))
    nc.vector.engine_nop().then_inc(b.counted, 1)
    dve.wait_ge(b.summed, 1)
    link(nc.vector.tensor_copy(b.offset[:, :], b.before_ps[:, :]))
    link(nc.vector.tensor_tensor_scan(b.end[:, :], b.one[:, 0:NT], b.total_ps[:, :], 0.0, ALU.mult, ALU.add))
    link(nc.vector.tensor_tensor(b.offset[:, 1:NT], b.offset[:, 1:NT], b.end[:, 0:NT - 1], ALU.add))
    for t in range(NT):
        link(nc.vector.tensor_scalar(b.mask, b.bucket, float(t), None, ALU.is_equal))
        link(nc.vector.tensor_tensor_scan(b.scan, b.one, b.mask, b.offset[:, t:t + 1], ALU.mult, ALU.add))
        if t >= 2:
            dve.wait_ge(b.added, t)
        nc.vector.tensor_tensor(b.prod[t % 2], b.scan, b.mask, ALU.mult).then_inc(b.prod_ready, 1)
        dve.wait_ge(b.prod_ready, t + 1)
    dve.wait_ge(b.added, NT + 1)
    link(nc.vector.tensor_copy(out, b.place))


def sort_adds(nc, pool, b):
    nc.gpsimd.memset(b.place, -1.0).then_inc(b.added, 1)
    for t in range(NT):
        pool.wait_ge(b.prod_ready, t + 1)
        pool.wait_ge(b.added, t + 1)
        nc.gpsimd.tensor_tensor(b.place, b.place, b.prod[t % 2], ALU.add).then_inc(b.added, 1)


def sort_sums(nc, pe, m, b):
    pe.wait_ge(b.counted, 1)
    nc.tensor.matmul(b.before_ps[:, :], m.lower[:, :], b.count[:, :], start=True, stop=True)
    nc.tensor.matmul(b.total_ps[:, :], m.ones[:, :], b.count[:, :], start=True, stop=True).then_inc(b.summed, 1)


def raw_views(m):
    return m.place[:, :], m.work[:, 0:NE].bitcast(i32)


def load(nc, ctx, m, ins, dram):
    raw_src, raw_dst = raw_views(m)
    _, after, tile_a, tile_b, diff = carve(m, [NE], [NE], [NE], [NE], [NE])
    after = after.bitcast(i32)
    worst, row = m.stat[:, 0, 0:1], m.work[0:1, 5 * NE:5 * NE + P]
    sb = lambda n, s, d=fp32: ctx.enter_context(nc.sbuf_tensor(n, s, d))
    icol, inode, ibase = sb("icol", [P, P], i32), sb("inode", [P, NT], i32), sb("ibase", [P, NT], i32)
    worst_ps = ctx.enter_context(nc.psum_tensor("worst_ps", [1, P], fp32))
    sem = lambda n: ctx.enter_context(nc.semaphore(n))
    dst_in, rest_in, iotas, dchain, worst_ready, worst_row = (
        sem("dst_in"), sem("rest_in"), sem("iotas"), sem("load_chain"), sem("worst_ready"), sem("worst_row"))

    with nc.Block() as block:

        @block.sync
        def _(sp):
            sp.dma_start(raw_dst, ins.dst_laid).then_inc(dst_in, 16)
            sp.dma_start(after, ins.dst_after).then_inc(dst_in, 16)
            for to, what in ((raw_src, ins.src), (m.w[:, :], ins.w), (m.w1[:, :], ins.w1),
                             (m.row1[:, :], ins.type4), (m.row2[:, :], ins.type8)):
                sp.dma_start(to, what).then_inc(rest_in, 16)
            sp.wait_ge(rest_in, 80)

        @block.gpsimd
        def _(pool):
            nc.gpsimd.iota(icol[:, :], [[1, P]], 0, 0)
            nc.gpsimd.iota(inode[:, :], [[P, NT]], 0, 1)
            nc.gpsimd.iota(ibase[:, :], [[P, NT]], 0, 0).then_inc(iotas, 1)

        @block.vector
        def _(dve):
            link = Chain(dve, dchain)
            dve.wait_ge(iotas, 1)
            nc.vector.tensor_copy(m.iota[:, :], icol[:, :])
            nc.vector.tensor_copy(m.iota_bf[:, :], icol[:, :])
            nc.vector.tensor_copy(m.base[:, :], ibase[:, :])
            nc.vector.memset(m.zero[:, :], 0.0)
            nc.vector.memset(m.ones[:, :], 1.0)
            link(nc.vector.tensor_copy(m.node[:, :], inode[:, :]))
            number = m.node[:, 0:1]
            nc.vector.tensor_scalar(m.lower[:, :], m.iota[:, :], number, None, ALU.is_gt)
            nc.vector.tensor_scalar(m.ident_bf[:, :], m.iota_bf[:, :], number, None, ALU.is_equal)
            link(nc.vector.tensor_scalar(m.ident[:, :], m.iota[:, :], number, None, ALU.is_equal))
            dve.wait_ge(dst_in, 32)
            link(nc.vector.tensor_scalar(tile_a.bitcast(i32), raw_dst, 7, None, ALU.arith_shift_right))
            link(nc.vector.tensor_scalar(tile_b.bitcast(i32), after, 7, None, ALU.arith_shift_right))
            link(nc.vector.tensor_tensor(diff, tile_a.bitcast(i32), tile_b.bitcast(i32), ALU.subtract))
            nc.vector.tensor_reduce(worst, diff, AX.X, ALU.max).then_inc(worst_ready, 1)
            dve.wait_ge(worst_row, 1)
            link(nc.vector.tensor_reduce(row[0:1, 0:1], worst_ps[0:1, :], AX.X, ALU.max))
            link(nc.vector.tensor_scalar(m.unsorted[:, :], row[0:1, 0:1], 0.0, None, ALU.is_gt))

        @block.tensor
        def _(pe):
            pe.wait_ge(worst_ready, 1)
            nc.tensor.matmul(worst_ps[0:1, :], worst, m.ident[:, :], start=True, stop=True).then_inc(worst_row, 1)


def reorder(nc, ctx, m, ins, dram):
    raw_src, raw_dst = raw_views(m)
    edge = m.work[:, 8 * NE:8 * NE + T * SORTED].rearrange("p (t f) -> p t f", f=SORTED)
    fields = (raw_src, raw_dst, m.w[:, :], m.w1[:, :], m.row1[:, :], m.row2[:, :])
    spot_all = m.acc[:, :, :].rearrange("p j f -> p (j f)")[:, 0:NE].bitcast(i32)
    spot = ctx.enter_context(nc.sbuf_tensor("spot", [P, T], i32))
    b = sort_buffers(nc, ctx, m, "r_")
    sem = lambda n: ctx.enter_context(nc.semaphore(n))
    dchain, attr_in, filled, scattered, fields_in, dst_out, placed = (
        sem("r_chain"), sem("r_attr"), sem("r_filled"), sem("r_scattered"), sem("r_fields"), sem("r_dst"), sem("r_placed"))
    buffer_free, pool_turns, sp_turns = sem("r_free"), sem("r_pool_turns"), sem("r_sp_turns")

    def flag(eng):
        return eng.value_load(m.unsorted[0:1, 0:1], min_val=0, max_val=1)

    with nc.Block() as block:

        @block.sync
        def _(sp):
            with sp.If(flag(sp)), nc.allow_non_contiguous_dma(reason="the general path"):
                sp.wait_ge(placed, 1)
                with sp.Fori(0, NC) as v:
                    c = sp.snap(v, min_val=0, max_val=NC - 1)
                    sp.wait_ge(buffer_free, c + 1)
                    sp.sem_inc(sp_turns, 1)
                    sp.dma_start(edge[:, :, 0:R], ins.attr.rearrange("(c p t) r -> p c t r", p=P, t=T)[:, col(c), :, :]
                                 .rearrange("p c t r -> p (c t) r")).then_inc(attr_in, 16)
                sp.wait_ge(buffer_free, NC + 1)
                with sp.Fori(0, NC) as v:
                    c = sp.snap(v, min_val=0, max_val=NC - 1)
                    for f, to in enumerate(fields):
                        to = to if f in (2, 3) else to.bitcast(fp32)
                        sp.dma_start(to[:, cols(c)],
                                     dram.sorted.rearrange("(c p t) f -> p c t f", p=P, t=T)[:, col(c), :, R + f]
                                     .rearrange("p c t -> p (c t)")).then_inc(fields_in, 16)
                sp.wait_ge(fields_in, 16 * NC * len(fields))
                for t in range(T):
                    sp.dma_start(dram.dst.rearrange("(c t p) -> p c t", p=P, t=T)[:, :, t],
                                 raw_dst.rearrange("p (c t) -> p c t", t=T)[:, :, t]).then_inc(dst_out, 16)
                sp.wait_ge(dst_out, 16 * T)

        @block.tensor
        def _(pe):
            with pe.If(flag(pe)):
                sort_sums(nc, pe, m, b)

        @block.vector
        def _(dve):
            with dve.If(flag(dve)):
                link = Chain(dve, dchain)
                sort_places(nc, dve, link, b, raw_dst, spot_all, spot_all)
                nc.vector.engine_nop().then_inc(placed, 1)
                with dve.Fori(0, NC) as v:
                    c = dve.snap(v, min_val=0, max_val=NC - 1)
                    dve.wait_ge(attr_in, c * 16 + 16)
                    for f, have in enumerate(fields):
                        to = edge[:, :, R + f]
                        nc.vector.tensor_copy(to if f in (2, 3) else to.bitcast(i32), have[:, cols(c)])
                    nc.vector.tensor_copy(spot[:, :], spot_all[:, cols(c)]).then_inc(filled, 1)

        @block.gpsimd
        def _(pool):
            with pool.If(flag(pool)):
                sort_adds(nc, pool, b)
                pool.sem_inc(buffer_free, 1)
                with pool.Fori(0, NC) as v:
                    c = pool.snap(v, min_val=0, max_val=NC - 1)
                    pool.wait_ge(filled, c + 1)
                    pool.sem_inc(pool_turns, 1)
                    for t in range(T):
                        nc.gpsimd.indirect_dma_start(
                            out=dram.sorted, out_offset=bass.IndirectOffsetOnAxis(ap=spot[:, t:t + 1], axis=0),
                            in_=edge[:, t, :], in_offset=None).then_inc(scattered, 16)
                    pool.wait_ge(scattered, c * (16 * T) + 16 * T)
                    pool.sem_inc(buffer_free, 1)


def setup(nc, ctx, m, ins, dram):
    raw_src, raw_dst = raw_views(m)
    bucket_raw = m.cut[:, :].bitcast(i32)
    b = sort_buffers(nc, ctx, m, "s_")
    angles, inside = b.prod
    sb = lambda n, s, d=fp32: ctx.enter_context(nc.sbuf_tensor(n, s, d))
    edge0, tiles = sb("edge0", [1, NC]), sb("tiles", [1, NC])
    iitem, item, item_chunk = sb("iitem", [1, ITEMS], i32), sb("item", [1, ITEMS]), sb("item_chunk", [1, ITEMS])
    iedge = sb("iedge", [1, NC], i32)
    draw = sb("draw", [1, 2, NC], i32)
    ztype = sb("ztype", [P, NT], i32)
    embT, adaptT, both = sb("embT", [G, NTYPE]), sb("adaptT", [G, G]), sb("both", [NTYPE, 2 * G])
    ps_emb = ctx.enter_context(nc.psum_tensor("ps_emb", [P, G], fp32))
    ps_base = ctx.enter_context(nc.psum_tensor("ps_base", [P, ITEMS], fp32))
    sem = lambda n: ctx.enter_context(nc.semaphore(n))
    x_in, emb_in, iotas, emb_mm, both_ready, both_out, emb_rows_in, ends_in = (
        sem("x_in"), sem("emb_in"), sem("s_iotas"), sem("emb_mm"), sem("both_ready"), sem("both_out"),
        sem("emb_rows_in"), sem("ends_in"))
    var_ready, std_ready, dchain, cut_ready, angle, item_ready, base_ready = (
        sem("var0"), sem("std0"), sem("setup_chain"), sem("cut_ready"), sem("angle"), sem("item_ready"), sem("base_ready"))
    wide48 = lambda a: a.unsqueeze(2).to_broadcast([P, NT, H])

    with nc.Block() as block:

        @block.sync
        def _(sp):
            with nc.allow_non_contiguous_dma(reason="small arrays, once"):
                sp.dma_start(embT[:, :], ins.embT).then_inc(emb_in, 16)
                sp.dma_start(adaptT[:, :], ins.adaptT).then_inc(emb_in, 16)
                sp.dma_start(both[:, 0:G], ins.emb).then_inc(emb_in, 16)
                sp.dma_start(ztype[:, :], ins.ztype).then_inc(emb_in, 16)
                sp.dma_start(m.x[:, :, :], ins.x.rearrange("(j p) f -> p j f", p=P)).then_inc(x_in, 16)
                sp.dma_start(m.mult[:, :], ins.mult).then_inc(x_in, 16)
                sp.dma_start(draw[0:1, 0, :], raw_dst.rearrange("p (c t) -> p c t", t=T)[0:1, :, 0]).then_inc(ends_in, 16)
                sp.dma_start(draw[0:1, 1, :], raw_dst.rearrange("p (c t) -> p c t", t=T)[P - 1:P, :, T - 1]).then_inc(ends_in, 16)
            sp.wait_ge(both_ready, 1)
            sp.dma_start(dram.emb, both[:, :]).then_inc(both_out, 16)

        @block.gpsimd
        def _(pool):
            nc.gpsimd.iota(iedge[:, :], [[CH, NC]], 0, 0)
            nc.gpsimd.iota(iitem[:, :], [[1, ITEMS]], 0, 0).then_inc(iotas, 1)
            sort_adds(nc, pool, b)
            pool.wait_ge(emb_in, 64)
            pool.wait_ge(both_out, 16)
            for j in range(NT):
                nc.gpsimd.indirect_dma_start(
                    out=m.emb[:, j, :], out_offset=None, in_=dram.emb,
                    in_offset=bass.IndirectOffsetOnAxis(ap=ztype[:, j:j + 1], axis=0)).then_inc(emb_rows_in, 16)

        @block.tensor
        def _(pe):
            pe.wait_ge(emb_in, 64)
            nc.tensor.matmul(ps_emb[0:NTYPE, :], embT[:, :], adaptT[:, :], start=True, stop=True).then_inc(emb_mm, 1)
            sort_sums(nc, pe, m, b)
            pe.wait_ge(item_ready, 1)
            nc.tensor.matmul(ps_base[:, :], m.ones[0:1, :], item[:, :], start=True, stop=True).then_inc(base_ready, 1)

        @block.scalar
        def _(act):
            act.wait_ge(angle, 1)
            nc.scalar.activation(m.cut[:, :], m.cut[:, :], ACT.Sin).then_inc(cut_ready, 1)
            square_root(nc, act, m, var_ready, std_ready, 1)

        @block.vector
        def _(dve):
            link = Chain(dve, dchain)
            dve.wait_ge(emb_mm, 1)
            nc.vector.tensor_copy(both[:, G:2 * G], ps_emb[0:NTYPE, :]).then_inc(both_ready, 1)
            nc.vector.tensor_copy(m.srcf[:, :], raw_src)
            link(nc.vector.tensor_copy(m.dstf[:, :], raw_dst))
            link(nc.vector.scalar_tensor_tensor(m.row1[:, :], m.dstf[:, :], float(NREL1), m.row1[:, :], ALU.mult, ALU.add))
            link(nc.vector.scalar_tensor_tensor(m.row2[:, :], m.srcf[:, :], float(NREL2), m.row2[:, :], ALU.mult, ALU.add))
            dve.wait_ge(ends_in, 32)
            nc.vector.tensor_scalar(m.dfirst[:, :], draw[0:1, 0, :], 7, None, ALU.arith_shift_right)
            link(nc.vector.tensor_scalar(m.dlast[:, :], draw[0:1, 1, :], 7, None, ALU.arith_shift_right))

            sort_places(nc, dve, link, b, raw_src, bucket_raw, m.place[:, :])

            link(nc.vector.scalar_tensor_tensor(angles, m.w[:, :], -1.0, m.w[:, :], ALU.mult, ALU.max))
            link(nc.vector.tensor_scalar(angles, angles, CUTOFF, None, ALU.min))
            nc.vector.tensor_scalar(m.cut[:, :], angles, -float(np.pi) / CUTOFF, HALFPI,
                                    ALU.mult, ALU.add).then_inc(angle, 1)
            link(nc.vector.tensor_scalar(inside, m.w[:, :], CUTOFF, 0.5, ALU.is_lt, ALU.mult))
            dve.wait_ge(cut_ready, 1)
            link(nc.vector.scalar_tensor_tensor(m.cut[:, :], m.cut[:, :], 1.0, inside, ALU.add, ALU.mult))

            dve.wait_ge(iotas, 1)
            nc.vector.tensor_copy(item[:, :], iitem[:, :])
            link(nc.vector.tensor_copy(edge0[:, :], iedge[:, :]))
            grid = m.work[0:1, 0:NC * NT].rearrange("p (c b) -> p c b", b=NT)
            tile_end = b.end[0:1, :].unsqueeze(1).to_broadcast([1, NC, NT])
            for out in (m.sfirst, m.slast):
                if out is m.slast:
                    link(nc.vector.tensor_scalar(edge0[:, :], edge0[:, :], float(CH - 1), None, ALU.add))
                link(nc.vector.tensor_tensor(grid, tile_end, edge0[0:1, :].unsqueeze(2).to_broadcast([1, NC, NT]),
                                             ALU.is_le))
                link(nc.vector.reduce_sum(tiles[:, :], grid, AX.X))
                link(nc.vector.tensor_copy(out[:, :], tiles[:, :]))
            link(nc.vector.tensor_tensor(tiles[:, :], tiles[:, :], item[:, 0:NC], ALU.add))
            grid = m.work[0:1, 0:(ITEMS * NC + 1) // 2 * 1].bitcast(bf16)[:, 0:ITEMS * NC].rearrange("p (k c) -> p k c", c=NC)
            link(nc.vector.tensor_tensor(grid, tiles[0:1, :].unsqueeze(1).to_broadcast([1, ITEMS, NC]),
                                         item[0:1, :].unsqueeze(2).to_broadcast([1, ITEMS, NC]), ALU.is_lt))
            link(nc.vector.reduce_sum(item_chunk[:, :], grid, AX.X))
            link(nc.vector.tensor_copy(m.ichunk[:, :], item_chunk[:, :]))
            link(nc.vector.tensor_tensor(item[:, :], item[:, :], item_chunk[:, :], ALU.subtract))
            nc.vector.tensor_copy(m.itile[:, :], item[:, :]).then_inc(item_ready, 1)
            dve.wait_ge(base_ready, 1)
            link(nc.vector.tensor_scalar(m.ibase[:, :], ps_base[:, :], float(P), None, ALU.mult))

            dve.wait_ge(x_in, 32)
            layer_norm(nc, dve, link, m, m.x[:, :, :], m.h[:, :, :],
                       m.work[:, 0:NT * H].rearrange("p (j f) -> p j f", f=H), var_ready, std_ready, 1)
            rows, rest = carve(m, [NT, TW], [NT, TW])
            link(nc.vector.tensor_tensor(rows[:, :, 0:H], m.h[:, :, :], wide48(m.mult[:, :]), ALU.mult))
            dve.wait_ge(emb_rows_in, 16 * NT)
            link(nc.vector.tensor_copy(rows[:, :, H:H + G], m.emb[:, :, G:2 * G]))
            link(nc.vector.tensor_copy(rows[:, :, H + G], m.mult[:, :]))
            split(nc, link, *(m.t0[:, :, a, 0:TW] for a in range(3)), rows, rest)
            parts = m.work[:, 0:NT * 3 * G // 2].bitcast(bf16).rearrange("p (j a f) -> p j a f", a=3, f=G)
            rest = rest[:, :, 0:G]
            split(nc, link, *(parts[:, :, a, :] for a in range(3)), m.emb[:, :, 0:G], rest)
            link(nc.vector.tensor_copy(m.emb3, parts.rearrange("p j a f -> p j (a f)")))


def layer0_edges(nc, ctx, m, ins, dram):
    attr, dr0, dr1, onehot, z, rec0, rec1 = carve(
        m, [4, 512], [CH], [CH], [CH // 2], [2, 512], [T, REC], [T, REC])
    onehot = onehot.bitcast(bf16)
    rec = (rec0, rec1)
    drow = (dr0.bitcast(i32), dr1.bitcast(i32))
    sb = lambda n, s, d=fp32: ctx.enter_context(nc.sbuf_tensor(n, s, d))
    place = (sb("place_a", [P, T], i32), sb("place_b", [P, T], i32))
    w1T, w2T, b1 = sb("w1T", [R, H]), sb("w2T", [H + 1, H]), sb("b1c", [H, 1])
    pb = lambda n, s: ctx.enter_context(nc.psum_tensor(n, s, fp32))
    rows_ps = pb("rows_ps", [P, T, P])
    gate_ps = pb("gate_ps", [P, T, 64])
    z_ps = pb("z_ps", [P, 2, 512])
    sem = lambda n: ctx.enter_context(nc.semaphore(n))
    weights_in = sem("weights_in")
    attr_in = [sem(f"attr_in{g}") for g in range(4)]
    drow_in = (sem("drow_in0"), sem("drow_in1"))
    tile_in = sem("tile_in")
    onehot_ready, onehot_free, chunk_items = sem("onehot_ready"), sem("onehot_free"), sem("chunk_items")
    rows_ready, rows_scaled, rows_copied = sem("rows_ready"), sem("rows_scaled"), sem("rows_copied")
    z_ready, silu_done, gate_ready, rec_ready, ones_set = (
        sem("z_ready"), sem("silu_done"), sem("gate_ready"), sem("rec_ready"), sem("ones_set"))
    scattered = (sem("scattered0"), sem("scattered1"))
    pool_turns, pe_turns, sp_turns = sem("pool_turns"), sem("pe_turns"), sem("sp_turns")

    with nc.Block() as block:

        @block.sync
        def _(sp):
            sp.dma_start(w1T[:, :], ins.W1T).then_inc(weights_in, 16)
            sp.dma_start(w2T[:, :], ins.W2T).then_inc(weights_in, 16)
            sp.dma_start(b1[:, :], ins.b1).then_inc(weights_in, 16)
            laid = ins.attrT.rearrange("r (c g e) -> r c g e", g=4, e=512)
            found = dram.sorted.rearrange("(c p t) f -> f c t p", p=P, t=T)[0:R]

            def loads(dst_row, attributes):
                def chunk(c, u, s):
                    if not before(c, 2):
                        sp.wait_ge(chunk_items, c - 1)
                        sp.sem_inc(sp_turns, 1)
                    sp.dma_start(drow[s], dst_row.rearrange("(c e) -> c e", e=CH)[col(c), :]
                                 .to_broadcast([P, CH])).then_inc(drow_in[s], 16)
                    for g in range(4):
                        if not before(c, 1):
                            sp.wait_ge(z_ready, c * 4 + (g - 3))
                            sp.sem_inc(sp_turns, 1)
                        attributes(c, g)
                over_chunks(sp, chunk)

            unsorted = sp.value_load(m.unsorted[0:1, 0:1], min_val=0, max_val=1)
            def whole_quarter(c, g):
                sp.dma_start(attr[0:R, g, :], laid[:, col(c), g, :].rearrange("r c e -> r (c e)")).then_inc(attr_in[g], 16)

            def tile_by_tile(c, g):
                for t in range(4):
                    sp.dma_start(attr[0:R, g, t * P:(t + 1) * P],
                                 found[:, col(c), 4 * g + t, :].rearrange("r c p -> r (c p)")).then_inc(tile_in, 16)
                sp.wait_ge(tile_in, c * 256 + (g + 1) * 64)
                sp.sem_inc(attr_in[g], 16)

            with sp.If(unsorted), nc.allow_non_contiguous_dma(reason="the general path"):
                loads(dram.dst, tile_by_tile)
            with sp.Else():
                loads(ins.dst, whole_quarter)

        @block.tensor
        def _(pe):
            pe.wait_ge(weights_in, 48)
            pe.wait_ge(ones_set, 1)
            pe.sem_inc(onehot_free, 2)
            with pe.register("k_edges") as k:
                pe.reg_mov(k, 0)

                def chunk(c, u, s):
                    def hidden(g):
                        pe.wait_ge(attr_in[g], c * 16 + 16)
                        pe.sem_inc(pe_turns, 1)
                        if not (before(c, 1) and g < 2):
                            pe.wait_ge(silu_done, c * 4 + (g - 1))
                            pe.sem_inc(pe_turns, 1)
                        nc.tensor.matmul(z_ps[0:H, g % 2, :], w1T[:, :], attr[0:R, g, :],
                                         start=True, stop=True).then_inc(z_ready, 1)

                    def gates(g):
                        pe.wait_ge(silu_done, c * 4 + (g + 1))
                        if g == 0 and not before(c, 1):
                            pe.wait_ge(rec_ready, c)
                        for t in range(4):
                            last = nc.tensor.matmul(gate_ps[:, 4 * g + t, 0:H], z[0:H + 1, g % 2, t * P:(t + 1) * P],
                                                    w2T[:, :], start=True, stop=True)
                        if g == 3:
                            last.then_inc(gate_ready, 1)

                    hidden(0)
                    for g in range(1, 4):
                        hidden(g)
                        gates(g - 1)
                    gates(3)

                    if not before(c, 1):
                        pe.wait_ge(rows_copied, c)
                    for b in range(4):
                        nc.tensor.matmul(rows_ps[:, 4 * b:4 * b + 4, :].rearrange("p t f -> p (t f)"),
                                         m.zero[:, 0:P], m.zero[:, :], start=True, stop=False)

                    def item(k, j):
                        for half in (0, 1):
                            pe.wait_ge(onehot_ready, k * 2 + (half + 1))
                            for t in range(half * T // 2, (half + 1) * T // 2):
                                for a in range(3):
                                    last = nc.tensor.matmul(
                                        rows_ps[:, t, 0:TW], onehot[:, t * P:(t + 1) * P],
                                        m.t0[:, col(j), a, 0:TW].rearrange("p j f -> p (j f)"), start=False, stop=False)
                            last.then_inc(onehot_free, 1)
                    over_items(pe, k, m.dfirst, m.dlast, c, item)
                    for b in range(4):
                        last = nc.tensor.matmul(rows_ps[:, 4 * b:4 * b + 4, :].rearrange("p t f -> p (t f)"),
                                                m.zero[:, 0:P], m.zero[:, :], start=False, stop=True)
                    last.then_inc(rows_ready, 1)
                over_chunks(pe, chunk)

        @block.scalar
        def _(act):
            act.wait_ge(ones_set, 1)
            act.wait_ge(weights_in, 48)

            def chunk(c, u, s):
                for g in range(4):
                    act.wait_ge(z_ready, c * 4 + (g + 1))
                    nc.scalar.activation(z[0:H, g % 2, :], z_ps[0:H, g % 2, :], ACT.Silu, bias=b1[:, 0:1]).then_inc(silu_done, 1)
                if not before(u, 1):
                    act.wait_ge(scattered[s], u * (16 * T))
                act.wait_ge(rows_scaled, c + 1)
                nc.scalar.copy(rec[s][:, :, 2 * H:2 * H + G + 1], rows_ps[:, :, H:TW]).then_inc(rows_copied, 1)
            over_chunks(act, chunk)

        @block.vector
        def _(dve):
            nc.vector.memset(z[0:64, :, :], 1.0).then_inc(ones_set, 1)
            with dve.register("k_edges") as k:
                dve.reg_mov(k, 0)

                def chunk(c, u, s):
                    dve.wait_ge(drow_in[s], u * 16 + 16)

                    def item(k, j):
                        for half in (0, 1):
                            part = slice(half * CH // 2, (half + 1) * CH // 2)
                            dve.wait_ge(onehot_free, k * 2 + (half + 1))
                            nc.vector.tensor_scalar(onehot[:, part], drow[s][:, part], m.node[:, col(j)], None,
                                                    ALU.is_equal).then_inc(onehot_ready, 1)
                    over_items(dve, k, m.dfirst, m.dlast, c, item)
                    if not before(u, 1):
                        dve.wait_ge(scattered[s], u * (16 * T))
                    nc.vector.tensor_copy(place[s][:, :], m.place[:, cols(c)]).then_inc(chunk_items, 1)
                    nc.vector.tensor_copy(rec[s][:, :, SRC], m.srcf[:, cols(c)])
                    nc.vector.tensor_copy(rec[s][:, :, ROW1], m.row1[:, cols(c)])
                    nc.vector.tensor_copy(rec[s][:, :, WEIGHT], m.w[:, cols(c)])
                    dve.wait_ge(rows_ready, c + 1)
                    nc.vector.tensor_tensor(rec[s][:, :, H:2 * H], rows_ps[:, :, 0:H],
                                            m.cut[:, cols(c)].unsqueeze(2).to_broadcast([P, T, H]),
                                            ALU.mult).then_inc(rows_scaled, 1)
                    dve.wait_ge(gate_ready, c + 1)
                    dve.wait_ge(rows_scaled, c + 1)
                    nc.vector.tensor_tensor(rec[s][:, :, 0:H], gate_ps[:, :, 0:H], rec[s][:, :, H:2 * H],
                                            ALU.mult).then_inc(rec_ready, 1)
                over_chunks(dve, chunk)

        @block.gpsimd
        def _(pool):
            def chunk(c, u, s):
                pool.wait_ge(rec_ready, c + 1)
                pool.wait_ge(rows_copied, c + 1)
                pool.sem_inc(pool_turns, 1)
                for t in range(T):
                    nc.gpsimd.indirect_dma_start(
                        out=dram.rec, out_offset=bass.IndirectOffsetOnAxis(ap=place[s][:, t:t + 1], axis=0),
                        in_=rec[s][:, t, :], in_offset=None).then_inc(scattered[s], 16)
            over_chunks(pool, chunk)
            pool.wait_ge(scattered[0], 16 * T * ((NC + 1) // 2))
            pool.wait_ge(scattered[1], 16 * T * (NC // 2))


def layer0_sums(nc, ctx, m, dram):
    PART = H + 2
    r0, r1, r2, r3, o0, o1, o2, o3, t0, t1, a0, a1, m0, m1, d0, d1, p0, p1 = carve(
        m, *[[T, REC]] * 4, *[[T * P // 2]] * 6, *[[T, H]] * 2, *[[T, H + 1]] * 4, *[[T * 3 * PART // 2]] * 2,
        all_of_it=True)
    tiles = lambda a: a.bitcast(bf16).rearrange("p (t n) -> p t n", n=P)
    rec, onehot, onehotT = (r0, r1, r2, r3), [tiles(a) for a in (o0, o1, o2, o3)], [tiles(a) for a in (t0, t1)]
    scaled, msg, rest = (a0, a1), (m0, m1), (d0, d1)
    parts = [a.bitcast(bf16).rearrange("p (t a f) -> p t a f", a=3, f=PART) for a in (p0, p1)]
    prod = [a.rearrange("p a b -> p (a b)")[:, 0:T * G].rearrange("p (a b) -> p a b", b=G) for a in scaled]
    s_src, s_row1, s_w = m.in_src_order()
    sb = lambda n, s, d=fp32: ctx.enter_context(nc.sbuf_tensor(n, s, d))
    local, adapt, total = sb("local", [P, 2, T]), sb("adapt", [P, 2, T]), sb("total", [P, PART])
    pb = lambda n, s, d=fp32: ctx.enter_context(nc.psum_tensor(n, s, d))
    tr_ps, emb_ps, sum_ps = pb("tr_ps", [P, 2, T, P], bf16), pb("emb_ps", [P, 2, T, G]), pb("sum_ps", [P, 2, 512])
    sem = lambda n: ctx.enter_context(nc.semaphore(n))
    rec_in = [sem(f"rec_in{i}") for i in range(4)]
    ones_set, local_ready, onehot_ready, tr_ready, tr_copied, kept, emb_ready = (
        sem("c_ones"), sem("c_local"), sem("c_onehot"), sem("c_tr"), sem("c_copied"), sem("c_kept"), sem("c_emb"))
    prod_ready, adapt_ready, scaled_ready, msg_ready, sum_ready, total_ready, acc_done = (
        sem("c_prod"), sem("c_adapt"), sem("c_scaled"), sem("c_msg"), sem("c_sum"), sem("c_total"), sem("c_acc"))
    hi_ready, rest_ready, mid_ready, lo_ready = sem("c_hi"), sem("c_rest"), sem("c_mid"), sem("c_lo")
    sp_turns = sem("c_sp_turns")
    RING = 4
    HALF = (slice(0, T // 2), slice(T // 2, T))

    with nc.Block() as block:

        @block.sync
        def _(sp):
            def item(k, u, s):
                c = sp.value_load(m.ichunk[0:1, col(k)], min_val=0, max_val=NC - 1)
                if not before(k, 4):
                    sp.wait_ge(msg_ready, k * 2 - 6)
                    sp.sem_inc(sp_turns, 1)
                    sp.wait_ge(kept, k * 3 - 9)
                    sp.sem_inc(sp_turns, 1)
                sp.dma_start(rec[s % RING].rearrange("p t f -> p (t f)"),
                             dram.rec.rearrange("(c p t) f -> p c (t f)", p=P, t=T)[:, col(c), :]
                             .rearrange("p c f -> p (c f)")).then_inc(rec_in[s % RING], 16)
            over_steps(sp, ITEMS, RING, item)

        def arrived(eng, k, u, s):
            eng.wait_ge(rec_in[s % RING], u * 16 + 16)

        @block.vector
        def _(dve):
            for a in parts:
                nc.vector.memset(a[:, :, 1:3, PART - 1], 0.0)
                nc.vector.memset(a[:, :, 0, PART - 1], 1.0)
            nc.vector.memset(m.acc[:, :, :], 0.0).then_inc(acc_done, 1)
            nc.vector.engine_nop().then_inc(ones_set, 1)

            def build(k, u, s):
                arrived(dve, k, u, s)
                nc.vector.tensor_scalar(local[:, s % 2, :], rec[s % RING][:, :, SRC], m.ibase[:, col(k)], None,
                                        ALU.subtract).then_inc(local_ready, 1)
                dve.wait_ge(local_ready, k + 1)
                if not before(k, 4):
                    dve.wait_ge(sum_ready, k - 3)
                for g in (0, 1):
                    nc.vector.tensor_tensor(onehot[s % RING][:, HALF[g], :],
                                            m.iota_bf[:, :].unsqueeze(1).to_broadcast([P, T // 2, P]),
                                            local[:, s % 2, HALF[g]].unsqueeze(2).to_broadcast([P, T // 2, P]),
                                            ALU.is_equal).then_inc(onehot_ready, 1)

            def adapted(k, s):
                r = rec[s % RING]
                dve.wait_ge(emb_ready, k + 1)
                if not before(k, 2):
                    dve.wait_ge(msg_ready, k * 2 - 2)
                nc.vector.tensor_tensor(prod[s % 2], emb_ps[:, s % 2, :, :], r[:, :, 2 * H:2 * H + G],
                                        ALU.mult).then_inc(prod_ready, 1)
                dve.wait_ge(prod_ready, k + 1)
                nc.vector.reduce_sum(adapt[:, s % 2, :], prod[s % 2], AX.X).then_inc(adapt_ready, 1)

            def low_part(k, s):
                dve.wait_ge(mid_ready, k + 1)
                nc.vector.tensor_tensor(parts[s % 2][:, :, 2, 0:H + 1], rest[s % 2], parts[s % 2][:, :, 1, 0:H + 1],
                                        ALU.subtract).then_inc(lo_ready, 1)

            def add_up(k, s, j):
                dve.wait_ge(sum_ready, k + 1)
                dve.wait_ge(acc_done, k + 1)
                nc.vector.reduce_sum(total[:, :], sum_ps[:, s % 2, 0:3 * PART].rearrange("p (a f) -> p f a", f=PART),
                                     AX.X).then_inc(total_ready, 1)
                dve.wait_ge(total_ready, k + 1)
                acc = m.acc[:, col(j), :].rearrange("p j f -> p (j f)")
                nc.vector.tensor_tensor(acc, acc, total[:, :], ALU.add).then_inc(acc_done, 1)

            def tile_of(k):
                return dve.value_load(m.itile[0:1, col(k)], min_val=0, max_val=NT - 1)

            def item(k, u, s):
                if not before(k, 3):
                    low_part(k - 3, s + 1)
                build(k, u, s)
                if not before(k, 3):
                    j = tile_of(k - 3)
                if not before(k, 1):
                    adapted(k - 1, s + 3)
                if not before(k, 3):
                    add_up(k - 3, s + 1, j)
            over_steps(dve, ITEMS, RING, item)
            end = ITEMS % RING
            adapted(ITEMS - 1, end + 3)
            for k in (3, 2, 1):
                low_part(ITEMS - k, end + 4 - k)
            for k in (3, 2, 1):
                add_up(ITEMS - k, end + 4 - k, tile_of(ITEMS - k))

        @block.gpsimd
        def _(pool):
            pool.wait_ge(ones_set, 1)

            def message(k, s):
                r = rec[s % RING]
                if not before(k, 2):
                    pool.wait_ge(rest_ready, k - 1)
                pool.wait_ge(adapt_ready, k + 1)
                nc.gpsimd.tensor_tensor(scaled[s % 2], r[:, :, H:2 * H],
                                        adapt[:, s % 2, :].unsqueeze(2).to_broadcast([P, T, H]),
                                        ALU.mult).then_inc(scaled_ready, 1)
                nc.gpsimd.tensor_copy(msg[s % 2][:, :, H], r[:, :, 2 * H + G]).then_inc(msg_ready, 1)
                pool.wait_ge(scaled_ready, k + 1)
                nc.gpsimd.tensor_tensor(msg[s % 2][:, :, 0:H], scaled[s % 2], r[:, :, 0:H],
                                        ALU.add).then_inc(msg_ready, 1)

            def rest_of(k, s):
                pool.wait_ge(hi_ready, k + 1)
                if not before(k, 2):
                    pool.wait_ge(lo_ready, k - 1)
                nc.gpsimd.tensor_tensor(rest[s % 2], msg[s % 2], parts[s % 2][:, :, 0, 0:H + 1],
                                        ALU.subtract).then_inc(rest_ready, 1)

            def item(k, u, s):
                if not before(k, 1):
                    rest_of(k - 1, s + 3)
                message(k, s)
            over_steps(pool, ITEMS, RING, item)
            rest_of(ITEMS - 1, ITEMS % RING + 3)

        @block.scalar
        def _(act):
            act.wait_ge(ones_set, 1)

            def high_part(k, s):
                act.wait_ge(msg_ready, k * 2 + 2)
                if not before(k, 2):
                    act.wait_ge(sum_ready, k - 1)
                nc.scalar.copy(parts[s % 2][:, :, 0, 0:H + 1], msg[s % 2]).then_inc(hi_ready, 1)

            def middle_part(k, s):
                act.wait_ge(rest_ready, k + 1)
                nc.scalar.copy(parts[s % 2][:, :, 1, 0:H + 1], rest[s % 2]).then_inc(mid_ready, 1)

            def item(k, u, s):
                c = act.value_load(m.ichunk[0:1, col(k)], min_val=0, max_val=NC - 1)
                arrived(act, k, u, s)
                if not before(k, 1):
                    act.wait_ge(kept, k * 3)
                for to, field in ((s_src, SRC), (s_row1, ROW1), (s_w, WEIGHT)):
                    nc.scalar.copy(to[:, cols(c)], rec[s % RING][:, :, field]).then_inc(kept, 1)
                for g in (0, 1):
                    act.wait_ge(tr_ready, k * 2 + (g + 1))
                    if g == 0 and not before(k, 2):
                        act.wait_ge(emb_ready, k - 1)
                    nc.scalar.copy(onehotT[s % 2][:, HALF[g], :], tr_ps[:, s % 2, HALF[g], :]).then_inc(tr_copied, 1)
                    if g == 0 and not before(k, 2):
                        middle_part(k - 2, s + 2)
                if not before(k, 1):
                    high_part(k - 1, s + 3)
            over_steps(act, ITEMS, RING, item)
            end = ITEMS % RING
            middle_part(ITEMS - 2, end + 2)
            high_part(ITEMS - 1, end + 3)
            middle_part(ITEMS - 1, end + 3)

        @block.tensor
        def _(pe):
            def sums(k, s):
                pe.wait_ge(lo_ready, k + 1)
                if not before(k, 2):
                    pe.wait_ge(acc_done, k)
                for t in range(T):
                    last = nc.tensor.matmul(sum_ps[:, s % 2, 0:3 * PART], onehot[s % RING][:, t, :],
                                            parts[s % 2][:, t, :, :].rearrange("p a f -> p (a f)"),
                                            start=(t == 0), stop=(t == T - 1))
                last.then_inc(sum_ready, 1)

            def item(k, u, s):
                if not before(k, 3):
                    sums(k - 3, s + 1)
                for g in (0, 1):
                    pe.wait_ge(onehot_ready, k * 2 + (g + 1))
                    if not before(k, 2):
                        pe.wait_ge(tr_copied, k * 2 + (g - 3))
                    for t in range(T)[HALF[g]]:
                        last = nc.tensor.transpose(tr_ps[:, s % 2, t, :], onehot[s % RING][:, t, :], m.ident_bf[:, :])
                    last.then_inc(tr_ready, 1)
                j = pe.value_load(m.itile[0:1, col(k)], min_val=0, max_val=NT - 1)
                if not before(k, 2):
                    pe.wait_ge(prod_ready, k - 1)
                for g in (0, 1):
                    pe.wait_ge(tr_copied, k * 2 + (g + 1))
                    for t in range(T)[HALF[g]]:
                        for a in range(3):
                            last = nc.tensor.matmul(emb_ps[:, s % 2, t, :], onehotT[s % 2][:, t, :],
                                                    m.emb3[:, col(j), a * G:(a + 1) * G].rearrange("p j f -> p (j f)"),
                                                    start=(a == 0), stop=(a == 2))
                last.then_inc(emb_ready, 1)
            over_steps(pe, ITEMS, RING, item)
            for k in (3, 2, 1):
                sums(ITEMS - k, ITEMS % RING + 4 - k)


RING = 4


def gather_sums(nc, ctx, m, name, table, rows, weight, key, first, last_tile):
    *got, onehot = carve(m, *[[T, H]] * RING, [T, P])
    sb = lambda n, s, d=fp32: ctx.enter_context(nc.sbuf_tensor(name + n, s, d))
    row = [sb(f"row{i}", [P, T], i32) for i in range(RING)]
    local = sb("local", [P, T])
    sum_ps = ctx.enter_context(nc.psum_tensor(name + "sum_ps", [P, H], fp32))
    sem = lambda n: ctx.enter_context(nc.semaphore(name + n))
    gathered = [sem(f"gathered{i}") for i in range(RING)]
    pool_turns = sem("pool_turns")
    row_ready, got_used, onehot_ready, sum_ready, acc_done, dchain = (
        sem("row_ready"), sem("got_used"), sem("onehot"), sem("sum"), sem("acc"), sem("chain"))

    with nc.Block() as block:

        @block.scalar
        def _(act):
            def chunk(c, u, s):
                if not before(u, 1):
                    act.wait_ge(gathered[s], u * (16 * T))
                nc.scalar.copy(row[s][:, :], rows[:, cols(c)]).then_inc(row_ready, 1)
            over_chunks(act, chunk, RING)

        @block.gpsimd
        def _(pool):
            def chunk(c, u, s):
                pool.wait_ge(row_ready, c + 1)
                if not before(c, RING):
                    pool.wait_ge(got_used, c - (RING - 1))
                pool.sem_inc(pool_turns, 1)
                for t in range(T):
                    nc.gpsimd.indirect_dma_start(
                        out=got[s][:, t, :], out_offset=None, in_=table,
                        in_offset=bass.IndirectOffsetOnAxis(ap=row[s][:, t:t + 1], axis=0)).then_inc(gathered[s], 16)
            over_chunks(pool, chunk, RING)

        @block.vector
        def _(dve):
            nc.vector.memset(m.acc[:, :, :], 0.0).then_inc(acc_done, 1)
            with dve.register(name + "k") as k:
                dve.reg_mov(k, 0)

                def chunk(c, u, s):
                    dve.wait_ge(gathered[s], u * (16 * T) + 16 * T)

                    def item(k, j):
                        nc.vector.tensor_scalar(local[:, :], key[:, cols(c)], m.base[:, bass.ds(j, 1)], None,
                                                ALU.subtract).then_inc(dchain, 1)
                        dve.wait_ge(dchain, k + 1)
                        for t in range(T):
                            at = c * T + t
                            wt = weight[:, at:at + 1] if isinstance(at, int) else weight[:, bass.ds(at, 1)]
                            last = nc.vector.tensor_scalar(onehot[:, t, :], m.iota[:, :], local[:, t:t + 1], wt,
                                                           ALU.is_equal, ALU.mult)
                            if t % 4 == 3:
                                last.then_inc(onehot_ready, 1)
                        dve.wait_ge(sum_ready, k + 1)
                        dve.wait_ge(acc_done, k + 1)
                        acc = m.acc[:, bass.ds(j, 1), 0:H].rearrange("p j f -> p (j f)")
                        nc.vector.tensor_tensor(acc, acc, sum_ps[:, :], ALU.add).then_inc(acc_done, 1)
                    over_items(dve, k, first, last_tile, c, item)
                    nc.vector.engine_nop().then_inc(got_used, 1)
                over_chunks(dve, chunk, RING)

        @block.tensor
        def _(pe):
            with pe.register(name + "k") as k:
                pe.reg_mov(k, 0)

                def chunk(c, u, s):
                    def item(k, j):
                        for t in range(T):
                            if t % 4 == 0:
                                pe.wait_ge(onehot_ready, k * 4 + (t // 4 + 1))
                            last = nc.tensor.matmul(sum_ps[:, :], onehot[:, t, :], got[s][:, t, :],
                                                    start=(t == 0), stop=(t == T - 1))
                        last.then_inc(sum_ready, 1)
                    over_items(pe, k, first, last_tile, c, item)
                over_chunks(pe, chunk, RING)


GN = 7
NG = NT // GN
assert NG * GN == NT


def node_layer1(nc, ctx, m, ins, dram):
    scratch, hT, y = carve(m, [NT, H], [GN, P], [GN, NREL1 * H])
    sb = lambda n, s, d=fp32: ctx.enter_context(nc.sbuf_tensor(n, s, d))
    gamma, beta, w = sb("gamma", [P, H]), sb("beta", [P, H]), sb("w_rel", [H, NREL1 * H])
    pb = lambda n, s: ctx.enter_context(nc.psum_tensor(n, s, fp32))
    hT_ps, y_ps = pb("hT_ps", [P, 8, P]), pb("y_ps", [P, 8, 256])
    sem = lambda n: ctx.enter_context(nc.semaphore(n))
    in_sem, var_ready, std_ready, dchain, h_ready = sem("n1_in"), sem("n1_var"), sem("n1_std"), sem("n1_chain"), sem("n1_h")
    tr_ready, tr_copied, y_ready, y_copied, y_out = sem("n1_tr"), sem("n1_trc"), sem("n1_y"), sem("n1_yc"), sem("n1_out")
    wide = lambda a: a.unsqueeze(2).to_broadcast([P, NT, H])

    with nc.Block() as block:

        @block.sync
        def _(sp):
            sp.dma_start(gamma[:, :], ins.gamma.to_broadcast([P, H])).then_inc(in_sem, 16)
            sp.dma_start(beta[:, :], ins.beta.to_broadcast([P, H])).then_inc(in_sem, 16)
            sp.dma_start(w[:, :].rearrange("i (r o) -> i r o", o=H), ins.W.rearrange("(r i) o -> i r o", i=H)).then_inc(in_sem, 16)
            for q in range(NG):
                sp.wait_ge(y_copied, q + 1)
                sp.dma_start(dram.tab1.rearrange("(j p r) f -> p j (r f)", p=P, r=NREL1)[:, q * GN:(q + 1) * GN, :],
                             y).then_inc(y_out, 16)
            sp.wait_ge(y_out, 16 * NG)

        @block.scalar
        def _(act):
            for n in (1, 2, 3):
                square_root(nc, act, m, var_ready, std_ready, n)

        @block.vector
        def _(dve):
            link = Chain(dve, dchain)
            total, count = m.stat[:, 3, :], m.stat[:, 1, :]
            dve.wait_ge(in_sem, 48)
            link(nc.vector.tensor_scalar(total, m.acc[:, :, H], 1e-8, None, ALU.max))
            link(nc.vector.reciprocal(total, total))
            link(nc.vector.tensor_tensor(m.acc[:, :, 0:H], m.acc[:, :, 0:H], wide(total), ALU.mult))
            link(nc.vector.tensor_tensor(m.acc[:, :, 0:H], m.acc[:, :, 0:H], m.h[:, :, :], ALU.add))
            layer_norm(nc, dve, link, m, m.acc[:, :, 0:H], m.h[:, :, :], scratch, var_ready, std_ready, 1,
                       gamma[:, :], beta[:, :])
            link(nc.vector.tensor_tensor(m.x[:, :, :], m.x[:, :, :], m.h[:, :, :], ALU.add))
            nc.vector.tensor_scalar(count, m.acc[:, :, H + 1], 1.0, None, ALU.max).then_inc(var_ready, 1)
            dve.wait_ge(std_ready, 2)
            link(nc.vector.reciprocal(m.rdeg[:, :], m.stat[:, 2, :]))
            layer_norm(nc, dve, link, m, m.x[:, :, :], m.h[:, :, :], scratch, var_ready, std_ready, 3)
            nc.vector.engine_nop().then_inc(h_ready, 1)
            for q in range(NG):
                dve.wait_ge(tr_ready, q + 1)
                nc.vector.tensor_copy(hT[0:H, :, :], hT_ps[0:H, 0:GN, :]).then_inc(tr_copied, 1)
                dve.wait_ge(y_ready, q + 1)
                if q:
                    dve.wait_ge(y_out, 16 * q)
                nc.vector.tensor_copy(y, y_ps[:, 0:GN, 0:NREL1 * H]).then_inc(y_copied, 1)

        @block.tensor
        def _(pe):
            pe.wait_ge(h_ready, 1)
            for q in range(NG):
                for t in range(GN):
                    last = nc.tensor.transpose(hT_ps[0:H, t, :], m.h[:, q * GN + t, :], m.ident[:, :])
                last.then_inc(tr_ready, 1)
                pe.wait_ge(tr_copied, q + 1)
                if q:
                    pe.wait_ge(y_copied, q)
                for t in range(GN):
                    last = nc.tensor.matmul(y_ps[:, t, 0:NREL1 * H], hT[0:H, t, :], w[:, :], start=True, stop=True)
                last.then_inc(y_ready, 1)


def node_layer2(nc, ctx, m, ins, dram):
    scratch, hT, mid, y = carve(m, [NT, H], [GN, P], [4, GN * P], [GN, NREL2 * H])
    NPAIR = NREL2 // 2
    sb = lambda n, s, d=fp32: ctx.enter_context(nc.sbuf_tensor(n, s, d))
    bias = sb("n2_bias", [P, H])
    wa, wb, ba = sb("wa", [H, NREL2 * H]), sb("wb", [2 * H, NPAIR, 2 * H]), sb("ba", [2 * H, 1])
    pb = lambda n, s: ctx.enter_context(nc.psum_tensor(n, s, fp32))
    hT_ps, mid_ps, y_ps = pb("n2_hT_ps", [P, 8, P]), pb("mid_ps", [P, 2, 512]), pb("n2_y_ps", [P, 4, 512])
    HALF = (4 * P, 3 * P)
    sem = lambda n: ctx.enter_context(nc.semaphore(n))
    in_sem, z_ready, var_ready, std_ready, dchain, h_ready = (
        sem("n2_in"), sem("n2_zero"), sem("n2_var"), sem("n2_std"), sem("n2_chain"), sem("n2_h"))
    tr_ready, tr_copied, mid_ready, mid_done, y_ready, y_copied, y_out = (
        sem("n2_tr"), sem("n2_trc"), sem("n2_mid"), sem("n2_midc"), sem("n2_y"), sem("n2_yc"), sem("n2_out"))

    with nc.Block() as block:

        @block.sync
        def _(sp):
            sp.wait_ge(z_ready, 1)
            sp.dma_start(bias[:, :], ins.b.to_broadcast([P, H])).then_inc(in_sem, 16)
            sp.dma_start(wa[:, :].rearrange("i (r o) -> i r o", o=H), ins.weight1.rearrange("r i o -> i r o")).then_inc(in_sem, 16)
            for a in (0, 1):
                sp.dma_start(wb[a * H:(a + 1) * H, :, a * H:(a + 1) * H],
                             ins.weight2.rearrange("(q a) i o -> a i q o", a=2)[a]).then_inc(in_sem, 16)
                sp.dma_start(ba[a * H:(a + 1) * H, :], ins.bias1).then_inc(in_sem, 16)
            for q in range(NG):
                sp.wait_ge(y_copied, (q + 1) * GN)
                sp.dma_start(dram.tab2.rearrange("(j p r) f -> p j (r f)", p=P, r=NREL2)[:, q * GN:(q + 1) * GN, :],
                             y).then_inc(y_out, 16)
            sp.wait_ge(y_out, 16 * NG)

        @block.scalar
        def _(act):
            square_root(nc, act, m, var_ready, std_ready, 1)
            act.wait_ge(in_sem, 96)
            for q in range(NG):
                for r in range(NPAIR):
                    for a, at in ((0, 0), (1, 4 * P)):
                        n = (q * NPAIR + r) * 2 + a
                        act.wait_ge(mid_ready, n + 1)
                        nc.scalar.activation(mid[0:2 * H, r, at:at + HALF[a]], mid_ps[0:2 * H, a, 0:HALF[a]],
                                             ACT.Relu, bias=ba[:, 0:1]).then_inc(mid_done, 1)

        @block.vector
        def _(dve):
            link = Chain(dve, dchain)
            nc.vector.memset(wb[:, :, :], 0.0).then_inc(z_ready, 1)
            dve.wait_ge(in_sem, 96)
            link(nc.vector.tensor_tensor(m.x[:, :, :], m.x[:, :, :], m.acc[:, :, 0:H], ALU.add))
            link(nc.vector.tensor_tensor(m.x[:, :, :], m.x[:, :, :],
                                         bias[:, :].unsqueeze(1).to_broadcast([P, NT, H]), ALU.add))
            layer_norm(nc, dve, link, m, m.x[:, :, :], m.h[:, :, :], scratch, var_ready, std_ready, 1)
            nc.vector.engine_nop().then_inc(h_ready, 1)
            for q in range(NG):
                dve.wait_ge(tr_ready, q + 1)
                nc.vector.tensor_copy(hT[0:H, :, :], hT_ps[0:H, 0:GN, :]).then_inc(tr_copied, 1)
                for t in range(GN):
                    dve.wait_ge(y_ready, q * GN + t + 1)
                    if t == 0 and q:
                        dve.wait_ge(y_out, 16 * q)
                    nc.vector.tensor_copy(y[:, t, :], y_ps[:, (q * GN + t) % 4, 0:NREL2 * H]).then_inc(y_copied, 1)

        @block.tensor
        def _(pe):
            pe.wait_ge(h_ready, 1)
            pe.wait_ge(in_sem, 96)
            for q in range(NG):
                for t in range(GN):
                    last = nc.tensor.transpose(hT_ps[0:H, t, :], m.h[:, q * GN + t, :], m.ident[:, :])
                last.then_inc(tr_ready, 1)
                pe.wait_ge(tr_copied, q + 1)
                flat = hT.rearrange("p a b -> p (a b)")
                for r in range(NPAIR):
                    for a, at in ((0, 0), (1, 4 * P)):
                        n = (q * NPAIR + r) * 2 + a
                        if n >= 2:
                            pe.wait_ge(mid_done, n - 1)
                        nc.tensor.matmul(mid_ps[0:2 * H, a, 0:HALF[a]], wa[:, 2 * H * r:2 * H * (r + 1)],
                                         flat[0:H, at:at + HALF[a]], start=True, stop=True).then_inc(mid_ready, 1)
                pe.wait_ge(mid_done, (q + 1) * NPAIR * 2)
                for t in range(GN):
                    n = q * GN + t
                    if n >= 4:
                        pe.wait_ge(y_copied, n - 3)
                    for r in range(NPAIR):
                        last = nc.tensor.matmul(y_ps[:, n % 4, 2 * H * r:2 * H * (r + 1)],
                                                mid[0:2 * H, r, t * P:(t + 1) * P], wb[:, r, :],
                                                start=True, stop=True)
                    last.then_inc(y_ready, 1)


def node_layer3(nc, ctx, m, ins, dram):
    scratch, = carve(m, [NT, H])
    bias = ctx.enter_context(nc.sbuf_tensor("n3_bias", [P, H], fp32))
    sem = lambda n: ctx.enter_context(nc.semaphore(n))
    in_sem, var_ready, std_ready, dchain, tab_out, h_ready = (
        sem("n3_in"), sem("n3_var"), sem("n3_std"), sem("n3_chain"), sem("n3_out"), sem("n3_h"))

    with nc.Block() as block:

        @block.sync
        def _(sp):
            sp.dma_start(bias[:, :], ins.bias2.to_broadcast([P, H])).then_inc(in_sem, 16)
            sp.wait_ge(h_ready, 1)
            sp.dma_start(dram.tab3.rearrange("(j p) f -> p j f", p=P), m.h[:, :, :]).then_inc(tab_out, 16)
            sp.wait_ge(tab_out, 16)

        @block.scalar
        def _(act):
            square_root(nc, act, m, var_ready, std_ready, 1)

        @block.vector
        def _(dve):
            link = Chain(dve, dchain)
            dve.wait_ge(in_sem, 16)
            link(nc.vector.tensor_tensor(m.acc[:, :, 0:H], m.acc[:, :, 0:H],
                                         bias[:, :].unsqueeze(1).to_broadcast([P, NT, H]), ALU.add))
            link(nc.vector.tensor_scalar(m.acc[:, :, 0:H], m.acc[:, :, 0:H], 0.0, None, ALU.max))
            link(nc.vector.tensor_tensor(m.x[:, :, :], m.x[:, :, :], m.acc[:, :, 0:H], ALU.add))
            layer_norm(nc, dve, link, m, m.x[:, :, :], m.h[:, :, :], scratch, var_ready, std_ready, 1)
            nc.vector.tensor_tensor(m.h[:, :, :], m.h[:, :, :], m.rdeg[:, :].unsqueeze(2).to_broadcast([P, NT, H]),
                                    ALU.mult).then_inc(h_ready, 1)


def finish(nc, ctx, m, out):
    sem = lambda n: ctx.enter_context(nc.semaphore(n))
    dchain, x_ready, stored = sem("f_chain"), sem("f_ready"), sem("stored")

    with nc.Block() as block:

        @block.vector
        def _(dve):
            link = Chain(dve, dchain)
            link(nc.vector.tensor_tensor(m.acc[:, :, 0:H], m.acc[:, :, 0:H],
                                         m.rdeg[:, :].unsqueeze(2).to_broadcast([P, NT, H]), ALU.mult))
            nc.vector.tensor_tensor(m.x[:, :, :], m.x[:, :, :], m.acc[:, :, 0:H], ALU.add).then_inc(x_ready, 1)

        @block.sync
        def _(sp):
            sp.wait_ge(x_ready, 1)
            sp.dma_start(out.rearrange("(j p) f -> p j f", p=P), m.x[:, :, :]).then_inc(stored, 16)
            sp.wait_ge(stored, 16)


def gnn(nc, ins, out):
    dram = Memory()
    dram.emb = nc.dram_tensor("emb_both", [NTYPE, 2 * G], fp32).ap()
    dram.sorted = nc.dram_tensor("sorted_edges", [EP, SORTED], fp32).ap()
    dram.dst = nc.dram_tensor("sorted_dst", [EP], i32).ap()
    dram.rec = nc.dram_tensor("records", [EP, REC], fp32).ap()
    dram.tab1 = nc.dram_tensor("table1", [NP * NREL1, H], fp32).ap()
    dram.tab2 = nc.dram_tensor("table2", [NP * NREL2, H], fp32).ap()
    dram.tab3 = nc.dram_tensor("table3", [NP, H], fp32).ap()
    with ExitStack() as whole:
        m = allocate(nc, whole)
        with ExitStack() as ctx:
            load(nc, ctx, m, ins, dram)
        with ExitStack() as ctx:
            reorder(nc, ctx, m, ins, dram)
        with ExitStack() as ctx:
            setup(nc, ctx, m, ins, dram)
        with ExitStack() as ctx:
            layer0_edges(nc, ctx, m, ins, dram)
        with ExitStack() as ctx:
            layer0_sums(nc, ctx, m, dram)
        with ExitStack() as ctx:
            node_layer1(nc, ctx, m, ins, dram)
        with ExitStack() as ctx:
            s_src, s_row1, s_w = m.in_src_order()
            gather_sums(nc, ctx, m, "l1_", dram.tab1, s_row1, s_w, s_src, m.sfirst, m.slast)
        with ExitStack() as ctx:
            node_layer2(nc, ctx, m, ins, dram)
        with ExitStack() as ctx:
            gather_sums(nc, ctx, m, "l2_", dram.tab2, m.row2, m.w1, m.dstf, m.dfirst, m.dlast)
        with ExitStack() as ctx:
            node_layer3(nc, ctx, m, ins, dram)
        with ExitStack() as ctx:
            gather_sums(nc, ctx, m, "l3_", dram.tab3, m.srcf, m.w, m.dstf, m.dfirst, m.dlast)
        with ExitStack() as ctx:
            finish(nc, ctx, m, out)


def kernel(x, src, dst, edge_attr_40, edge_type_4, edge_type_8, edge_weight, edge_weight1, node_type_119, node_vec,
           L0_gnn_W1, L0_gnn_b1, L0_gnn_W2, L0_gnn_b2, L0_gnn_emb, L0_gnn_adaptW, L0_gnn_gamma, L0_gnn_beta,
           L1_gnn_W, L1_gnn_b, L2_gnn_weight1, L2_gnn_weight2, L2_gnn_bias1, L2_gnn_bias2):
    import numpy as _np
    import concourse.bacc as _bacc
    from concourse import mybir as _mybir
    from concourse.bass_utils import run_bass_kernel_spmd as _run

    def padded(a, n, fill=0):
        a = _np.asarray(a)
        out = _np.full((n,) + a.shape[1:], fill, a.dtype)
        out[:a.shape[0]] = a
        return out

    def by_chunk(a):
        return a.reshape(NC, P, T).transpose(1, 0, 2).reshape(P, NE)

    def by_tile(a):
        return a.reshape(NT, P).T

    dst_natural = padded(dst, EP + 1, N)
    attr = padded(edge_attr_40, EP)
    laid = {
        "x": padded(x, NP), "src": by_chunk(padded(src, EP, N)), "dst": dst_natural[:EP].reshape(NC, P, T).transpose(0, 2, 1).reshape(EP),
        "dst_laid": by_chunk(dst_natural[:EP]), "dst_after": by_chunk(dst_natural[1:]),
        "attr": attr, "attrT": attr.reshape(NC, P, T, R).transpose(3, 0, 2, 1).reshape(R, EP),
        "type4": by_chunk(padded(edge_type_4, EP)), "type8": by_chunk(padded(edge_type_8, EP)),
        "w": by_chunk(padded(edge_weight, EP)), "w1": by_chunk(padded(_np.asarray(edge_weight1).reshape(-1), EP)),
        "ztype": by_tile(padded(node_type_119, NP)), "mult": by_tile(padded(node_vec, NP)),
        "W1T": _np.asarray(L0_gnn_W1).T, "b1": _np.asarray(L0_gnn_b1).reshape(H, 1),
        "W2T": _np.concatenate([_np.asarray(L0_gnn_W2).T, _np.asarray(L0_gnn_b2).reshape(1, H)]),
        "emb": L0_gnn_emb, "embT": _np.asarray(L0_gnn_emb).T, "adaptT": _np.asarray(L0_gnn_adaptW).T,
        "gamma": _np.asarray(L0_gnn_gamma).reshape(1, H), "beta": _np.asarray(L0_gnn_beta).reshape(1, H),
        "W": L1_gnn_W, "b": _np.asarray(L1_gnn_b).reshape(1, H),
        "weight1": L2_gnn_weight1, "weight2": L2_gnn_weight2,
        "bias1": _np.asarray(L2_gnn_bias1).reshape(H, 1), "bias2": _np.asarray(L2_gnn_bias2).reshape(1, H),
    }
    nc = _bacc.Bacc("TRN2", target_bir_lowering=False, num_devices=1)
    arrays, ins = {}, Memory()
    for name, a in laid.items():
        a = _np.ascontiguousarray(a)
        arrays[f"in_{name}"] = a
        ins.__dict__[name] = nc.dram_tensor(f"in_{name}", a.shape, _mybir.dt.from_np(a.dtype), kind="ExternalInput").ap()
    out = nc.dram_tensor("out_x", (NP, H), fp32, kind="ExternalOutput").ap()
    gnn(nc, ins, out)
    r = _run(nc, [arrays], core_ids=[0])
    return r.results[0]["out_x"][:N]
```

```python
import concourse.bass as bass
from concourse import mybir
from contextlib import ExitStack
import numpy as np

fp32 = mybir.dt.float32
bf16 = mybir.dt.bfloat16
i32 = mybir.dt.int32
ALU = mybir.AluOpType
ACT = mybir.ActivationFunctionType
AX = mybir.AxisListType

P = 128
N = 6250
H = 48
E = 206250
R = 40
G = 32
NTYPE = 119
NREL1, NREL2 = 4, 8
NT = -(-N // P)
NP = NT * P
T = 16
CH = T * P
NC = -(-E // CH)
EP = NC * CH
NE = NC * T
ITEMS = NC + NT - 1
REC = 2 * H + G + 4
SRC, ROW1, WEIGHT = 2 * H + G + 1, 2 * H + G + 2, 2 * H + G + 3
TW = H + G + 1
CUTOFF = 6.0
EPS = 1e-5
HALFPI = float(np.pi / 2)


class Memory:

    def in_src_order(self):
        return self.cut[:, :], self.place[:, :], self.row1[:, :].bitcast(fp32)


def allocate(nc, ctx):
    m = Memory()

    def sb(name, shape, dt=fp32):
        return ctx.enter_context(nc.sbuf_tensor(name, shape, dt))

    m.srcf = sb("srcf", [P, NE])
    m.dstf = sb("dstf", [P, NE])
    m.w = sb("w", [P, NE])
    m.w1 = sb("w1", [P, NE])
    m.cut = sb("cut", [P, NE])
    m.row1 = sb("row1", [P, NE], i32)
    m.row2 = sb("row2", [P, NE], i32)
    m.place = sb("place", [P, NE], i32)
    m.x = sb("x_res", [P, NT, H])
    m.h = sb("h_norm", [P, NT, H])
    m.acc = sb("acc", [P, NT, H + 2])
    m.emb = sb("emb_rows", [P, NT, 2 * G])
    m.mult = sb("mult", [P, NT])
    m.rdeg = sb("rdeg", [P, NT])
    m.iota = sb("iota", [P, P])
    m.node = sb("node", [P, NT])
    m.base = sb("base", [P, NT])
    m.ident = sb("ident", [P, P])
    m.lower = sb("lower", [P, P])
    m.ones = sb("ones", [P, P])
    m.sfirst = sb("sfirst", [1, NC], i32)
    m.slast = sb("slast", [1, NC], i32)
    m.dfirst = sb("dfirst", [1, NC], i32)
    m.dlast = sb("dlast", [1, NC], i32)
    m.stat = sb("stat", [P, 4, NT])
    m.square = sb("square", [P, H])
    m.zero = sb("zero_bf", [P, 512], bf16)
    m.iota_bf = sb("iota_bf", [P, P], bf16)
    m.ident_bf = sb("ident_bf", [P, P], bf16)
    m.work = sb("work", [P, WORK + T0])
    m.t0 = m.work[:, WORK:].bitcast(bf16).rearrange("p (j a f) -> p j a f", a=3, f=TW + 1)
    m.emb3 = m.emb[:, :, 0:3 * G // 2].bitcast(bf16)
    m.ichunk = sb("ichunk", [1, ITEMS], i32)
    m.itile = sb("itile", [1, ITEMS], i32)
    m.ibase = sb("item_base", [P, ITEMS])
    m.unsorted = sb("unsorted", [1, 1], i32)
    m.sp_turns, m.pool_turns, m.pe_turns, m.dve_turns = (
        ctx.enter_context(nc.semaphore(n)) for n in ("sp_turns", "pool_turns", "pe_turns", "dve_turns"))
    return m


WORK = 15700
T0 = NT * 3 * (TW + 1) // 2
SORTED = R + 6


def carve(m, *shapes, all_of_it=False):
    at, out = 0, []
    for shape in shapes:
        n = int(np.prod(shape))
        v = m.work[:, at:at + n]
        if len(shape) == 2:
            v = v.rearrange("p (a b) -> p a b", b=shape[1])
        out.append(v)
        at += n
    assert at <= (WORK + T0 if all_of_it else WORK), at
    return out


def over_steps(eng, total, ring, step):
    for n in range(ring):
        step(n, 0, n)
    rounds = total // ring
    with eng.Fori(1, rounds) as v:
        u = eng.snap(v, min_val=1, max_val=rounds - 1)
        for s in range(ring):
            step(u * ring + s, u, s)
    for n in range(rounds * ring, total):
        step(n, rounds, n % ring)


def over_chunks(eng, chunk, ring=2):
    over_steps(eng, NC, ring, chunk)


def before(n, least):
    return isinstance(n, int) and n < least


def col(n):
    return bass.ds(n, 1) if not isinstance(n, int) else slice(n, n + 1)


def over_items(eng, k, first, last, c, item):
    at = bass.ds(c, 1) if not isinstance(c, int) else slice(c, c + 1)
    lo = eng.value_load(first[0:1, at], min_val=0, max_val=NT - 1)
    hi = eng.value_load(last[0:1, at], min_val=0, max_val=NT - 1)
    with eng.Fori(lo, hi + 1) as v:
        item(eng.snap(k, min_val=0, max_val=NC + NT), eng.snap(v, min_val=0, max_val=NT - 1))
        eng.reg_add(k, k, 1)
    return hi


def cols(c, n=T):
    return bass.ds(c * n, n) if not isinstance(c, int) else slice(c * n, (c + 1) * n)


class Chain:

    def __init__(self, eng, sem, base=0):
        self.eng, self.sem, self.base, self.n = eng, sem, base, 0

    def __call__(self, step):
        self.n += 1
        step.then_inc(self.sem, 1)
        self.eng.wait_ge(self.sem, self.base + self.n)


def layer_norm(nc, dve, link, m, src, out, scratch, var_ready, std_ready, nth, gamma=None, beta=None):
    mean, var = m.stat[:, 0, :], m.stat[:, 1, :]
    wide = lambda a: a.unsqueeze(2).to_broadcast([P, NT, H])
    link(nc.vector.reduce_sum(mean, src, AX.X))
    link(nc.vector.tensor_scalar(mean, mean, -1.0 / H, None, ALU.mult))
    link(nc.vector.tensor_tensor(out, src, wide(mean), ALU.add))
    link(nc.vector.tensor_tensor(scratch, out, out, ALU.mult))
    link(nc.vector.reduce_sum(var, scratch, AX.X))
    nc.vector.tensor_scalar(var, var, 1.0 / H, EPS, ALU.mult, ALU.add).then_inc(var_ready, 1)
    dve.wait_ge(std_ready, nth)
    link(nc.vector.reciprocal(var, m.stat[:, 2, :]))
    link(nc.vector.tensor_tensor(out, out, wide(var), ALU.mult))
    if gamma is None:
        link(nc.vector.tensor_scalar(out, out, 0.0, None, ALU.max))
    else:
        feat = lambda a: a.unsqueeze(1).to_broadcast([P, NT, H])
        link(nc.vector.tensor_tensor(out, out, feat(gamma), ALU.mult))
        link(nc.vector.tensor_tensor(out, out, feat(beta), ALU.add))


def split(nc, link, hi, mid, lo, x, rest):
    link(nc.vector.tensor_copy(hi, x))
    link(nc.vector.tensor_tensor(rest, x, hi, ALU.subtract))
    link(nc.vector.tensor_copy(mid, rest))
    link(nc.vector.tensor_tensor(lo, rest, mid, ALU.subtract))


def square_root(nc, act, m, var_ready, std_ready, nth):
    act.wait_ge(var_ready, nth)
    nc.scalar.activation(m.stat[:, 2, :], m.stat[:, 1, :], ACT.Sqrt).then_inc(std_ready, 1)


def sort_buffers(nc, ctx, m, name):
    b = Memory()
    sb = lambda n, s, d=fp32: ctx.enter_context(nc.sbuf_tensor(name + n, s, d))
    _, bucket, mask, b.scan, one, b.place, prod0, prod1 = carve(
        m, [NE], [NE // 2], [NE // 2], [NE], [NE // 2], [NE], [NE], [NE])
    b.bucket, b.mask, b.one = bucket.bitcast(bf16), mask.bitcast(bf16), one.bitcast(bf16)
    b.prod = (prod0, prod1)
    b.count = sb("count", [P, NT])
    b.offset = sb("offset", [P, NT])
    b.end = sb("end", [P, NT])
    b.before_ps = ctx.enter_context(nc.psum_tensor(name + "before_ps", [P, NT], fp32))
    b.total_ps = ctx.enter_context(nc.psum_tensor(name + "total_ps", [P, NT], fp32))
    sem = lambda n: ctx.enter_context(nc.semaphore(name + n))
    b.counted, b.summed, b.prod_ready, b.added = sem("counted"), sem("summed"), sem("prod_ready"), sem("added")
    return b


def sort_places(nc, dve, link, b, raw, bucket_raw, out):
    link(nc.vector.memset(b.one, 1.0))
    link(nc.vector.tensor_scalar(bucket_raw, raw, 7, None, ALU.arith_shift_right))
    link(nc.vector.tensor_copy(b.bucket, bucket_raw))
    for t in range(NT):
        link(nc.vector.tensor_scalar(b.mask, b.bucket, float(t), 0.0, ALU.is_equal, ALU.add,
                                     accum_out=b.count[:, t:t + 1]))
    nc.vector.engine_nop().then_inc(b.counted, 1)
    dve.wait_ge(b.summed, 1)
    link(nc.vector.tensor_copy(b.offset[:, :], b.before_ps[:, :]))
    link(nc.vector.tensor_tensor_scan(b.end[:, :], b.one[:, 0:NT], b.total_ps[:, :], 0.0, ALU.mult, ALU.add))
    link(nc.vector.tensor_tensor(b.offset[:, 1:NT], b.offset[:, 1:NT], b.end[:, 0:NT - 1], ALU.add))
    for t in range(NT):
        link(nc.vector.tensor_scalar(b.mask, b.bucket, float(t), None, ALU.is_equal))
        link(nc.vector.tensor_tensor_scan(b.scan, b.one, b.mask, b.offset[:, t:t + 1], ALU.mult, ALU.add))
        if t >= 2:
            dve.wait_ge(b.added, t)
        nc.vector.tensor_tensor(b.prod[t % 2], b.scan, b.mask, ALU.mult).then_inc(b.prod_ready, 1)
        dve.wait_ge(b.prod_ready, t + 1)
    dve.wait_ge(b.added, NT + 1)
    link(nc.vector.tensor_copy(out, b.place))


def sort_adds(nc, pool, b):
    nc.gpsimd.memset(b.place, -1.0).then_inc(b.added, 1)
    for t in range(NT):
        pool.wait_ge(b.prod_ready, t + 1)
        pool.wait_ge(b.added, t + 1)
        nc.gpsimd.tensor_tensor(b.place, b.place, b.prod[t % 2], ALU.add).then_inc(b.added, 1)


def sort_sums(nc, pe, m, b):
    pe.wait_ge(b.counted, 1)
    nc.tensor.matmul(b.before_ps[:, :], m.lower[:, :], b.count[:, :], start=True, stop=True)
    nc.tensor.matmul(b.total_ps[:, :], m.ones[:, :], b.count[:, :], start=True, stop=True).then_inc(b.summed, 1)


def raw_views(m):
    return m.place[:, :], m.work[:, 0:NE].bitcast(i32)


def load(nc, ctx, m, ins, dram):
    raw_src, raw_dst = raw_views(m)
    _, after, tile_a, tile_b, diff = carve(m, [NE], [NE], [NE], [NE], [NE])
    after = after.bitcast(i32)
    worst, row = m.stat[:, 0, 0:1], m.work[0:1, 5 * NE:5 * NE + P]
    sb = lambda n, s, d=fp32: ctx.enter_context(nc.sbuf_tensor(n, s, d))
    icol, inode, ibase = sb("icol", [P, P], i32), sb("inode", [P, NT], i32), sb("ibase", [P, NT], i32)
    worst_ps = ctx.enter_context(nc.psum_tensor("worst_ps", [1, P], fp32))
    sem = lambda n: ctx.enter_context(nc.semaphore(n))
    dst_in, rest_in, iotas, dchain, worst_ready, worst_row = (
        sem("dst_in"), sem("rest_in"), sem("iotas"), sem("load_chain"), sem("worst_ready"), sem("worst_row"))

    with nc.Block() as block:

        @block.sync
        def _(sp):
            sp.dma_start(raw_dst, ins.dst_laid).then_inc(dst_in, 16)
            sp.dma_start(after, ins.dst_after).then_inc(dst_in, 16)
            for to, what in ((raw_src, ins.src), (m.w[:, :], ins.w), (m.w1[:, :], ins.w1),
                             (m.row1[:, :], ins.type4), (m.row2[:, :], ins.type8)):
                sp.dma_start(to, what).then_inc(rest_in, 16)
            sp.wait_ge(rest_in, 80)

        @block.gpsimd
        def _(pool):
            nc.gpsimd.iota(icol[:, :], [[1, P]], 0, 0)
            nc.gpsimd.iota(inode[:, :], [[P, NT]], 0, 1)
            nc.gpsimd.iota(ibase[:, :], [[P, NT]], 0, 0).then_inc(iotas, 1)

        @block.vector
        def _(dve):
            link = Chain(dve, dchain)
            dve.wait_ge(iotas, 1)
            nc.vector.tensor_copy(m.iota[:, :], icol[:, :])
            nc.vector.tensor_copy(m.iota_bf[:, :], icol[:, :])
            nc.vector.tensor_copy(m.base[:, :], ibase[:, :])
            nc.vector.memset(m.zero[:, :], 0.0)
            nc.vector.memset(m.ones[:, :], 1.0)
            link(nc.vector.tensor_copy(m.node[:, :], inode[:, :]))
            number = m.node[:, 0:1]
            nc.vector.tensor_scalar(m.lower[:, :], m.iota[:, :], number, None, ALU.is_gt)
            nc.vector.tensor_scalar(m.ident_bf[:, :], m.iota_bf[:, :], number, None, ALU.is_equal)
            link(nc.vector.tensor_scalar(m.ident[:, :], m.iota[:, :], number, None, ALU.is_equal))
            dve.wait_ge(dst_in, 32)
            link(nc.vector.tensor_scalar(tile_a.bitcast(i32), raw_dst, 7, None, ALU.arith_shift_right))
            link(nc.vector.tensor_scalar(tile_b.bitcast(i32), after, 7, None, ALU.arith_shift_right))
            link(nc.vector.tensor_tensor(diff, tile_a.bitcast(i32), tile_b.bitcast(i32), ALU.subtract))
            nc.vector.tensor_reduce(worst, diff, AX.X, ALU.max).then_inc(worst_ready, 1)
            dve.wait_ge(worst_row, 1)
            link(nc.vector.tensor_reduce(row[0:1, 0:1], worst_ps[0:1, :], AX.X, ALU.max))
            link(nc.vector.tensor_scalar(m.unsorted[:, :], row[0:1, 0:1], 0.0, None, ALU.is_gt))

        @block.tensor
        def _(pe):
            pe.wait_ge(worst_ready, 1)
            nc.tensor.matmul(worst_ps[0:1, :], worst, m.ident[:, :], start=True, stop=True).then_inc(worst_row, 1)


def reorder(nc, ctx, m, ins, dram):
    raw_src, raw_dst = raw_views(m)
    edge = m.work[:, 8 * NE:8 * NE + T * SORTED].rearrange("p (t f) -> p t f", f=SORTED)
    fields = (raw_src, raw_dst, m.w[:, :], m.w1[:, :], m.row1[:, :], m.row2[:, :])
    spot_all = m.acc[:, :, :].rearrange("p j f -> p (j f)")[:, 0:NE].bitcast(i32)
    spot = ctx.enter_context(nc.sbuf_tensor("spot", [P, T], i32))
    b = sort_buffers(nc, ctx, m, "r_")
    sem = lambda n: ctx.enter_context(nc.semaphore(n))
    dchain, attr_in, filled, scattered, fields_in, dst_out, placed = (
        sem("r_chain"), sem("r_attr"), sem("r_filled"), sem("r_scattered"), sem("r_fields"), sem("r_dst"), sem("r_placed"))
    buffer_free = sem("r_free")

    def flag(eng):
        return eng.value_load(m.unsorted[0:1, 0:1], min_val=0, max_val=1)

    with nc.Block() as block:

        @block.sync
        def _(sp):
            with sp.If(flag(sp)), nc.allow_non_contiguous_dma(reason="the general path"):
                sp.wait_ge(placed, 1)
                with sp.Fori(0, NC) as v:
                    c = sp.snap(v, min_val=0, max_val=NC - 1)
                    sp.wait_ge(buffer_free, c + 1)
                    sp.sem_inc(m.sp_turns, 1)
                    sp.dma_start(edge[:, :, 0:R], ins.attr.rearrange("(c p t) r -> p c t r", p=P, t=T)[:, col(c), :, :]
                                 .rearrange("p c t r -> p (c t) r")).then_inc(attr_in, 16)
                sp.wait_ge(buffer_free, NC + 1)
                with sp.Fori(0, NC) as v:
                    c = sp.snap(v, min_val=0, max_val=NC - 1)
                    for f, to in enumerate(fields):
                        to = to if f in (2, 3) else to.bitcast(fp32)
                        sp.dma_start(to[:, cols(c)],
                                     dram.sorted.rearrange("(c p t) f -> p c t f", p=P, t=T)[:, col(c), :, R + f]
                                     .rearrange("p c t -> p (c t)")).then_inc(fields_in, 16)
                sp.wait_ge(fields_in, 16 * NC * len(fields))
                for t in range(T):
                    sp.dma_start(dram.dst.rearrange("(c t p) -> p c t", p=P, t=T)[:, :, t],
                                 raw_dst.rearrange("p (c t) -> p c t", t=T)[:, :, t]).then_inc(dst_out, 16)
                sp.wait_ge(dst_out, 16 * T)

        @block.tensor
        def _(pe):
            with pe.If(flag(pe)):
                sort_sums(nc, pe, m, b)

        @block.vector
        def _(dve):
            with dve.If(flag(dve)):
                link = Chain(dve, dchain)
                sort_places(nc, dve, link, b, raw_dst, spot_all, spot_all)
                nc.vector.engine_nop().then_inc(placed, 1)
                with dve.Fori(0, NC) as v:
                    c = dve.snap(v, min_val=0, max_val=NC - 1)
                    dve.wait_ge(attr_in, c * 16 + 16)
                    for f, have in enumerate(fields):
                        to = edge[:, :, R + f]
                        nc.vector.tensor_copy(to if f in (2, 3) else to.bitcast(i32), have[:, cols(c)])
                    nc.vector.tensor_copy(spot[:, :], spot_all[:, cols(c)]).then_inc(filled, 1)

        @block.gpsimd
        def _(pool):
            with pool.If(flag(pool)):
                sort_adds(nc, pool, b)
                pool.sem_inc(buffer_free, 1)
                with pool.Fori(0, NC) as v:
                    c = pool.snap(v, min_val=0, max_val=NC - 1)
                    pool.wait_ge(filled, c + 1)
                    pool.sem_inc(m.pool_turns, 1)
                    for t in range(T):
                        nc.gpsimd.indirect_dma_start(
                            out=dram.sorted, out_offset=bass.IndirectOffsetOnAxis(ap=spot[:, t:t + 1], axis=0),
                            in_=edge[:, t, :], in_offset=None).then_inc(scattered, 16)
                    pool.wait_ge(scattered, c * (16 * T) + 16 * T)
                    pool.sem_inc(buffer_free, 1)


def setup(nc, ctx, m, ins, dram):
    raw_src, raw_dst = raw_views(m)
    bucket_raw = m.cut[:, :].bitcast(i32)
    b = sort_buffers(nc, ctx, m, "s_")
    angles, inside = b.prod
    sb = lambda n, s, d=fp32: ctx.enter_context(nc.sbuf_tensor(n, s, d))
    edge0, column, order = sb("edge0", [P, NC]), sb("column", [P, 2]), sb("order", [1, NC])
    iitem, item, past = sb("iitem", [P, ITEMS], i32), sb("item", [P, ITEMS]), sb("past", [P, ITEMS])
    iedge, ended = sb("iedge", [P, NC], i32), sb("ended", [P, 2 * NC])
    draw = sb("draw", [1, 2, NC], i32)
    ztype = sb("ztype", [P, NT], i32)
    embT, adaptT, both = sb("embT", [G, NTYPE]), sb("adaptT", [G, G]), sb("both", [NTYPE, 2 * G])
    ps_emb = ctx.enter_context(nc.psum_tensor("ps_emb", [P, G], fp32))
    ps_column = ctx.enter_context(nc.psum_tensor("ps_column", [P, 2], fp32))
    ps_tiles = ctx.enter_context(nc.psum_tensor("ps_tiles", [P, 2 * NC], fp32))
    ps_chunk = ctx.enter_context(nc.psum_tensor("ps_chunk", [P, ITEMS], fp32))
    sem = lambda n: ctx.enter_context(nc.semaphore(n))
    x_in, emb_in, iotas, emb_mm, both_ready, both_out, emb_rows_in, ends_in = (
        sem("x_in"), sem("emb_in"), sem("s_iotas"), sem("emb_mm"), sem("both_ready"), sem("both_out"),
        sem("emb_rows_in"), sem("ends_in"))
    var_ready, std_ready, dchain, cut_ready, angle, table_in, table_sum = (
        sem("var0"), sem("std0"), sem("setup_chain"), sem("cut_ready"), sem("angle"), sem("table_in"), sem("table_sum"))
    wide48 = lambda a: a.unsqueeze(2).to_broadcast([P, NT, H])

    with nc.Block() as block:

        @block.sync
        def _(sp):
            with nc.allow_non_contiguous_dma(reason="small arrays, once"):
                sp.dma_start(embT[:, :], ins.embT).then_inc(emb_in, 16)
                sp.dma_start(adaptT[:, :], ins.adaptT).then_inc(emb_in, 16)
                sp.dma_start(both[:, 0:G], ins.emb).then_inc(emb_in, 16)
                sp.dma_start(ztype[:, :], ins.ztype).then_inc(emb_in, 16)
                sp.dma_start(m.x[:, :, :], ins.x.rearrange("(j p) f -> p j f", p=P)).then_inc(x_in, 16)
                sp.dma_start(m.mult[:, :], ins.mult).then_inc(x_in, 16)
                sp.dma_start(draw[0:1, 0, :], raw_dst.rearrange("p (c t) -> p c t", t=T)[0:1, :, 0]).then_inc(ends_in, 16)
                sp.dma_start(draw[0:1, 1, :], raw_dst.rearrange("p (c t) -> p c t", t=T)[P - 1:P, :, T - 1]).then_inc(ends_in, 16)
            sp.wait_ge(both_ready, 1)
            sp.dma_start(dram.emb, both[:, :]).then_inc(both_out, 16)

        @block.gpsimd
        def _(pool):
            nc.gpsimd.iota(iedge[:, :], [[CH, NC]], 0, 0)
            nc.gpsimd.iota(iitem[:, :], [[1, ITEMS]], 0, 0).then_inc(iotas, 1)
            sort_adds(nc, pool, b)
            pool.wait_ge(emb_in, 64)
            pool.wait_ge(both_out, 16)
            for j in range(NT):
                nc.gpsimd.indirect_dma_start(
                    out=m.emb[:, j, :], out_offset=None, in_=dram.emb,
                    in_offset=bass.IndirectOffsetOnAxis(ap=ztype[:, j:j + 1], axis=0)).then_inc(emb_rows_in, 16)

        @block.tensor
        def _(pe):
            pe.wait_ge(emb_in, 64)
            nc.tensor.matmul(ps_emb[0:NTYPE, :], embT[:, :], adaptT[:, :], start=True, stop=True).then_inc(emb_mm, 1)
            sort_sums(nc, pe, m, b)
            one = m.ones[0:1, 0:1]
            for n, (to, left, right) in enumerate((
                    (ps_column[0:NT, 0:1], b.end[0:1, :], one), (ps_tiles[:, :], m.ones[0:NT, :], ended[0:NT, :]),
                    (ps_column[0:NC, 1:2], order[:, :], one), (ps_chunk[:, :], m.ones[0:NC, :], past[0:NC, :]))):
                pe.wait_ge(table_in, n + 1)
                nc.tensor.matmul(to, left, right, start=True, stop=True).then_inc(table_sum, 1)

        @block.scalar
        def _(act):
            act.wait_ge(angle, 1)
            nc.scalar.activation(m.cut[:, :], m.cut[:, :], ACT.Sin).then_inc(cut_ready, 1)
            square_root(nc, act, m, var_ready, std_ready, 1)

        @block.vector
        def _(dve):
            link = Chain(dve, dchain)
            dve.wait_ge(emb_mm, 1)
            nc.vector.tensor_copy(both[:, G:2 * G], ps_emb[0:NTYPE, :]).then_inc(both_ready, 1)
            nc.vector.tensor_copy(m.srcf[:, :], raw_src)
            link(nc.vector.tensor_copy(m.dstf[:, :], raw_dst))
            link(nc.vector.scalar_tensor_tensor(m.row1[:, :], m.dstf[:, :], float(NREL1), m.row1[:, :], ALU.mult, ALU.add))
            link(nc.vector.scalar_tensor_tensor(m.row2[:, :], m.srcf[:, :], float(NREL2), m.row2[:, :], ALU.mult, ALU.add))
            dve.wait_ge(ends_in, 32)
            nc.vector.tensor_scalar(m.dfirst[:, :], draw[0:1, 0, :], 7, None, ALU.arith_shift_right)
            link(nc.vector.tensor_scalar(m.dlast[:, :], draw[0:1, 1, :], 7, None, ALU.arith_shift_right))

            sort_places(nc, dve, link, b, raw_src, bucket_raw, m.place[:, :])

            link(nc.vector.scalar_tensor_tensor(angles, m.w[:, :], -1.0, m.w[:, :], ALU.mult, ALU.max))
            link(nc.vector.tensor_scalar(angles, angles, CUTOFF, None, ALU.min))
            nc.vector.tensor_scalar(m.cut[:, :], angles, -float(np.pi) / CUTOFF, HALFPI,
                                    ALU.mult, ALU.add).then_inc(angle, 1)
            link(nc.vector.tensor_scalar(inside, m.w[:, :], CUTOFF, 0.5, ALU.is_lt, ALU.mult))
            dve.wait_ge(cut_ready, 1)
            link(nc.vector.scalar_tensor_tensor(m.cut[:, :], m.cut[:, :], 1.0, inside, ALU.add, ALU.mult))

            dve.wait_ge(iotas, 1)
            nc.vector.tensor_copy(item[:, :], iitem[:, :])
            link(nc.vector.tensor_copy(edge0[:, :], iedge[:, :]))
            nc.vector.engine_nop().then_inc(table_in, 1)
            dve.wait_ge(table_sum, 1)
            link(nc.vector.tensor_copy(column[0:NT, 0:1], ps_column[0:NT, 0:1]))
            link(nc.vector.tensor_scalar(ended[0:NT, 0:NC], edge0[0:NT, :], column[0:NT, 0:1], None, ALU.is_ge))
            link(nc.vector.tensor_scalar(edge0[:, :], edge0[:, :], float(CH - 1), None, ALU.add))
            nc.vector.tensor_scalar(ended[0:NT, NC:2 * NC], edge0[0:NT, :], column[0:NT, 0:1], None,
                                    ALU.is_ge).then_inc(table_in, 1)
            dve.wait_ge(table_sum, 2)
            nc.vector.tensor_copy(m.sfirst[:, :], ps_tiles[0:1, 0:NC])
            nc.vector.tensor_copy(m.slast[:, :], ps_tiles[0:1, NC:2 * NC])
            nc.vector.tensor_tensor(order[:, :], ps_tiles[0:1, NC:2 * NC], item[0:1, 0:NC], ALU.add).then_inc(table_in, 1)
            dve.wait_ge(table_sum, 3)
            link(nc.vector.tensor_copy(column[0:NC, 1:2], ps_column[0:NC, 1:2]))
            nc.vector.tensor_scalar(past[0:NC, :], item[0:NC, :], column[0:NC, 1:2], None, ALU.is_gt).then_inc(table_in, 1)
            dve.wait_ge(table_sum, 4)
            nc.vector.tensor_copy(m.ichunk[:, :], ps_chunk[0:1, :])
            link(nc.vector.tensor_tensor(item[:, :], item[:, :], ps_chunk[:, :], ALU.subtract))
            nc.vector.tensor_copy(m.itile[:, :], item[0:1, :])
            link(nc.vector.tensor_scalar(m.ibase[:, :], item[:, :], float(P), None, ALU.mult))

            dve.wait_ge(x_in, 32)
            layer_norm(nc, dve, link, m, m.x[:, :, :], m.h[:, :, :],
                       m.work[:, 0:NT * H].rearrange("p (j f) -> p j f", f=H), var_ready, std_ready, 1)
            rows, rest = carve(m, [NT, TW], [NT, TW])
            link(nc.vector.tensor_tensor(rows[:, :, 0:H], m.h[:, :, :], wide48(m.mult[:, :]), ALU.mult))
            dve.wait_ge(emb_rows_in, 16 * NT)
            link(nc.vector.tensor_copy(rows[:, :, H:H + G], m.emb[:, :, G:2 * G]))
            link(nc.vector.tensor_copy(rows[:, :, H + G], m.mult[:, :]))
            split(nc, link, *(m.t0[:, :, a, 0:TW] for a in range(3)), rows, rest)
            parts = m.work[:, 0:NT * 3 * G // 2].bitcast(bf16).rearrange("p (j a f) -> p j a f", a=3, f=G)
            rest = rest[:, :, 0:G]
            split(nc, link, *(parts[:, :, a, :] for a in range(3)), m.emb[:, :, 0:G], rest)
            link(nc.vector.tensor_copy(m.emb3, parts.rearrange("p j a f -> p j (a f)")))


def layer0_edges(nc, ctx, m, ins, dram):
    attr, dr0, dr1, onehot, z, rec0, rec1 = carve(
        m, [4, 512], [CH], [CH], [CH // 2], [2, 512], [T, REC], [T, REC])
    onehot = onehot.bitcast(bf16)
    rec = (rec0, rec1)
    drow = (dr0.bitcast(i32), dr1.bitcast(i32))
    sb = lambda n, s, d=fp32: ctx.enter_context(nc.sbuf_tensor(n, s, d))
    place = (sb("place_a", [P, T], i32), sb("place_b", [P, T], i32))
    w1T, w2T, b1 = sb("w1T", [R, H]), sb("w2T", [H + 1, H]), sb("b1c", [H, 1])
    pb = lambda n, s: ctx.enter_context(nc.psum_tensor(n, s, fp32))
    rows_ps = pb("rows_ps", [P, T, P])
    gate_ps = pb("gate_ps", [P, T, 64])
    z_ps = pb("z_ps", [P, 2, 512])
    sem = lambda n: ctx.enter_context(nc.semaphore(n))
    weights_in = sem("weights_in")
    attr_in = [sem(f"attr_in{g}") for g in range(4)]
    drow_in = (sem("drow_in0"), sem("drow_in1"))
    tile_in = sem("tile_in")
    onehot_ready, onehot_free, chunk_items = sem("onehot_ready"), sem("onehot_free"), sem("chunk_items")
    rows_ready, rows_scaled, rows_copied = sem("rows_ready"), sem("rows_scaled"), sem("rows_copied")
    z_ready, silu_done, gate_ready, rec_ready, ones_set = (
        sem("z_ready"), sem("silu_done"), sem("gate_ready"), sem("rec_ready"), sem("ones_set"))
    scattered = (sem("scattered0"), sem("scattered1"))

    with nc.Block() as block:

        @block.sync
        def _(sp):
            sp.dma_start(w1T[:, :], ins.W1T).then_inc(weights_in, 16)
            sp.dma_start(w2T[:, :], ins.W2T).then_inc(weights_in, 16)
            sp.dma_start(b1[:, :], ins.b1).then_inc(weights_in, 16)
            laid = ins.attrT.rearrange("r (c g e) -> r c g e", g=4, e=512)
            found = dram.sorted.rearrange("(c p t) f -> f c t p", p=P, t=T)[0:R]

            def loads(dst_row, attributes):
                def chunk(c, u, s):
                    if not before(c, 2):
                        sp.wait_ge(chunk_items, c - 1)
                        sp.sem_inc(m.sp_turns, 1)
                    sp.dma_start(drow[s], dst_row.rearrange("(c e) -> c e", e=CH)[col(c), :]
                                 .to_broadcast([P, CH])).then_inc(drow_in[s], 16)
                    for g in range(4):
                        if not before(c, 1):
                            sp.wait_ge(z_ready, c * 4 + (g - 3))
                            sp.sem_inc(m.sp_turns, 1)
                        attributes(c, g)
                over_chunks(sp, chunk)

            unsorted = sp.value_load(m.unsorted[0:1, 0:1], min_val=0, max_val=1)
            def whole_quarter(c, g):
                sp.dma_start(attr[0:R, g, :], laid[:, col(c), g, :].rearrange("r c e -> r (c e)")).then_inc(attr_in[g], 16)

            def tile_by_tile(c, g):
                for t in range(4):
                    sp.dma_start(attr[0:R, g, t * P:(t + 1) * P],
                                 found[:, col(c), 4 * g + t, :].rearrange("r c p -> r (c p)")).then_inc(tile_in, 16)
                sp.wait_ge(tile_in, c * 256 + (g + 1) * 64)
                sp.sem_inc(attr_in[g], 16)

            with sp.If(unsorted), nc.allow_non_contiguous_dma(reason="the general path"):
                loads(dram.dst, tile_by_tile)
            with sp.Else():
                loads(ins.dst, whole_quarter)

        @block.tensor
        def _(pe):
            pe.wait_ge(weights_in, 48)
            pe.wait_ge(ones_set, 1)
            pe.sem_inc(onehot_free, 2)
            with pe.register("k_edges") as k:
                pe.reg_mov(k, 0)

                def chunk(c, u, s):
                    def hidden(g):
                        pe.wait_ge(attr_in[g], c * 16 + 16)
                        pe.sem_inc(m.pe_turns, 1)
                        if not (before(c, 1) and g < 2):
                            pe.wait_ge(silu_done, c * 4 + (g - 1))
                            pe.sem_inc(m.pe_turns, 1)
                        nc.tensor.matmul(z_ps[0:H, g % 2, :], w1T[:, :], attr[0:R, g, :],
                                         start=True, stop=True).then_inc(z_ready, 1)

                    def gates(g):
                        pe.wait_ge(silu_done, c * 4 + (g + 1))
                        if g == 0 and not before(c, 1):
                            pe.wait_ge(rec_ready, c)
                        for t in range(4):
                            last = nc.tensor.matmul(gate_ps[:, 4 * g + t, 0:H], z[0:H + 1, g % 2, t * P:(t + 1) * P],
                                                    w2T[:, :], start=True, stop=True)
                        if g == 3:
                            last.then_inc(gate_ready, 1)

                    hidden(0)
                    for g in range(1, 4):
                        hidden(g)
                        gates(g - 1)
                    gates(3)

                    if not before(c, 1):
                        pe.wait_ge(rows_copied, c)
                    for b in range(4):
                        nc.tensor.matmul(rows_ps[:, 4 * b:4 * b + 4, :].rearrange("p t f -> p (t f)"),
                                         m.zero[:, 0:P], m.zero[:, :], start=True, stop=False)

                    def item(k, j):
                        for half in (0, 1):
                            pe.wait_ge(onehot_ready, k * 2 + (half + 1))
                            for t in range(half * T // 2, (half + 1) * T // 2):
                                for a in range(3):
                                    last = nc.tensor.matmul(
                                        rows_ps[:, t, 0:TW], onehot[:, t * P:(t + 1) * P],
                                        m.t0[:, col(j), a, 0:TW].rearrange("p j f -> p (j f)"), start=False, stop=False)
                            last.then_inc(onehot_free, 1)
                    over_items(pe, k, m.dfirst, m.dlast, c, item)
                    for b in range(4):
                        last = nc.tensor.matmul(rows_ps[:, 4 * b:4 * b + 4, :].rearrange("p t f -> p (t f)"),
                                                m.zero[:, 0:P], m.zero[:, :], start=False, stop=True)
                    last.then_inc(rows_ready, 1)
                over_chunks(pe, chunk)

        @block.scalar
        def _(act):
            act.wait_ge(ones_set, 1)
            act.wait_ge(weights_in, 48)

            def chunk(c, u, s):
                for g in range(4):
                    act.wait_ge(z_ready, c * 4 + (g + 1))
                    nc.scalar.activation(z[0:H, g % 2, :], z_ps[0:H, g % 2, :], ACT.Silu, bias=b1[:, 0:1]).then_inc(silu_done, 1)
                if not before(u, 1):
                    act.wait_ge(scattered[s], u * (16 * T))
                act.wait_ge(rows_scaled, c + 1)
                nc.scalar.copy(rec[s][:, :, 2 * H:2 * H + G + 1], rows_ps[:, :, H:TW]).then_inc(rows_copied, 1)
            over_chunks(act, chunk)

        @block.vector
        def _(dve):
            nc.vector.memset(z[0:64, :, :], 1.0).then_inc(ones_set, 1)
            with dve.register("k_edges") as k:
                dve.reg_mov(k, 0)

                def chunk(c, u, s):
                    dve.wait_ge(drow_in[s], u * 16 + 16)

                    def item(k, j):
                        for half in (0, 1):
                            part = slice(half * CH // 2, (half + 1) * CH // 2)
                            dve.wait_ge(onehot_free, k * 2 + (half + 1))
                            nc.vector.tensor_scalar(onehot[:, part], drow[s][:, part], m.node[:, col(j)], None,
                                                    ALU.is_equal).then_inc(onehot_ready, 1)
                    over_items(dve, k, m.dfirst, m.dlast, c, item)
                    if not before(u, 1):
                        dve.wait_ge(scattered[s], u * (16 * T))
                    nc.vector.tensor_copy(place[s][:, :], m.place[:, cols(c)]).then_inc(chunk_items, 1)
                    nc.vector.tensor_copy(rec[s][:, :, SRC], m.srcf[:, cols(c)])
                    nc.vector.tensor_copy(rec[s][:, :, ROW1], m.row1[:, cols(c)])
                    nc.vector.tensor_copy(rec[s][:, :, WEIGHT], m.w[:, cols(c)])
                    dve.wait_ge(rows_ready, c + 1)
                    nc.vector.tensor_tensor(rec[s][:, :, H:2 * H], rows_ps[:, :, 0:H],
                                            m.cut[:, cols(c)].unsqueeze(2).to_broadcast([P, T, H]),
                                            ALU.mult).then_inc(rows_scaled, 1)
                    dve.wait_ge(gate_ready, c + 1)
                    dve.wait_ge(rows_scaled, c + 1)
                    nc.vector.tensor_tensor(rec[s][:, :, 0:H], gate_ps[:, :, 0:H], rec[s][:, :, H:2 * H],
                                            ALU.mult).then_inc(rec_ready, 1)
                over_chunks(dve, chunk)

        @block.gpsimd
        def _(pool):
            def chunk(c, u, s):
                pool.wait_ge(rec_ready, c + 1)
                pool.wait_ge(rows_copied, c + 1)
                pool.sem_inc(m.pool_turns, 1)
                for t in range(T):
                    nc.gpsimd.indirect_dma_start(
                        out=dram.rec, out_offset=bass.IndirectOffsetOnAxis(ap=place[s][:, t:t + 1], axis=0),
                        in_=rec[s][:, t, :], in_offset=None).then_inc(scattered[s], 16)
            over_chunks(pool, chunk)
            pool.wait_ge(scattered[0], 16 * T * ((NC + 1) // 2))
            pool.wait_ge(scattered[1], 16 * T * (NC // 2))


def layer0_sums(nc, ctx, m, dram):
    PART = H + 2
    r0, r1, r2, r3, o0, o1, o2, o3, t0, t1, a0, a1, m0, m1, d0, d1, p0, p1 = carve(
        m, *[[T, REC]] * 4, *[[T * P // 2]] * 6, *[[T, H]] * 2, *[[T, H + 1]] * 4, *[[T * 3 * PART // 2]] * 2,
        all_of_it=True)
    tiles = lambda a: a.bitcast(bf16).rearrange("p (t n) -> p t n", n=P)
    rec, onehot, onehotT = (r0, r1, r2, r3), [tiles(a) for a in (o0, o1, o2, o3)], [tiles(a) for a in (t0, t1)]
    scaled, msg, rest = (a0, a1), (m0, m1), (d0, d1)
    parts = [a.bitcast(bf16).rearrange("p (t a f) -> p t a f", a=3, f=PART) for a in (p0, p1)]
    prod = [a.rearrange("p a b -> p (a b)")[:, 0:T * G].rearrange("p (a b) -> p a b", b=G) for a in scaled]
    s_src, s_row1, s_w = m.in_src_order()
    sb = lambda n, s, d=fp32: ctx.enter_context(nc.sbuf_tensor(n, s, d))
    local, adapt, total = sb("local", [P, 2, T]), sb("adapt", [P, 2, T]), sb("total", [P, PART])
    pb = lambda n, s, d=fp32: ctx.enter_context(nc.psum_tensor(n, s, d))
    tr_ps, emb_ps, sum_ps = pb("tr_ps", [P, 2, T, P], bf16), pb("emb_ps", [P, 2, T, G]), pb("sum_ps", [P, 2, 512])
    sem = lambda n: ctx.enter_context(nc.semaphore(n))
    rec_in = [sem(f"rec_in{i}") for i in range(4)]
    ones_set, local_ready, onehot_ready, tr_ready, tr_copied, kept, emb_ready = (
        sem("c_ones"), sem("c_local"), sem("c_onehot"), sem("c_tr"), sem("c_copied"), sem("c_kept"), sem("c_emb"))
    prod_ready, adapt_ready, scaled_ready, msg_ready, sum_ready, total_ready, acc_done = (
        sem("c_prod"), sem("c_adapt"), sem("c_scaled"), sem("c_msg"), sem("c_sum"), sem("c_total"), sem("c_acc"))
    hi_ready, rest_ready, mid_ready, lo_ready = sem("c_hi"), sem("c_rest"), sem("c_mid"), sem("c_lo")
    RING = 4
    HALF = (slice(0, T // 2), slice(T // 2, T))

    with nc.Block() as block:

        @block.sync
        def _(sp):
            def item(k, u, s):
                c = sp.value_load(m.ichunk[0:1, col(k)], min_val=0, max_val=NC - 1)
                if not before(k, 4):
                    sp.wait_ge(msg_ready, k * 2 - 6)
                    sp.sem_inc(m.sp_turns, 1)
                    sp.wait_ge(kept, k * 3 - 9)
                    sp.sem_inc(m.sp_turns, 1)
                sp.dma_start(rec[s % RING].rearrange("p t f -> p (t f)"),
                             dram.rec.rearrange("(c p t) f -> p c (t f)", p=P, t=T)[:, col(c), :]
                             .rearrange("p c f -> p (c f)")).then_inc(rec_in[s % RING], 16)
            over_steps(sp, ITEMS, RING, item)

        def arrived(eng, k, u, s):
            eng.wait_ge(rec_in[s % RING], u * 16 + 16)

        @block.vector
        def _(dve):
            for a in parts:
                nc.vector.memset(a[:, :, 1:3, PART - 1], 0.0)
                nc.vector.memset(a[:, :, 0, PART - 1], 1.0)
            nc.vector.memset(m.acc[:, :, :], 0.0).then_inc(acc_done, 1)
            nc.vector.engine_nop().then_inc(ones_set, 1)

            def build(k, u, s):
                arrived(dve, k, u, s)
                nc.vector.tensor_scalar(local[:, s % 2, :], rec[s % RING][:, :, SRC], m.ibase[:, col(k)], None,
                                        ALU.subtract).then_inc(local_ready, 1)
                dve.wait_ge(local_ready, k + 1)
                if not before(k, 4):
                    dve.wait_ge(sum_ready, k - 3)
                for g in (0, 1):
                    nc.vector.tensor_tensor(onehot[s % RING][:, HALF[g], :],
                                            m.iota_bf[:, :].unsqueeze(1).to_broadcast([P, T // 2, P]),
                                            local[:, s % 2, HALF[g]].unsqueeze(2).to_broadcast([P, T // 2, P]),
                                            ALU.is_equal).then_inc(onehot_ready, 1)

            def adapted(k, s):
                r = rec[s % RING]
                dve.wait_ge(emb_ready, k + 1)
                if not before(k, 2):
                    dve.wait_ge(msg_ready, k * 2 - 2)
                nc.vector.tensor_tensor(prod[s % 2], emb_ps[:, s % 2, :, :], r[:, :, 2 * H:2 * H + G],
                                        ALU.mult).then_inc(prod_ready, 1)
                dve.wait_ge(prod_ready, k + 1)
                nc.vector.reduce_sum(adapt[:, s % 2, :], prod[s % 2], AX.X).then_inc(adapt_ready, 1)

            def low_part(k, s):
                dve.wait_ge(mid_ready, k + 1)
                nc.vector.tensor_tensor(parts[s % 2][:, :, 2, 0:H + 1], rest[s % 2], parts[s % 2][:, :, 1, 0:H + 1],
                                        ALU.subtract).then_inc(lo_ready, 1)

            def add_up(k, s, j):
                dve.wait_ge(sum_ready, k + 1)
                dve.wait_ge(acc_done, k + 1)
                nc.vector.reduce_sum(total[:, :], sum_ps[:, s % 2, 0:3 * PART].rearrange("p (a f) -> p f a", f=PART),
                                     AX.X).then_inc(total_ready, 1)
                dve.wait_ge(total_ready, k + 1)
                acc = m.acc[:, col(j), :].rearrange("p j f -> p (j f)")
                nc.vector.tensor_tensor(acc, acc, total[:, :], ALU.add).then_inc(acc_done, 1)

            def item_tile(k):
                return dve.value_load(m.itile[0:1, col(k)], min_val=0, max_val=NT - 1)

            def item(k, u, s):
                if not before(k, 3):
                    low_part(k - 3, s + 1)
                build(k, u, s)
                if not before(k, 3):
                    j = item_tile(k - 3)
                if not before(k, 1):
                    adapted(k - 1, s + 3)
                if not before(k, 3):
                    add_up(k - 3, s + 1, j)
            over_steps(dve, ITEMS, RING, item)
            end = ITEMS % RING
            adapted(ITEMS - 1, end + 3)
            for k in (3, 2, 1):
                low_part(ITEMS - k, end + 4 - k)
            for k in (3, 2, 1):
                add_up(ITEMS - k, end + 4 - k, item_tile(ITEMS - k))

        @block.gpsimd
        def _(pool):
            pool.wait_ge(ones_set, 1)

            def message(k, s):
                r = rec[s % RING]
                if not before(k, 2):
                    pool.wait_ge(rest_ready, k - 1)
                pool.wait_ge(adapt_ready, k + 1)
                nc.gpsimd.tensor_tensor(scaled[s % 2], r[:, :, H:2 * H],
                                        adapt[:, s % 2, :].unsqueeze(2).to_broadcast([P, T, H]),
                                        ALU.mult).then_inc(scaled_ready, 1)
                nc.gpsimd.tensor_copy(msg[s % 2][:, :, H], r[:, :, 2 * H + G]).then_inc(msg_ready, 1)
                pool.wait_ge(scaled_ready, k + 1)
                nc.gpsimd.tensor_tensor(msg[s % 2][:, :, 0:H], scaled[s % 2], r[:, :, 0:H],
                                        ALU.add).then_inc(msg_ready, 1)

            def rest_of(k, s):
                pool.wait_ge(hi_ready, k + 1)
                if not before(k, 2):
                    pool.wait_ge(lo_ready, k - 1)
                nc.gpsimd.tensor_tensor(rest[s % 2], msg[s % 2], parts[s % 2][:, :, 0, 0:H + 1],
                                        ALU.subtract).then_inc(rest_ready, 1)

            def item(k, u, s):
                if not before(k, 1):
                    rest_of(k - 1, s + 3)
                message(k, s)
            over_steps(pool, ITEMS, RING, item)
            rest_of(ITEMS - 1, ITEMS % RING + 3)

        @block.scalar
        def _(act):
            act.wait_ge(ones_set, 1)

            def high_part(k, s):
                act.wait_ge(msg_ready, k * 2 + 2)
                if not before(k, 2):
                    act.wait_ge(sum_ready, k - 1)
                nc.scalar.copy(parts[s % 2][:, :, 0, 0:H + 1], msg[s % 2]).then_inc(hi_ready, 1)

            def middle_part(k, s):
                act.wait_ge(rest_ready, k + 1)
                nc.scalar.copy(parts[s % 2][:, :, 1, 0:H + 1], rest[s % 2]).then_inc(mid_ready, 1)

            def item(k, u, s):
                c = act.value_load(m.ichunk[0:1, col(k)], min_val=0, max_val=NC - 1)
                arrived(act, k, u, s)
                if not before(k, 1):
                    act.wait_ge(kept, k * 3)
                for to, field in ((s_src, SRC), (s_row1, ROW1), (s_w, WEIGHT)):
                    nc.scalar.copy(to[:, cols(c)], rec[s % RING][:, :, field]).then_inc(kept, 1)
                for g in (0, 1):
                    act.wait_ge(tr_ready, k * 2 + (g + 1))
                    if g == 0 and not before(k, 2):
                        act.wait_ge(emb_ready, k - 1)
                    nc.scalar.copy(onehotT[s % 2][:, HALF[g], :], tr_ps[:, s % 2, HALF[g], :]).then_inc(tr_copied, 1)
                    if g == 0 and not before(k, 2):
                        middle_part(k - 2, s + 2)
                if not before(k, 1):
                    high_part(k - 1, s + 3)
            over_steps(act, ITEMS, RING, item)
            end = ITEMS % RING
            middle_part(ITEMS - 2, end + 2)
            high_part(ITEMS - 1, end + 3)
            middle_part(ITEMS - 1, end + 3)

        @block.tensor
        def _(pe):
            def sums(k, s):
                pe.wait_ge(lo_ready, k + 1)
                if not before(k, 2):
                    pe.wait_ge(acc_done, k)
                for t in range(T):
                    last = nc.tensor.matmul(sum_ps[:, s % 2, 0:3 * PART], onehot[s % RING][:, t, :],
                                            parts[s % 2][:, t, :, :].rearrange("p a f -> p (a f)"),
                                            start=(t == 0), stop=(t == T - 1))
                last.then_inc(sum_ready, 1)

            def item(k, u, s):
                if not before(k, 3):
                    sums(k - 3, s + 1)
                for g in (0, 1):
                    pe.wait_ge(onehot_ready, k * 2 + (g + 1))
                    if not before(k, 2):
                        pe.wait_ge(tr_copied, k * 2 + (g - 3))
                    for t in range(T)[HALF[g]]:
                        last = nc.tensor.transpose(tr_ps[:, s % 2, t, :], onehot[s % RING][:, t, :], m.ident_bf[:, :])
                    last.then_inc(tr_ready, 1)
                j = pe.value_load(m.itile[0:1, col(k)], min_val=0, max_val=NT - 1)
                if not before(k, 2):
                    pe.wait_ge(prod_ready, k - 1)
                for g in (0, 1):
                    pe.wait_ge(tr_copied, k * 2 + (g + 1))
                    for t in range(T)[HALF[g]]:
                        for a in range(3):
                            last = nc.tensor.matmul(emb_ps[:, s % 2, t, :], onehotT[s % 2][:, t, :],
                                                    m.emb3[:, col(j), a * G:(a + 1) * G].rearrange("p j f -> p (j f)"),
                                                    start=(a == 0), stop=(a == 2))
                last.then_inc(emb_ready, 1)
            over_steps(pe, ITEMS, RING, item)
            for k in (3, 2, 1):
                sums(ITEMS - k, ITEMS % RING + 4 - k)


RING = 4


def tile_of(a, j):
    return a[:, col(j), :].rearrange("p j f -> p (j f)")


def finished_tiles(eng, done, last, step):
    lo = eng.snap(done, min_val=0, max_val=NT - 1)
    with eng.If(lo < last):
        with eng.Fori(lo, last) as v:
            step(eng.snap(v, min_val=0, max_val=NT - 2))
        eng.reg_mov(done, last)


def tile_norm(nc, dve, link, m, j, h, var_ready, std_ready):
    x, square = tile_of(m.x, j), m.square[:, :]
    mean, var, std = (m.stat[:, i, col(j)] for i in (0, 1, 2))
    link(nc.vector.reduce_sum(mean, x, AX.X))
    link(nc.vector.tensor_scalar(mean, mean, -1.0 / H, None, ALU.mult))
    link(nc.vector.tensor_scalar(h, x, mean, None, ALU.add))
    link(nc.vector.tensor_tensor(square, h, h, ALU.mult))
    link(nc.vector.reduce_sum(var, square, AX.X))
    nc.vector.tensor_scalar(var, var, 1.0 / H, EPS, ALU.mult, ALU.add).then_inc(var_ready, 1)
    dve.wait_ge(std_ready, j + 1)
    link(nc.vector.reciprocal(var, std))
    return nc.vector.tensor_scalar(h, h, var, 0.0, ALU.mult, ALU.max)


def tile_root(nc, act, m, j, var_ready, std_ready):
    act.wait_ge(var_ready, j + 1)
    nc.scalar.activation(m.stat[:, 2, col(j)], m.stat[:, 1, col(j)], ACT.Sqrt).then_inc(std_ready, 1)


def gather_sums(nc, ctx, m, name, table, rows, weight, key, first, last_tile, nodes):
    *got, onehot, rest = carve(m, *[[T, H]] * RING, [T, P], [WORK - RING * T * H - T * P])
    node = nodes(nc, ctx, m, rest)
    sb = lambda n, s, d=fp32: ctx.enter_context(nc.sbuf_tensor(name + n, s, d))
    row = [sb(f"row{i}", [P, T], i32) for i in range(RING)]
    local = sb("local", [P, T])
    sum_ps = ctx.enter_context(nc.psum_tensor(name + "sum_ps", [P, H], fp32))
    sem = lambda n: ctx.enter_context(nc.semaphore(name + n))
    gathered = [sem(f"gathered{i}") for i in range(RING)]
    row_ready, got_used, onehot_ready, onehot_free, acc_done, dchain, weight_ready = (
        sem("row_ready"), sem("got_used"), sem("onehot"), sem("free"), sem("acc"), sem("chain"), sem("weight_ready"))
    now = sb("now", [P, 2, T])

    with nc.Block() as block:

        @block.sync
        def _(sp):
            node.sync(sp)

        @block.scalar
        def _(act):
            node.scalar_begins(act)
            done = ctx.enter_context(act.register(name + "act_done"))
            act.reg_mov(done, 0)

            def finished(c):
                last = act.value_load(last_tile[0:1, col(c)], min_val=0, max_val=NT - 1)
                finished_tiles(act, done, last, lambda j: node.scalar(act, j))

            def chunk(c, u, s):
                if not before(u, 1):
                    act.wait_ge(gathered[s], u * (16 * T))
                nc.scalar.copy(row[s][:, :], rows[:, cols(c)]).then_inc(row_ready, 1)
                if not before(c, RING):
                    finished(c - RING)
            over_chunks(act, chunk, RING)
            for c in range(NC - RING, NC):
                finished(c)
            node.scalar(act, NT - 1)

        @block.gpsimd
        def _(pool):
            def chunk(c, u, s):
                pool.wait_ge(row_ready, c + 1)
                if not before(c, RING):
                    pool.wait_ge(got_used, c - (RING - 2))
                pool.sem_inc(m.pool_turns, 1)
                for t in range(T):
                    nc.gpsimd.indirect_dma_start(
                        out=got[s][:, t, :], out_offset=None, in_=table,
                        in_offset=bass.IndirectOffsetOnAxis(ap=row[s][:, t:t + 1], axis=0)).then_inc(gathered[s], 16)
            over_chunks(pool, chunk, RING)

        @block.vector
        def _(dve):
            nc.vector.memset(m.acc[:, :, :], 0.0).then_inc(acc_done, 1)
            node.vector_begins(dve)
            with (dve.register(name + "k") as k, dve.register(name + "dve_done") as done,
                  dve.register(name + "dve_last") as last, dve.register(name + "dve_tile") as tile):
                for r in (k, done, last, tile):
                    dve.reg_mov(r, 0)

                def add_up(k):
                    j = dve.snap(tile, min_val=0, max_val=NT - 1)
                    dve.wait_ge(onehot_free, k * 4 + 4)
                    dve.wait_ge(acc_done, k + 1)
                    acc = tile_of(m.acc[:, :, 0:H], j)
                    nc.vector.tensor_tensor(acc, acc, sum_ps[:, :], ALU.add).then_inc(acc_done, 1)

                def chunk(c, u, s):
                    nc.vector.tensor_copy(now[:, s % 2, :], weight[:, cols(c)]).then_inc(weight_ready, 1)
                    dve.wait_ge(weight_ready, c + 1)
                    dve.wait_ge(gathered[s], u * (16 * T) + 16 * T)
                    dve.sem_inc(m.dve_turns, 1)

                    def item(k, j):
                        nc.vector.tensor_scalar(local[:, :], key[:, cols(c)], m.base[:, bass.ds(j, 1)], None,
                                                ALU.subtract).then_inc(dchain, 1)
                        dve.wait_ge(dchain, k + 1)
                        for g in range(4):
                            if g == 3:
                                add_up(k)
                            dve.wait_ge(onehot_free, k * 4 + (g + 1))
                            for t in range(g * T // 4, (g + 1) * T // 4):
                                last = nc.vector.tensor_scalar(onehot[:, t, :], m.iota[:, :], local[:, t:t + 1],
                                                               now[:, s % 2, t:t + 1], ALU.is_equal, ALU.mult)
                            last.then_inc(onehot_ready, 1)
                        dve.wait_ge(onehot_ready, k * 4 + 4)
                        dve.sem_inc(m.dve_turns, 1)
                        dve.reg_mov(tile, j)
                    hi = over_items(dve, k, first, last_tile, c, item)
                    dve.wait_ge(acc_done, dve.snap(k, min_val=1, max_val=NC + NT) + 1)
                    dve.sem_inc(m.dve_turns, 1)
                    nc.vector.engine_nop().then_inc(got_used, 1)
                    finished_tiles(dve, done, dve.snap(last, min_val=0, max_val=NT - 1), lambda j: node.vector(dve, j))
                    dve.reg_mov(last, hi)
                over_chunks(dve, chunk, RING)
                add_up(dve.snap(k, min_val=1, max_val=NC + NT))
                dve.wait_ge(acc_done, dve.snap(k, min_val=1, max_val=NC + NT) + 2)
                dve.sem_inc(m.dve_turns, 1)
                finished_tiles(dve, done, dve.snap(last, min_val=0, max_val=NT - 1), lambda j: node.vector(dve, j))
                node.vector(dve, NT - 1)

        @block.tensor
        def _(pe):
            if node.tensor:
                node.tensor_begins(pe)
            for g in range(4):
                nc.tensor.matmul(sum_ps[:, :], m.zero[:, 0:P], m.zero[:, 0:H], start=True, stop=True).then_inc(onehot_free, 1)
            with (pe.register(name + "k") as k, pe.register(name + "pe_done") as done,
                  pe.register(name + "pe_last") as last):
                for r in (k, done, last):
                    pe.reg_mov(r, 0)

                def chunk(c, u, s):
                    def item(k, j):
                        pe.wait_ge(acc_done, k + 2)
                        for g in range(4):
                            pe.wait_ge(onehot_ready, k * 4 + (g + 1))
                            for t in range(g * T // 4, (g + 1) * T // 4):
                                mm = nc.tensor.matmul(sum_ps[:, :], onehot[:, t, :], got[s][:, t, :],
                                                      start=(t == 0), stop=(t == T - 1))
                            mm.then_inc(onehot_free, 1)
                    hi = over_items(pe, k, first, last_tile, c, item)
                    if node.tensor:
                        finished_tiles(pe, done, pe.snap(last, min_val=0, max_val=NT - 1), lambda j: node.tensor(pe, j))
                        pe.reg_mov(last, hi)
                over_chunks(pe, chunk, RING)
                if node.tensor:
                    finished_tiles(pe, done, pe.snap(last, min_val=0, max_val=NT - 1), lambda j: node.tensor(pe, j))
                    node.tensor(pe, NT - 1)


GN = 7
NG = NT // GN
assert NG * GN == NT


def node_layer1(nc, ctx, m, ins, dram):
    scratch, hT, y = carve(m, [NT, H], [GN, P], [GN, NREL1 * H])
    sb = lambda n, s, d=fp32: ctx.enter_context(nc.sbuf_tensor(n, s, d))
    gamma, beta, w = sb("gamma", [P, H]), sb("beta", [P, H]), sb("w_rel", [H, NREL1 * H])
    pb = lambda n, s: ctx.enter_context(nc.psum_tensor(n, s, fp32))
    hT_ps, y_ps = pb("hT_ps", [P, 8, P]), pb("y_ps", [P, 8, 256])
    sem = lambda n: ctx.enter_context(nc.semaphore(n))
    in_sem, var_ready, std_ready, dchain, h_ready = sem("n1_in"), sem("n1_var"), sem("n1_std"), sem("n1_chain"), sem("n1_h")
    tr_ready, tr_copied, y_ready, y_copied, y_out = sem("n1_tr"), sem("n1_trc"), sem("n1_y"), sem("n1_yc"), sem("n1_out")
    wide = lambda a: a.unsqueeze(2).to_broadcast([P, NT, H])

    with nc.Block() as block:

        @block.sync
        def _(sp):
            sp.dma_start(gamma[:, :], ins.gamma.to_broadcast([P, H])).then_inc(in_sem, 16)
            sp.dma_start(beta[:, :], ins.beta.to_broadcast([P, H])).then_inc(in_sem, 16)
            sp.dma_start(w[:, :].rearrange("i (r o) -> i r o", o=H), ins.W.rearrange("(r i) o -> i r o", i=H)).then_inc(in_sem, 16)
            for q in range(NG):
                sp.wait_ge(y_copied, q + 1)
                sp.dma_start(dram.tab1.rearrange("(j p r) f -> p j (r f)", p=P, r=NREL1)[:, q * GN:(q + 1) * GN, :],
                             y).then_inc(y_out, 16)
            sp.wait_ge(y_out, 16 * NG)

        @block.scalar
        def _(act):
            for n in (1, 2, 3):
                square_root(nc, act, m, var_ready, std_ready, n)

        @block.vector
        def _(dve):
            link = Chain(dve, dchain)
            total, count = m.stat[:, 3, :], m.stat[:, 1, :]
            dve.wait_ge(in_sem, 48)
            link(nc.vector.tensor_scalar(total, m.acc[:, :, H], 1e-8, None, ALU.max))
            link(nc.vector.reciprocal(total, total))
            link(nc.vector.tensor_tensor(m.acc[:, :, 0:H], m.acc[:, :, 0:H], wide(total), ALU.mult))
            link(nc.vector.tensor_tensor(m.acc[:, :, 0:H], m.acc[:, :, 0:H], m.h[:, :, :], ALU.add))
            layer_norm(nc, dve, link, m, m.acc[:, :, 0:H], m.h[:, :, :], scratch, var_ready, std_ready, 1,
                       gamma[:, :], beta[:, :])
            link(nc.vector.tensor_tensor(m.x[:, :, :], m.x[:, :, :], m.h[:, :, :], ALU.add))
            nc.vector.tensor_scalar(count, m.acc[:, :, H + 1], 1.0, None, ALU.max).then_inc(var_ready, 1)
            dve.wait_ge(std_ready, 2)
            link(nc.vector.reciprocal(m.rdeg[:, :], m.stat[:, 2, :]))
            layer_norm(nc, dve, link, m, m.x[:, :, :], m.h[:, :, :], scratch, var_ready, std_ready, 3)
            nc.vector.engine_nop().then_inc(h_ready, 1)
            for q in range(NG):
                dve.wait_ge(tr_ready, q + 1)
                nc.vector.tensor_copy(hT[0:H, :, :], hT_ps[0:H, 0:GN, :]).then_inc(tr_copied, 1)
                dve.wait_ge(y_ready, q + 1)
                if q:
                    dve.wait_ge(y_out, 16 * q)
                nc.vector.tensor_copy(y, y_ps[:, 0:GN, 0:NREL1 * H]).then_inc(y_copied, 1)

        @block.tensor
        def _(pe):
            pe.wait_ge(h_ready, 1)
            for q in range(NG):
                for t in range(GN):
                    last = nc.tensor.transpose(hT_ps[0:H, t, :], m.h[:, q * GN + t, :], m.ident[:, :])
                last.then_inc(tr_ready, 1)
                pe.wait_ge(tr_copied, q + 1)
                if q:
                    pe.wait_ge(y_copied, q)
                for t in range(GN):
                    last = nc.tensor.matmul(y_ps[:, t, 0:NREL1 * H], hT[0:H, t, :], w[:, :], start=True, stop=True)
                last.then_inc(y_ready, 1)


class Node:

    tensor = None


def layer2_table(ins, dram):
    def nodes(nc, ctx, m, work):
        NPAIR = NREL2 // 2
        hT, mid, y = work[:, 0:P], work[:, P:5 * P], work[:, 5 * P:5 * P + NREL2 * H]
        h = work[:, 5 * P + NREL2 * H:5 * P + NREL2 * H + H]
        sb = lambda n, s, d=fp32: ctx.enter_context(nc.sbuf_tensor(n, s, d))
        bias = sb("n2_bias", [P, H])
        wa, wb, ba = sb("wa", [H, NREL2 * H]), sb("wb", [2 * H, NPAIR, 2 * H]), sb("ba", [2 * H, 1])
        pb = lambda n: ctx.enter_context(nc.psum_tensor(n, [P, 512], fp32))
        hT_ps, mid_ps, y_ps = pb("n2_hT_ps"), pb("mid_ps"), pb("n2_y_ps")
        sem = lambda n: ctx.enter_context(nc.semaphore(n))
        in_sem, z_ready, var_ready, std_ready, dchain, h_ready = (
            sem("n2_in"), sem("n2_zero"), sem("n2_var"), sem("n2_std"), sem("n2_chain"), sem("n2_h"))
        tr_ready, tr_copied, mid_ready, mid_done, y_ready = (
            sem("n2_tr"), sem("n2_trc"), sem("n2_mid"), sem("n2_midc"), sem("n2_y"))
        y_moved, y_free = sem("n2_moved"), sem("n2_free")
        node = Node()

        def sync(sp):
            sp.dma_start(bias[:, :], ins.b.to_broadcast([P, H])).then_inc(y_free, 16)
            sp.wait_ge(z_ready, 1)
            sp.dma_start(wa[:, :].rearrange("i (r o) -> i r o", o=H), ins.weight1.rearrange("r i o -> i r o")).then_inc(in_sem, 16)
            for a in (0, 1):
                sp.dma_start(wb[a * H:(a + 1) * H, :, a * H:(a + 1) * H],
                             ins.weight2.rearrange("(q a) i o -> a i q o", a=2)[a]).then_inc(in_sem, 16)
                sp.dma_start(ba[a * H:(a + 1) * H, :], ins.bias1).then_inc(in_sem, 16)
            with sp.Fori(0, NT) as v:
                j = sp.snap(v, min_val=0, max_val=NT - 1)
                sp.wait_ge(y_moved, j + 2)
                sp.sem_inc(m.sp_turns, 1)
                sp.dma_start(tile_of(dram.tab2.rearrange("(j p r) f -> p j (r f)", p=P, r=NREL2), j), y).then_inc(y_free, 16)
            sp.wait_ge(y_free, 16 * NT + 16)

        def scalar_begins(act):
            act.wait_ge(in_sem, 80)
            act.sem_inc(tr_copied, 1)
            act.sem_inc(y_moved, 1)

        def scalar(act, j):
            tile_root(nc, act, m, j, var_ready, std_ready)
            act.wait_ge(tr_ready, j + 1)
            nc.scalar.copy(hT[0:H, :], hT_ps[0:H, 0:P]).then_inc(tr_copied, 1)
            act.wait_ge(mid_ready, j + 1)
            nc.scalar.activation(mid[0:2 * H, :], mid_ps[0:2 * H, :], ACT.Relu, bias=ba[:, 0:1]).then_inc(mid_done, 1)
            act.wait_ge(y_ready, j + 1)
            act.wait_ge(y_free, j * 16 + 16)
            nc.scalar.copy(y, y_ps[:, 0:NREL2 * H]).then_inc(y_moved, 1)

        def vector_begins(dve):
            nc.vector.memset(wb[:, :, :], 0.0).then_inc(z_ready, 1)
            dve.wait_ge(in_sem, 80)
            dve.wait_ge(y_free, 16)

        def vector(dve, j):
            link = Chain(dve, dchain, j * 8)
            link(nc.vector.tensor_tensor(tile_of(m.x, j), tile_of(m.x, j), tile_of(m.acc[:, :, 0:H], j), ALU.add))
            link(nc.vector.tensor_tensor(tile_of(m.x, j), tile_of(m.x, j), bias[:, :], ALU.add))
            dve.wait_ge(tr_copied, j + 1)
            tile_norm(nc, dve, link, m, j, h, var_ready, std_ready).then_inc(h_ready, 1)
            assert link.n == 8

        def tensor_begins(pe):
            pe.wait_ge(in_sem, 80)

        def tensor(pe, j):
            pe.wait_ge(h_ready, j + 1)
            pe.sem_inc(m.pe_turns, 1)
            nc.tensor.transpose(hT_ps[0:H, 0:P], h, m.ident[:, :]).then_inc(tr_ready, 1)
            pe.wait_ge(tr_copied, j + 2)
            for r in range(NPAIR):
                last = nc.tensor.matmul(mid_ps[0:2 * H, r * P:(r + 1) * P], wa[:, 2 * H * r:2 * H * (r + 1)], hT[0:H, :],
                                        start=True, stop=True)
            last.then_inc(mid_ready, 1)
            pe.wait_ge(mid_done, j + 1)
            pe.wait_ge(y_moved, j + 1)
            for r in range(NPAIR):
                last = nc.tensor.matmul(y_ps[:, 2 * H * r:2 * H * (r + 1)], mid[0:2 * H, r * P:(r + 1) * P], wb[:, r, :],
                                        start=True, stop=True)
            last.then_inc(y_ready, 1)

        node.sync, node.scalar_begins, node.scalar = sync, scalar_begins, scalar
        node.vector_begins, node.vector, node.tensor_begins, node.tensor = vector_begins, vector, tensor_begins, tensor
        return node
    return nodes


def layer3_table(ins, dram):
    def nodes(nc, ctx, m, work):
        bias = ctx.enter_context(nc.sbuf_tensor("n3_bias", [P, H], fp32))
        sem = lambda n: ctx.enter_context(nc.semaphore(n))
        in_sem, var_ready, std_ready, dchain, tab_out, h_ready = (
            sem("n3_in"), sem("n3_var"), sem("n3_std"), sem("n3_chain"), sem("n3_out"), sem("n3_h"))
        node = Node()

        def sync(sp):
            sp.dma_start(bias[:, :], ins.bias2.to_broadcast([P, H])).then_inc(in_sem, 16)
            with sp.Fori(0, NT) as v:
                j = sp.snap(v, min_val=0, max_val=NT - 1)
                sp.wait_ge(h_ready, j + 1)
                sp.sem_inc(m.sp_turns, 1)
                sp.dma_start(tile_of(dram.tab3.rearrange("(j p) f -> p j f", p=P), j), tile_of(m.h, j)).then_inc(tab_out, 16)
            sp.wait_ge(tab_out, 16 * NT)

        def scalar_begins(act):
            pass

        def scalar(act, j):
            tile_root(nc, act, m, j, var_ready, std_ready)

        def vector_begins(dve):
            dve.wait_ge(in_sem, 16)

        def vector(dve, j):
            link = Chain(dve, dchain, j * 10)
            sums = tile_of(m.acc[:, :, 0:H], j)
            link(nc.vector.tensor_tensor(sums, sums, bias[:, :], ALU.add))
            link(nc.vector.tensor_scalar(sums, sums, 0.0, None, ALU.max))
            link(nc.vector.tensor_tensor(tile_of(m.x, j), tile_of(m.x, j), sums, ALU.add))
            link(tile_norm(nc, dve, link, m, j, tile_of(m.h, j), var_ready, std_ready))
            assert link.n == 10
            nc.vector.tensor_scalar(tile_of(m.h, j), tile_of(m.h, j), m.rdeg[:, col(j)], None, ALU.mult).then_inc(h_ready, 1)

        node.sync, node.scalar_begins, node.scalar = sync, scalar_begins, scalar
        node.vector_begins, node.vector = vector_begins, vector
        return node
    return nodes


def result(out):
    def nodes(nc, ctx, m, work):
        sem = lambda n: ctx.enter_context(nc.semaphore(n))
        dchain, x_ready, stored = sem("f_chain"), sem("f_ready"), sem("stored")
        node = Node()

        def sync(sp):
            with sp.Fori(0, NT) as v:
                j = sp.snap(v, min_val=0, max_val=NT - 1)
                sp.wait_ge(x_ready, j + 1)
                sp.sem_inc(m.sp_turns, 1)
                sp.dma_start(tile_of(out.rearrange("(j p) f -> p j f", p=P), j), tile_of(m.x, j)).then_inc(stored, 16)
            sp.wait_ge(stored, 16 * NT)

        def nothing(eng, j=None):
            pass

        def vector(dve, j):
            link = Chain(dve, dchain, j)
            sums = tile_of(m.acc[:, :, 0:H], j)
            link(nc.vector.tensor_scalar(sums, sums, m.rdeg[:, col(j)], None, ALU.mult))
            nc.vector.tensor_tensor(tile_of(m.x, j), tile_of(m.x, j), sums, ALU.add).then_inc(x_ready, 1)

        node.sync, node.scalar_begins, node.scalar, node.vector_begins, node.vector = (
            sync, nothing, nothing, nothing, vector)
        return node
    return nodes


def gnn(nc, ins, out):
    dram = Memory()
    dram.emb = nc.dram_tensor("emb_both", [NTYPE, 2 * G], fp32).ap()
    dram.sorted = nc.dram_tensor("sorted_edges", [EP, SORTED], fp32).ap()
    dram.dst = nc.dram_tensor("sorted_dst", [EP], i32).ap()
    dram.rec = nc.dram_tensor("records", [EP, REC], fp32).ap()
    dram.tab1 = nc.dram_tensor("table1", [NP * NREL1, H], fp32).ap()
    dram.tab2 = nc.dram_tensor("table2", [NP * NREL2, H], fp32).ap()
    dram.tab3 = nc.dram_tensor("table3", [NP, H], fp32).ap()
    with ExitStack() as whole:
        m = allocate(nc, whole)
        with ExitStack() as ctx:
            load(nc, ctx, m, ins, dram)
        with ExitStack() as ctx:
            reorder(nc, ctx, m, ins, dram)
        with ExitStack() as ctx:
            setup(nc, ctx, m, ins, dram)
        with ExitStack() as ctx:
            layer0_edges(nc, ctx, m, ins, dram)
        with ExitStack() as ctx:
            layer0_sums(nc, ctx, m, dram)
        with ExitStack() as ctx:
            node_layer1(nc, ctx, m, ins, dram)
        with ExitStack() as ctx:
            s_src, s_row1, s_w = m.in_src_order()
            gather_sums(nc, ctx, m, "l1_", dram.tab1, s_row1, s_w, s_src, m.sfirst, m.slast, layer2_table(ins, dram))
        with ExitStack() as ctx:
            gather_sums(nc, ctx, m, "l2_", dram.tab2, m.row2, m.w1, m.dstf, m.dfirst, m.dlast, layer3_table(ins, dram))
        with ExitStack() as ctx:
            gather_sums(nc, ctx, m, "l3_", dram.tab3, m.srcf, m.w, m.dstf, m.dfirst, m.dlast, result(out))


def kernel(x, src, dst, edge_attr_40, edge_type_4, edge_type_8, edge_weight, edge_weight1, node_type_119, node_vec,
           L0_gnn_W1, L0_gnn_b1, L0_gnn_W2, L0_gnn_b2, L0_gnn_emb, L0_gnn_adaptW, L0_gnn_gamma, L0_gnn_beta,
           L1_gnn_W, L1_gnn_b, L2_gnn_weight1, L2_gnn_weight2, L2_gnn_bias1, L2_gnn_bias2):
    import numpy as _np
    import concourse.bacc as _bacc
    from concourse import mybir as _mybir
    from concourse.bass_utils import run_bass_kernel_spmd as _run

    def padded(a, n, fill=0):
        a = _np.asarray(a)
        out = _np.full((n,) + a.shape[1:], fill, a.dtype)
        out[:a.shape[0]] = a
        return out

    def by_chunk(a):
        return a.reshape(NC, P, T).transpose(1, 0, 2).reshape(P, NE)

    def by_tile(a):
        return a.reshape(NT, P).T

    dst_natural = padded(dst, EP + 1, N)
    attr = padded(edge_attr_40, EP)
    laid = {
        "x": padded(x, NP), "src": by_chunk(padded(src, EP, N)), "dst": dst_natural[:EP].reshape(NC, P, T).transpose(0, 2, 1).reshape(EP),
        "dst_laid": by_chunk(dst_natural[:EP]), "dst_after": by_chunk(dst_natural[1:]),
        "attr": attr, "attrT": attr.reshape(NC, P, T, R).transpose(3, 0, 2, 1).reshape(R, EP),
        "type4": by_chunk(padded(edge_type_4, EP)), "type8": by_chunk(padded(edge_type_8, EP)),
        "w": by_chunk(padded(edge_weight, EP)), "w1": by_chunk(padded(_np.asarray(edge_weight1).reshape(-1), EP)),
        "ztype": by_tile(padded(node_type_119, NP)), "mult": by_tile(padded(node_vec, NP)),
        "W1T": _np.asarray(L0_gnn_W1).T, "b1": _np.asarray(L0_gnn_b1).reshape(H, 1),
        "W2T": _np.concatenate([_np.asarray(L0_gnn_W2).T, _np.asarray(L0_gnn_b2).reshape(1, H)]),
        "emb": L0_gnn_emb, "embT": _np.asarray(L0_gnn_emb).T, "adaptT": _np.asarray(L0_gnn_adaptW).T,
        "gamma": _np.asarray(L0_gnn_gamma).reshape(1, H), "beta": _np.asarray(L0_gnn_beta).reshape(1, H),
        "W": L1_gnn_W, "b": _np.asarray(L1_gnn_b).reshape(1, H),
        "weight1": L2_gnn_weight1, "weight2": L2_gnn_weight2,
        "bias1": _np.asarray(L2_gnn_bias1).reshape(H, 1), "bias2": _np.asarray(L2_gnn_bias2).reshape(1, H),
    }
    nc = _bacc.Bacc("TRN2", target_bir_lowering=False, num_devices=1)
    arrays, ins = {}, Memory()
    for name, a in laid.items():
        a = _np.ascontiguousarray(a)
        arrays[f"in_{name}"] = a
        ins.__dict__[name] = nc.dram_tensor(f"in_{name}", a.shape, _mybir.dt.from_np(a.dtype), kind="ExternalInput").ap()
    out = nc.dram_tensor("out_x", (NP, H), fp32, kind="ExternalOutput").ap()
    gnn(nc, ins, out)
    r = _run(nc, [arrays], core_ids=[0])
    return r.results[0]["out_x"][:N]
```
